# Optimizing a Trainium2 kernel written in Bass

```python
import numpy as np
import jax
import jax.numpy as jnp

def _softmax(x, axis=-1):
    return jax.nn.softmax(x, axis=axis)

def _gelu(x):
    return jax.nn.gelu(x, approximate=True)

def _silu(x):
    return jax.nn.silu(x)

def _sigmoid(x):
    return jax.nn.sigmoid(x)

def _layernorm(x, axis=-1, eps=1e-05):
    m = jnp.mean(x, axis=axis, keepdims=True)
    v = jnp.var(x, axis=axis, keepdims=True)
    return (x - m) / jnp.sqrt(v + eps)

def _scatter_add(tgt, idx, src, axis=0):
    return tgt.at[idx].add(src)

def _segment_sum(src, seg, n):
    return jax.ops.segment_sum(src, seg, n)
kernel_name = 'mk_gnn_resnorm_d4_gnn_r64_ebd3d9'

def setup_inputs(seed: int=0):
    np.random.seed(seed)
    _w = jnp.asarray

    def _rec_inputs():
        import jax
        import jax.numpy as jnp
        _gk = jax.random.key(seed)
        x = -0.000202 + 1 * jax.random.normal(jax.random.fold_in(_gk, 1), (100000, 64), jnp.float32)
        src = jax.random.randint(jax.random.fold_in(_gk, 2), (50000,), 0, 100000, jnp.int32)
        dst = jax.random.randint(jax.random.fold_in(_gk, 3), (50000,), 0, 100000, jnp.int32)
        _o = jnp.argsort(dst, stable=True)
        src = src[_o]
        dst = dst[_o]
        edge_type_14 = jax.random.randint(jax.random.fold_in(_gk, 12), (50000,), 0, 14, jnp.int32)
        edge_weight1 = 0.000614103 + 0.999867 * jax.random.normal(jax.random.fold_in(_gk, 13), (50000, 1), jnp.float32)
        return (x, src, dst, edge_type_14, edge_weight1)
    x, src, dst, edge_type_14, edge_weight1 = _rec_inputs()

    def _L0_gnn_setup():
        import jax, jax.numpy as jnp
        import numpy as np
        R = 14
        N = 100000
        E = 25000
        B = 8
        DIN, DH, DOUT = (64, 64, 64)

        def _rel_scatter_max(h_rel, src, dst, edge_type):
            msgs = h_rel[edge_type, src]
            seg = edge_type * N + dst
            agg = jax.ops.segment_max(msgs, seg, num_segments=R * N)
            agg = jnp.where(jnp.isneginf(agg), 0.0, agg)
            return agg.reshape(R, N, -1).sum(axis=0)
        key = jax.random.key(seed)
        ks = jax.random.split(key, 10)
        x = jax.random.normal(ks[0], (N, DIN), jnp.float32)
        edge_index = jax.random.randint(ks[1], (2, E), 0, N)
        edge_type = jax.random.randint(ks[2], (E,), 0, R)
        w1 = jax.random.normal(ks[3], (R, B, DIN // B, DH // B), jnp.float32) * 0.1
        root1 = jax.random.normal(ks[4], (DIN, DH), jnp.float32) * 0.1
        bias1 = jnp.zeros((DH,), jnp.float32)
        comp2 = jax.random.normal(ks[5], (R, B), jnp.float32) * 0.3
        bases2 = jax.random.normal(ks[6], (B, DH, DOUT), jnp.float32) * 0.1
        root2 = jax.random.normal(ks[7], (DH, DOUT), jnp.float32) * 0.1
        bias2 = jnp.zeros((DOUT,), jnp.float32)
        return {'x': x, 'edge_index': edge_index, 'edge_type': edge_type, 'w1': w1, 'root1': root1, 'bias1': bias1, 'comp2': comp2, 'bases2': bases2, 'root2': root2, 'bias2': bias2}
    _L0_gnn_all = _L0_gnn_setup()
    _L0_gnn_in = {k: v for k, v in _L0_gnn_all.items() if k in ('w1', 'root1', 'bias1', 'comp2', 'bases2', 'root2', 'bias2')}
    del _L0_gnn_all

    def _L1_gnn_setup():
        import jax, jax.numpy as jnp
        import numpy as np
        N, E = (50000, 12500)
        IN_D, HID, H1, OUT_D, H2, EDGE_D = (64, 16, 8, 64, 2, 1)
        NEG_SLOPE = 0.2

        def gatv2_layer(x, src, dst, edge_attr, Wl, Wr, We, att, bias, concat):
            n = x.shape[0]
            H, C = att.shape
            xl = (x @ Wl).reshape(n, H, C)
            xr = (x @ Wr).reshape(n, H, C)
            ee = (edge_attr @ We).reshape(-1, H, C)
            z = jax.nn.leaky_relu(xl[src] + xr[dst] + ee, NEG_SLOPE)
            score = jnp.einsum('ehc,hc->eh', z, att)
            m = jax.ops.segment_max(score, dst, num_segments=n)
            m = jnp.where(jnp.isfinite(m), m, 0.0)
            a = jnp.exp(score - m[dst])
            denom = jax.ops.segment_sum(a, dst, num_segments=n)
            alpha = a / (denom[dst] + 1e-16)
            msg = xl[src] * alpha[..., None]
            out = jax.ops.segment_sum(msg, dst, num_segments=n)
            if concat:
                return out.reshape(n, H * C) + bias
            return out.mean(axis=1) + bias

        def layer_norm(x, g, b):
            mu = x.mean(-1, keepdims=True)
            var = ((x - mu) ** 2).mean(-1, keepdims=True)
            return (x - mu) * jax.lax.rsqrt(var + 1e-05) * g + b
        key = jax.random.key(seed)
        ks = jax.random.split(key, 24)

        def w(k, *shape):
            fan_in = shape[0]
            return jax.random.normal(k, shape, dtype=jnp.float32) * (1.0 / np.sqrt(fan_in))
        inp = {'x': jax.random.normal(ks[0], (N, IN_D), dtype=jnp.float32), 'edge_index': jax.random.randint(ks[1], (2, E), 0, N, dtype=jnp.int64), 'edge_attr': jax.random.normal(ks[2], (E, EDGE_D), dtype=jnp.float32), 'w1_l': w(ks[3], IN_D, H1 * HID), 'w1_r': w(ks[4], IN_D, H1 * HID), 'w1_e': w(ks[5], EDGE_D, H1 * HID), 'att1': jax.random.normal(ks[6], (H1, HID), dtype=jnp.float32) * 0.1, 'b1': jnp.zeros((H1 * HID,), dtype=jnp.float32), 'w2_l': w(ks[7], H1 * HID, H2 * OUT_D), 'w2_r': w(ks[8], H1 * HID, H2 * OUT_D), 'w2_e': w(ks[9], EDGE_D, H2 * OUT_D), 'att2': jax.random.normal(ks[10], (H2, OUT_D), dtype=jnp.float32) * 0.1, 'b2': jnp.zeros((OUT_D,), dtype=jnp.float32), 'wc': w(ks[11], OUT_D, OUT_D), 'bc': jnp.zeros((OUT_D,), dtype=jnp.float32), 'ln_g': jnp.ones((OUT_D,), dtype=jnp.float32), 'ln_b': jnp.zeros((OUT_D,), dtype=jnp.float32), 'wr': w(ks[12], OUT_D, OUT_D), 'br': jnp.zeros((OUT_D,), dtype=jnp.float32), 'lnr_g': jnp.ones((OUT_D,), dtype=jnp.float32), 'lnr_b': jnp.zeros((OUT_D,), dtype=jnp.float32)}
        return inp
    _L1_gnn_all = _L1_gnn_setup()
    _L1_gnn_in = {k: v for k, v in _L1_gnn_all.items() if k in ('w1_l', 'w1_r', 'w1_e', 'att1', 'b1', 'w2_l', 'w2_r', 'w2_e', 'att2', 'b2', 'wc', 'bc', 'ln_g', 'ln_b', 'wr', 'br', 'lnr_g', 'lnr_b')}
    del _L1_gnn_all

    def _L2_gnn_setup():
        import jax, jax.numpy as jnp
        import numpy as np
        N_NODES = 100000
        N_EDGES = 25000
        D = 64

        def _sage_conv(x, src, dst, Wl, Wr, b, n_nodes):
            msg = x[src]
            agg = jax.ops.segment_sum(msg, dst, num_segments=n_nodes)
            deg = jax.ops.segment_sum(jnp.ones((src.shape[0],), x.dtype), dst, num_segments=n_nodes)
            mean = agg / jnp.maximum(deg, 1.0)[:, None]
            return mean @ Wl.T + x @ Wr.T + b
        key = jax.random.key(seed)
        ks = jax.random.split(key, 7)
        x = jax.random.normal(ks[0], (N_NODES, D), dtype=jnp.float32)
        edge_index = jax.random.randint(ks[1], (2, N_EDGES), 0, N_NODES, dtype=jnp.int64)
        s = 1.0 / np.sqrt(D)
        Wl1 = jax.random.normal(ks[2], (D, D), dtype=jnp.float32) * s
        Wr1 = jax.random.normal(ks[3], (D, D), dtype=jnp.float32) * s
        b1 = jnp.zeros((D,), dtype=jnp.float32)
        Wl2 = jax.random.normal(ks[4], (D, D), dtype=jnp.float32) * s
        Wr2 = jax.random.normal(ks[5], (D, D), dtype=jnp.float32) * s
        b2 = jnp.zeros((D,), dtype=jnp.float32)
        return {'x': x, 'edge_index': edge_index, 'Wl1': Wl1, 'Wr1': Wr1, 'b1': b1, 'Wl2': Wl2, 'Wr2': Wr2, 'b2': b2}
    _L2_gnn_all = _L2_gnn_setup()
    _L2_gnn_in = {k: v for k, v in _L2_gnn_all.items() if k in ('Wl1', 'Wr1', 'b1', 'Wl2', 'Wr2', 'b2')}
    del _L2_gnn_all

    def _L3_gnn_setup():
        import jax, jax.numpy as jnp
        import numpy as np
        N, E, D, L = (50000, 12500, 64, 3)
        EPS = 1e-05

        def _transformer_conv(x, src, dst, Wq, bq, Wk, bk, Wv, bv, Ws, bs):
            n = x.shape[0]
            d = x.shape[1]
            q = x @ Wq + bq
            k = x @ Wk + bk
            v = x @ Wv + bv
            skip = x @ Ws + bs
            scale = 1.0 / jnp.sqrt(jnp.asarray(d, x.dtype))
            s = jnp.sum(q[dst] * k[src], axis=-1) * scale
            m = jax.ops.segment_max(s, dst, num_segments=n)
            e = jnp.exp(s - m[dst])
            denom = jax.ops.segment_sum(e, dst, num_segments=n)
            alpha = e / denom[dst]
            agg = jax.ops.segment_sum(alpha[:, None] * v[src], dst, num_segments=n)
            return agg + skip

        def _batch_norm(x, gamma, beta):
            mean = jnp.mean(x, axis=0)
            var = jnp.mean((x - mean) ** 2, axis=0)
            return gamma * (x - mean) * jax.lax.rsqrt(var + EPS) + beta
        key = jax.random.key(seed)
        ks = jax.random.split(key, 12)
        x = jax.random.normal(ks[0], (N, D), dtype=jnp.float32)
        edge_index = jax.random.randint(ks[1], (2, E), 0, N, dtype=jnp.int64)
        w = lambda k: jax.random.normal(k, (L, D, D), dtype=jnp.float32) * 0.1
        return {'x': x, 'edge_index': edge_index, 'Wq': w(ks[2]), 'bq': jnp.zeros((L, D), jnp.float32), 'Wk': w(ks[3]), 'bk': jnp.zeros((L, D), jnp.float32), 'Wv': w(ks[4]), 'bv': jnp.zeros((L, D), jnp.float32), 'Ws': w(ks[5]), 'bs': jnp.zeros((L, D), jnp.float32), 'gamma': jnp.ones((L - 1, D), jnp.float32), 'beta': jnp.zeros((L - 1, D), jnp.float32)}
    _L3_gnn_all = _L3_gnn_setup()
    _L3_gnn_in = {k: v for k, v in _L3_gnn_all.items() if k in ('Wq', 'bq', 'Wk', 'bk', 'Wv', 'bv', 'Ws', 'bs', 'gamma', 'beta')}
    del _L3_gnn_all
    return {'x': x, 'src': src, 'dst': dst, 'edge_type_14': edge_type_14, 'edge_weight1': edge_weight1, 'L0_gnn_w1': _L0_gnn_in['w1'], 'L0_gnn_root1': _L0_gnn_in['root1'], 'L0_gnn_bias1': _L0_gnn_in['bias1'], 'L0_gnn_comp2': _L0_gnn_in['comp2'], 'L0_gnn_bases2': _L0_gnn_in['bases2'], 'L0_gnn_root2': _L0_gnn_in['root2'], 'L0_gnn_bias2': _L0_gnn_in['bias2'], 'L1_gnn_w1_l': _L1_gnn_in['w1_l'], 'L1_gnn_w1_r': _L1_gnn_in['w1_r'], 'L1_gnn_w1_e': _L1_gnn_in['w1_e'], 'L1_gnn_att1': _L1_gnn_in['att1'], 'L1_gnn_b1': _L1_gnn_in['b1'], 'L1_gnn_w2_l': _L1_gnn_in['w2_l'], 'L1_gnn_w2_r': _L1_gnn_in['w2_r'], 'L1_gnn_w2_e': _L1_gnn_in['w2_e'], 'L1_gnn_att2': _L1_gnn_in['att2'], 'L1_gnn_b2': _L1_gnn_in['b2'], 'L1_gnn_wc': _L1_gnn_in['wc'], 'L1_gnn_bc': _L1_gnn_in['bc'], 'L1_gnn_ln_g': _L1_gnn_in['ln_g'], 'L1_gnn_ln_b': _L1_gnn_in['ln_b'], 'L1_gnn_wr': _L1_gnn_in['wr'], 'L1_gnn_br': _L1_gnn_in['br'], 'L1_gnn_lnr_g': _L1_gnn_in['lnr_g'], 'L1_gnn_lnr_b': _L1_gnn_in['lnr_b'], 'L2_gnn_Wl1': _L2_gnn_in['Wl1'], 'L2_gnn_Wr1': _L2_gnn_in['Wr1'], 'L2_gnn_b1': _L2_gnn_in['b1'], 'L2_gnn_Wl2': _L2_gnn_in['Wl2'], 'L2_gnn_Wr2': _L2_gnn_in['Wr2'], 'L2_gnn_b2': _L2_gnn_in['b2'], 'L3_gnn_Wq': _L3_gnn_in['Wq'], 'L3_gnn_bq': _L3_gnn_in['bq'], 'L3_gnn_Wk': _L3_gnn_in['Wk'], 'L3_gnn_bk': _L3_gnn_in['bk'], 'L3_gnn_Wv': _L3_gnn_in['Wv'], 'L3_gnn_bv': _L3_gnn_in['bv'], 'L3_gnn_Ws': _L3_gnn_in['Ws'], 'L3_gnn_bs': _L3_gnn_in['bs'], 'L3_gnn_gamma': _L3_gnn_in['gamma'], 'L3_gnn_beta': _L3_gnn_in['beta']}

def reference(x, src, dst, edge_type_14, edge_weight1, L0_gnn_w1, L0_gnn_root1, L0_gnn_bias1, L0_gnn_comp2, L0_gnn_bases2, L0_gnn_root2, L0_gnn_bias2, L1_gnn_w1_l, L1_gnn_w1_r, L1_gnn_w1_e, L1_gnn_att1, L1_gnn_b1, L1_gnn_w2_l, L1_gnn_w2_r, L1_gnn_w2_e, L1_gnn_att2, L1_gnn_b2, L1_gnn_wc, L1_gnn_bc, L1_gnn_ln_g, L1_gnn_ln_b, L1_gnn_wr, L1_gnn_br, L1_gnn_lnr_g, L1_gnn_lnr_b, L2_gnn_Wl1, L2_gnn_Wr1, L2_gnn_b1, L2_gnn_Wl2, L2_gnn_Wr2, L2_gnn_b2, L3_gnn_Wq, L3_gnn_bq, L3_gnn_Wk, L3_gnn_bk, L3_gnn_Wv, L3_gnn_bv, L3_gnn_Ws, L3_gnn_bs, L3_gnn_gamma, L3_gnn_beta):
    import jax
    import jax.numpy as jnp

    def _L0_gnn_ref(x, edge_index, edge_type, w1, root1, bias1, comp2, bases2, root2, bias2):
        import jax, jax.numpy as jnp
        import numpy as np
        R = 14
        N = 100000
        E = 25000
        B = 8
        DIN, DH, DOUT = (64, 64, 64)

        def _rel_scatter_max(h_rel, src, dst, edge_type):
            msgs = h_rel[edge_type, src]
            seg = edge_type * N + dst
            agg = jax.ops.segment_max(msgs, seg, num_segments=R * N)
            agg = jnp.where(jnp.isneginf(agg), 0.0, agg)
            return agg.reshape(R, N, -1).sum(axis=0)
        src, dst = (edge_index[0], edge_index[1])
        xb = x.reshape(N, B, DIN // B)
        h = jnp.einsum('nbi,rbio->rnbo', xb, w1).reshape(R, N, DH)
        out = _rel_scatter_max(h, src, dst, edge_type) + x @ root1 + bias1
        x1 = jax.nn.relu(out)
        W2 = jnp.einsum('rb,bio->rio', comp2, bases2)
        h2 = jnp.einsum('ni,rio->rno', x1, W2)
        out2 = _rel_scatter_max(h2, src, dst, edge_type) + x1 @ root2 + bias2
        return out2

    def _L1_gnn_ref(x, edge_index, edge_attr, w1_l, w1_r, w1_e, att1, b1, w2_l, w2_r, w2_e, att2, b2, wc, bc, ln_g, ln_b, wr, br, lnr_g, lnr_b):
        import jax, jax.numpy as jnp
        import numpy as np
        N, E = (50000, 12500)
        IN_D, HID, H1, OUT_D, H2, EDGE_D = (64, 16, 8, 64, 2, 1)
        NEG_SLOPE = 0.2

        def gatv2_layer(x, src, dst, edge_attr, Wl, Wr, We, att, bias, concat):
            n = x.shape[0]
            H, C = att.shape
            xl = (x @ Wl).reshape(n, H, C)
            xr = (x @ Wr).reshape(n, H, C)
            ee = (edge_attr @ We).reshape(-1, H, C)
            z = jax.nn.leaky_relu(xl[src] + xr[dst] + ee, NEG_SLOPE)
            score = jnp.einsum('ehc,hc->eh', z, att)
            m = jax.ops.segment_max(score, dst, num_segments=n)
            m = jnp.where(jnp.isfinite(m), m, 0.0)
            a = jnp.exp(score - m[dst])
            denom = jax.ops.segment_sum(a, dst, num_segments=n)
            alpha = a / (denom[dst] + 1e-16)
            msg = xl[src] * alpha[..., None]
            out = jax.ops.segment_sum(msg, dst, num_segments=n)
            if concat:
                return out.reshape(n, H * C) + bias
            return out.mean(axis=1) + bias

        def layer_norm(x, g, b):
            mu = x.mean(-1, keepdims=True)
            var = ((x - mu) ** 2).mean(-1, keepdims=True)
            return (x - mu) * jax.lax.rsqrt(var + 1e-05) * g + b
        src, dst = (edge_index[0], edge_index[1])
        h = jax.nn.relu(gatv2_layer(x, src, dst, edge_attr, w1_l, w1_r, w1_e, att1, b1, True))
        h = jax.nn.relu(gatv2_layer(h, src, dst, edge_attr, w2_l, w2_r, w2_e, att2, b2, False))
        h = jax.nn.gelu(layer_norm(h @ wc + bc, ln_g, ln_b), approximate=False)
        h = h + jax.nn.gelu(layer_norm(h @ wr + br, lnr_g, lnr_b), approximate=False)
        return h

    def _L2_gnn_ref(x, edge_index, Wl1, Wr1, b1, Wl2, Wr2, b2):
        import jax, jax.numpy as jnp
        import numpy as np
        N_NODES = 100000
        N_EDGES = 25000
        D = 64

        def _sage_conv(x, src, dst, Wl, Wr, b, n_nodes):
            msg = x[src]
            agg = jax.ops.segment_sum(msg, dst, num_segments=n_nodes)
            deg = jax.ops.segment_sum(jnp.ones((src.shape[0],), x.dtype), dst, num_segments=n_nodes)
            mean = agg / jnp.maximum(deg, 1.0)[:, None]
            return mean @ Wl.T + x @ Wr.T + b
        src, dst = (edge_index[0], edge_index[1])
        n = x.shape[0]
        h = jax.nn.relu(_sage_conv(x, src, dst, Wl1, Wr1, b1, n))
        h = jax.nn.relu(_sage_conv(h, src, dst, Wl2, Wr2, b2, n))
        return h

    def _L3_gnn_ref(x, edge_index, Wq, bq, Wk, bk, Wv, bv, Ws, bs, gamma, beta):
        import jax, jax.numpy as jnp
        import numpy as np
        N, E, D, L = (50000, 12500, 64, 3)
        EPS = 1e-05

        def _transformer_conv(x, src, dst, Wq, bq, Wk, bk, Wv, bv, Ws, bs):
            n = x.shape[0]
            d = x.shape[1]
            q = x @ Wq + bq
            k = x @ Wk + bk
            v = x @ Wv + bv
            skip = x @ Ws + bs
            scale = 1.0 / jnp.sqrt(jnp.asarray(d, x.dtype))
            s = jnp.sum(q[dst] * k[src], axis=-1) * scale
            m = jax.ops.segment_max(s, dst, num_segments=n)
            e = jnp.exp(s - m[dst])
            denom = jax.ops.segment_sum(e, dst, num_segments=n)
            alpha = e / denom[dst]
            agg = jax.ops.segment_sum(alpha[:, None] * v[src], dst, num_segments=n)
            return agg + skip

        def _batch_norm(x, gamma, beta):
            mean = jnp.mean(x, axis=0)
            var = jnp.mean((x - mean) ** 2, axis=0)
            return gamma * (x - mean) * jax.lax.rsqrt(var + EPS) + beta
        src, dst = (edge_index[0], edge_index[1])
        num_layers = Wq.shape[0]
        h = x
        for l in range(num_layers):
            h = _transformer_conv(h, src, dst, Wq[l], bq[l], Wk[l], bk[l], Wv[l], bv[l], Ws[l], bs[l])
            if l != num_layers - 1:
                h = _batch_norm(h, gamma[l], beta[l])
                h = jax.nn.relu(h)
        return h
    edge_index = jnp.stack([src, dst])
    x = _layernorm(x + _L0_gnn_ref(x, edge_index, edge_type_14, L0_gnn_w1, L0_gnn_root1, L0_gnn_bias1, L0_gnn_comp2, L0_gnn_bases2, L0_gnn_root2, L0_gnn_bias2), axis=-1)
    x = _layernorm(x + _L1_gnn_ref(x, edge_index, edge_weight1, L1_gnn_w1_l, L1_gnn_w1_r, L1_gnn_w1_e, L1_gnn_att1, L1_gnn_b1, L1_gnn_w2_l, L1_gnn_w2_r, L1_gnn_w2_e, L1_gnn_att2, L1_gnn_b2, L1_gnn_wc, L1_gnn_bc, L1_gnn_ln_g, L1_gnn_ln_b, L1_gnn_wr, L1_gnn_br, L1_gnn_lnr_g, L1_gnn_lnr_b), axis=-1)
    x = _layernorm(x + _L2_gnn_ref(x, edge_index, L2_gnn_Wl1, L2_gnn_Wr1, L2_gnn_b1, L2_gnn_Wl2, L2_gnn_Wr2, L2_gnn_b2), axis=-1)
    x = _layernorm(x + _L3_gnn_ref(x, edge_index, L3_gnn_Wq, L3_gnn_bq, L3_gnn_Wk, L3_gnn_bk, L3_gnn_Wv, L3_gnn_bv, L3_gnn_Ws, L3_gnn_bs, L3_gnn_gamma, L3_gnn_beta), axis=-1)
    return x

_drawn_inputs = setup_inputs


def setup_inputs(seed=0):
    import zlib

    import numpy as np

    out = dict(_drawn_inputs(seed))
    spreads = {'L0_gnn_bias1': (0.0, 0.1),
     'L0_gnn_bias2': (0.0, 0.1),
     'L1_gnn_b1': (0.0, 0.1),
     'L1_gnn_b2': (0.0, 0.1),
     'L1_gnn_bc': (0.0, 0.1),
     'L1_gnn_ln_g': (1.0, 0.2),
     'L1_gnn_ln_b': (0.0, 0.1),
     'L1_gnn_br': (0.0, 0.1),
     'L1_gnn_lnr_g': (1.0, 0.2),
     'L1_gnn_lnr_b': (0.0, 0.1),
     'L2_gnn_b1': (0.0, 0.1),
     'L2_gnn_b2': (0.0, 0.1),
     'L3_gnn_bq': (0.0, 0.8),
     'L3_gnn_bk': (0.0, 0.8),
     'L3_gnn_bv': (0.0, 0.1),
     'L3_gnn_bs': (0.0, 0.1),
     'L3_gnn_gamma': (1.0, 0.2),
     'L3_gnn_beta': (0.0, 0.1)}
    factors = {'L1_gnn_w1_r': 7.742, 'L1_gnn_w1_e': 4.564, 'L1_gnn_w2_r': 5.922, 'L1_gnn_w2_e': 3.379}
    for name, (base, spread) in spreads.items():
        noise = np.random.default_rng([zlib.crc32(name.encode()), seed]).standard_normal(out[name].shape)
        drawn = base * np.exp(spread * noise) if base else spread * noise
        out[name] = jnp.asarray(drawn.astype(out[name].dtype))
    for name, factor in factors.items():
        out[name] = (out[name] * factor).astype(out[name].dtype)
    return out
```

```python
from contextlib import ExitStack

import concourse.bass as bass
from concourse import mybir

F32 = mybir.dt.float32
BF16 = mybir.dt.bfloat16
I32 = mybir.dt.int32
ALU = mybir.AluOpType
ACT = mybir.ActivationFunctionType
AX = mybir.AxisListType

P = 128
D = 64
N = 100000
E = 50000
R = 14
W = 512
LANES = 4
SLOTS = 8
CROWS = 1024
EP = 50176
NP = 100352
T = EP // P
SWEEPS = EP // W
NCH = NP // CROWS
ECH = EP // CROWS
LASTROWS = N - (NCH - 1) * CROWS
LASTP = LASTROWS // 8
SPARE_OUT = N + 256
PAD_DST = N + 200
OUT_ROWS = SPARE_OUT + EP
CONSTS = 37
UPTO = 4
BIG = 1.0e30
EPS = 1.0e-5
GB = 28


LOADED = ["bias1", "bias2", "g_b1", "g_b2", "g_bc", "g_lng", "g_lnb", "g_br", "g_lnrg", "g_lnrb", "att1", "att2",
          "s_b1", "s_b2"] + [f"{n}{i}" for n in ("bq", "bk", "bv", "bs") for i in range(3)] + \
    [f"{n}{i}" for n in ("gamma", "beta") for i in range(2)]
VECS = LOADED + ["bias2c", "g_bcc", "g_brc", "bs2c", "alone", "bn_s0", "bn_b0", "bn_s1", "bn_b1", "mean", "var"]
NVEC = len(VECS)
MATS = ["root1", "root2", "wc", "wr", "wl1", "wr1", "wl2", "wr2", "ws0", "ws1", "ws2"]

PACKED = [(n, P) for n in MATS] + [("basew", 4 * D), ("gw", P), ("g2l", P), ("g2r", P), ("we", 2 * P),
                                   ("wkv", 3 * P), ("wq", 3 * P), ("loaded", len(LOADED))]
BIGW = sum(w for _, w in PACKED)


class Phase:

    def __init__(self, names, chunks, base):
        self.steps = {n: i + 1 for i, n in enumerate(names)}
        self.first = list(base)
        self.chunks = chunks
        self.n = len(names)
        assert len(self.steps) == self.n
        self.last = [base[g] + self.n * len(range(g, chunks, LANES)) for g in range(LANES)]

    def at(self, g, k, step):
        return k * self.n + (self.first[g] + self.steps[step])

    def begin(self, g, k):
        return k * self.n + self.first[g]


class Seq:

    def __init__(self, names):
        self.steps = {n: i + 1 for i, n in enumerate(names)}
        assert len(self.steps) == len(names)

    def __getitem__(self, name):
        return self.steps[name]


class Dmas:

    def __init__(self, per, chunks, base, lanes=LANES):
        self.per, self.first, self.lanes = per, list(base), lanes
        self.last = [base[g] + 16 * per * len(range(g, chunks, lanes)) for g in range(lanes)]

    def before(self, g, k):
        return k * (16 * self.per) + self.first[g]

    def after(self, g, k):
        return k * (16 * self.per) + (self.first[g] + 16 * self.per)


def pass_groups(eng, chunks, work, peel=False):
    turns = chunks // LANES
    if peel:
        work([(g, 0, g) for g in range(LANES)])
    with eng.Fori(int(peel), turns, 1) as i:
        work([(g, i, i * LANES + g) for g in range(LANES)])
    if chunks % LANES:
        work([(g, turns, turns * LANES + g) for g in range(chunks % LANES)])


def sweep_groups(eng, work, peel=False):
    turns = SWEEPS // SLOTS

    def turn(i):
        for h in range(2):
            work([(g, i * 2 + h, i * SLOTS + (h * LANES + g), h * LANES + g, i) for g in range(LANES)])
    if peel:
        turn(0)
    with eng.Fori(int(peel), turns, 1) as i:
        turn(i)
    work([(g, turns * 2, turns * SLOTS + g, g, turns) for g in range(SWEEPS - turns * SLOTS)])


def build(nc, t, out, upto):
    with ExitStack() as ctx:
        def sb(name, shape, dt=F32):
            return ctx.enter_context(nc.sbuf_tensor(name, shape, dt))

        def sem(name):
            return ctx.enter_context(nc.semaphore(name))

        def dram(name, shape, dt=F32):
            return nc.dram_tensor(name, shape, dt, kind="Internal").ap()

        names = ["x1", "xa", "xb", "h2", "xc", "g1", "g2"]
        tab = {n: dram(f"tab_{n}", (NP + EP, D)) for n in names}
        h1 = dram("tab_h1", (EP + 1, P))
        agg = [dram(f"agg_{i}", (EP, D)) for i in range(4)]
        agg2 = dram("agg_gat2", (EP, P))
        aggh = [dram(f"agg_tr{i}", (EP, P)) for i in range(3)]
        xdst = dram("x_dst", (EP, D))
        rec = dram("rec", (EP, 4), I32)
        ptr = dram("ptr", (NP + EP, 2), I32)
        rows = dram("rows", (3, EP))
        dsts = dram("dsts", (2, EP), I32)
        keys = dram("keys", (1, EP + 2))
        flag = dram("flag", (6, EP), BF16)
        hot = dram("hot", (3 * R, EP), BF16)
        wrow = dram("wrow", (1, EP))

        def rows8(a, lo, count, width):
            return a[lo:lo + count * CROWS, :].rearrange("(c p j) d -> p c (j d)", p=P, j=8)

        def rows4(a, lo, width):
            return a[lo:lo + EP, :].rearrange("(c p j) d -> p c j d", p=P, j=4)

        ident = sb("ident", [P, P])
        center = sb("center", [P, P])
        mean2 = sb("mean2", [P, P])
        fold2 = sb("fold2", [P, D])
        mask64 = sb("mask64", [P, P])
        mask16 = sb("mask16", [P, P])
        sums = sb("sums", [P, 2, P])
        spread = sb("spread", [D, 4, P])
        mask3 = sb("mask3", [3 * R, 3])
        scale1 = sb("scale1", [P, P])
        zrow = sb("zrow", [1, P])
        sel = sb("sel", [6, 6, P], BF16)
        selbig = sb("selbig", [6, 6, P], BF16)
        eps = sb("eps", [P, 1])
        big = sb("big", [P, BIGW])
        at = 0
        part = {}
        for n, w in PACKED:
            part[n] = big[:, at:at + w]
            at += w
        bd = {n: part[n] for n in MATS}
        vec = sb("vec", [P, NVEC])
        cw_all = sb("cw", [P, 2, 4 * P])
        cw = cw_all[0:3 * R, :, :]
        cwb = sb("cwb", [3 * R, 2, 4, P], BF16)
        basew = part["basew"].rearrange("p (j d) -> p j d", j=4)
        gw, g2l, g2r = part["gw"], part["g2l"], part["g2r"]
        we = part["we"][0:1, :].rearrange("p (l m) -> p l m", l=2)
        wkv = part["wkv"].rearrange("p (l m) -> p l m", l=3)
        wq = part["wq"].rearrange("p (l m) -> p l m", l=3)
        att1m = sb("att1m", [P, P])
        att2m = sb("att2m", [P, P])
        recg = sb("recg", [P, T, 4], I32)
        spg = sb("spg", [P, T, 2], I32)
        idx = sb("idx", [P, 2, 4 * SLOTS], I32)
        idh = sb("idh", [P, T], I32)
        idd = sb("idd", [P, T], I32)
        ido = sb("ido", [P, T], I32)
        dst8 = sb("dst8", [P, T], I32)
        real84 = sb("real84", [P, 1])
        fbf = sb("fbf", [P, 4, T], BF16)
        rinv = sb("rinv", [P, T])
        first4 = sb("first4", [P, T])
        last8 = sb("last8", [P, T])
        first8 = sb("first8", [P, T])
        alone8 = sb("alone8", [P, NCH * 8])
        stats = sb("stats", [P, 2, 4])
        pos = sb("pos", [P, T], I32)
        pidx = sb("pidx", [P, T], I32)
        prec = sb("prec", [P, T, 2], I32)
        sidx = sb("sidx", [P, 2, GB // 2], I32)
        srec = sb("srec", [P, 2, GB // 2, 4], I32)
        iota_e = sb("iota_e", [P, T], I32)
        recm = sb("recm", [P, T, 4], I32)
        orow = [sb(f"orow{g}", [P, 4, P]) for g in range(LANES)]
        NT = 11
        L = [[sb(f"lane{g}_{i}", [P, W + 2]) for i in range(NT)] for g in range(LANES)]
        ft = [sb(f"flags{g}", [6, W], BF16) for g in range(LANES)]
        hots = [sb(f"hots{g}", [3 * R, W], BF16) for g in range(LANES)]
        wr_ = [sb(f"wrow{g}", [1, W]) for g in range(LANES)]
        ring = [sb(f"ring{r}", [P, 4, P]) for r in range(SLOTS)]
        hring = [cw_all[:, g, :].rearrange("p (j d) -> p j d", d=P) for g in range(2)] + \
            [sb(f"hring{g}", [P, 4, P]) for g in range(2, LANES)]
        bank = [[ctx.enter_context(nc.psum_tensor(f"bank{g}_{i}", [P, W], F32)) for i in range(2)]
                for g in range(LANES)]

        def tl(g, i):
            return L[g][i][:, 0:W]

        def v(name):
            i = VECS.index(name)
            return vec[:, i:i + 1]

        def hotm(r):
            return L[2][r // 2][:, :].bitcast(BF16)[:, 400 * (r % 2):400 * (r % 2) + T]

        lane = [sem(f"lane{g}_step") for g in range(LANES)]
        loaded = [sem(f"lane{g}_loaded") for g in range(LANES)]
        stored = [sem(f"lane{g}_stored") for g in range(LANES)]
        gathered = [sem(f"slot{r}_gathered") for r in range(SLOTS)]
        s_const = sem("constants_built")
        s_weights = sem("weights_loaded")
        s_in = sem("edges_loaded")
        s_link = sem("vector_chain")
        s_set = sem("setup_step")
        s_ptr0 = sem("ptr_filled")
        s_idx = sem("indices_copied")
        s_sc = [sem(f"setup_moved{h}") for h in range(2)]
        saved = [sem(f"slot{r}_saved") for r in range(SLOTS)]
        s_mid = sem("masks_moved")
        put = [sem(f"lane{g}_scattered") for g in range(LANES)]
        s_pre = sem("prepared")
        s_mask = sem("masks_loaded")
        s_rec = sem("records_loaded")
        s_keys = sem("keys_moved")
        s_spg = sem("pointers_gathered")
        s_ptr1 = sem("ptr_loaded")
        links = [0]

        def layernorm(i):
            return [f"y{i}_p", f"sq{i}", f"var{i}_p", f"sd{i}", f"rs{i}", f"n{i}"]

        NODE_A = ["x_t", "x", "x1_p", "x1", "x1_t", "x1_o"] + layernorm(0) + ["xa_t", "xa_o"] + layernorm(1) + \
            ["xb_t", "xb_o", "h2_p", "h2", "h2_t", "h2_o", "h3_p", "h3"] + layernorm(2) + \
            ["xc_t", "xc_o", "g1_p", "g1", "g1_t", "g1_o"]
        RGCN = [f"c{j}{s}" for j in range(4) for s in ("_p", "")] + \
            ["msg_p", "msg", "gfirst", "gmax", "glast", "gpick", "keep", "agg", "agg_t", "agg_o"]
        RG1 = ["x_t", "x"] + [f"x{j}{s}" for j in range(4) for s in ("_t", "")] + RGCN
        RG2 = ["x0_t", "x0"] + RGCN
        SAGE = ["src_t", "src", "keep", "agg", "agg_t", "agg_o"]
        SOFT = ["s_p", "s", "reset", "y", "d", "lo", "hi", "ex", "v_p", "wv"]
        GAT1 = ["src_t", "src", "dst_in", "keep", "dst", "z_p", "z_s", "z"] + SOFT + \
            ["num", "den", "num_t", "den_t", "rc", "rcp", "rows"]
        GAT2 = ["src_t", "src", "dst_t", "dst_in", "keep", "dst", "dst_b", "z_p", "z_s", "z"] + SOFT + \
            ["num", "den", "num_t", "den_t", "rcp", "rows"]
        TR = ["src_t", "src", "dst_in", "keep", "dst", "dst_b", "q_p", "q", "kv_p", "qk"] + SOFT + \
            ["nd", "nd_t", "h_t", "rcp", "rows", "hrows"]
        IN2 = ["a_t", "a", "b_t", "b"]
        LIN = ["lin_p", "lin"]
        OUT = ["o_t", "o"]
        STAT = ["q", "st_p", "st"]
        plan = [("nodeA", NODE_A, NCH, 1, 6, 0),
                ("rg1", RG1, SWEEPS, 2, 1, 8), ("e01", IN2 + LIN + OUT, ECH, 2, 1, 0),
                ("rg2", RG2, SWEEPS, 2, 1, 4), ("e02", IN2 + ["c_t", "c"] + layernorm(0) + OUT, ECH, 3, 1, 0)]
        if upto >= 2:
            plan += [("gat1", GAT1, SWEEPS, 3, 1, 4), ("gat2", GAT2, SWEEPS, 3, 1, 4),
                     ("e12", ["a_t", "a"] + layernorm(0) + ["ge0"] + layernorm(1) + ["ge1", "c_t", "c"] +
                      layernorm(2) + OUT, ECH, 3, 1, 0)]
        if upto >= 3:
            plan += [("sage1", SAGE, SWEEPS, 1, 1, 4), ("e21", IN2 + LIN + OUT, ECH, 2, 1, 0),
                     ("sage2", SAGE, SWEEPS, 1, 1, 4),
                     ("e22", IN2 + LIN + ["c_t", "c"] + layernorm(0) + OUT, ECH, 3, 1, 0)]
        if upto >= 4:
            plan += [("tr0", TR, SWEEPS, 2, 1, 4), ("e31", IN2 + LIN + OUT + STAT, ECH, 2, 1, 0),
                     ("nS", STAT, NCH, 1, 0, 0), ("tr1", TR, SWEEPS, 2, 1, 4),
                     ("e32", IN2 + LIN + OUT + STAT, ECH, 2, 1, 0),
                     ("n2", ["a_t", "a"] + LIN + OUT + STAT, NCH, 1, 1, 0), ("tr2", TR, SWEEPS, 2, 1, 4),
                     ("n3", ["a_t", "a", "c_t", "c"] + layernorm(0) + OUT, NCH, 2, 1, 0),
                     ("e33", IN2 + ["c_t", "c"] + layernorm(0) + OUT, ECH, 3, 0, 0)]
        else:
            plan += [("nOut", ["o"], NCH, 1, 1, 0), ("eOut", ["o"], ECH, 1, 0, 0)]
        ph, ld, st, ga = {}, {}, {}, {}
        b0, b1, b2, b3 = [200] * LANES, [0] * LANES, [0] * LANES, [0] * SLOTS
        for name, steps, chunks, loads, stores, gathers in plan:
            ph[name] = Phase(steps, chunks, b0)
            ld[name] = Dmas(loads, chunks, b1)
            st[name] = Dmas(stores, chunks, b2)
            ga[name] = Dmas(gathers, chunks if gathers else 0, b3, SLOTS)
            b0, b1, b2, b3 = ph[name].last, ld[name].last, st[name].last, ga[name].last
        last_pass = "e33" if upto >= 4 else "eOut"
        scattered = Dmas(8, ECH, [0] * LANES)
        START = 200

        LNP = lambda i: [f"y{i}_p", f"sq{i}", f"var{i}_p", f"sd{i}", f"n{i}"]
        SQ = Seq(["f_last", "f_turn", "f_scan", "f_back", "b_last", "b_turn", "b_scan", "b_back", "setup",
                  "att", "bias_p", "bias"] + LNP(0) + ["ge0"] + LNP(1) + ["ge1", "y2_p", "alone", "keys", "flags", "rows"] +
                 [f"bn{l}_{s}" for l in range(2) for s in ("p", "var", "sd", "done")])
        MIDS = 1 + 1 + 3 + 1 + 4
        MIDT = MIDS + 2 + 3 * R + 1

        INFO = {
            "rg1": (1, t["x"], None, agg[0]), "rg2": (1, tab["x1"], None, agg[1]),
            "gat1": (-1, tab["xa"], tab["xa"][NP:NP + EP, :], h1[0:EP, :]),
            "gat2": (1, h1, h1[0:EP, :], agg2),
            "sage1": (1, tab["xb"], None, agg[2]), "sage2": (1, tab["h2"], None, agg[3]),
            "tr0": (-1, tab["xc"], tab["xc"][NP:NP + EP, :], aggh[0]),
            "tr1": (1, tab["g1"], tab["g1"][NP:NP + EP, :], aggh[1]),
            "tr2": (-1, tab["g2"], tab["g2"][NP:NP + EP, :], aggh[2])}

        def there(c, way, count):
            return c if way > 0 else (count - 1) - c

        def tables_ready(eng, name):
            for g in range(LANES):
                eng.wait_ge(lane[g], ph[name].first[g])
                if st[name].first[g]:
                    eng.wait_ge(stored[g], st[name].first[g])

        def turned(a, way):
            return a if way > 0 else a[:, ::-1]

        def before(g, k):
            return (g - 1, k) if g else (LANES - 1, k - 1)

        def node_rows(a, c):
            return a[:, bass.ds(c, 1), :].rearrange("p a n -> p (a n)")

        tabn = {n: a[0:NP, :].rearrange("(c p j) d -> p c (j d)", p=P, j=8) for n, a in tab.items()}
        tabe = {n: a[NP:NP + EP, :].rearrange("(c p j) d -> p c (j d)", p=P, j=8) for n, a in tab.items()}
        xfull = t["x"][0:(NCH - 1) * CROWS, :].rearrange("(c p j) d -> p c (j d)", p=P, j=8)
        xlast = t["x"][(NCH - 1) * CROWS:N, :].rearrange("(p j) d -> p (j d)", j=8)
        ofull = out[0:(NCH - 1) * CROWS, :].rearrange("(c p j) d -> p c (j d)", p=P, j=8)
        olast = out[(NCH - 1) * CROWS:N, :].rearrange("(p j) d -> p (j d)", j=8)

        def e8(a):
            return a.rearrange("(c p j) d -> p c (j d)", p=P, j=8)

        def e4(a):
            return a.rearrange("(c p j) d -> p c j d", p=P, j=4)

        def halves(a):
            return a.rearrange("(c p h j) d -> p c h (j d)", p=P, h=2, j=4)

        block = ctx.enter_context(nc.Block())

        @block.sync
        def _(sp):
            for i in range(3):
                sp.dma_start(L[0][i][:, 0:T].bitcast(I32), t["edge_dst"][:, i, :]).then_inc(s_in, 16)
            sp.dma_start(recg[:, :, :], t["edge_rec"]).then_inc(s_in, 16)
            sp.dma_start(big[:, :], t["packed"]).then_inc(s_weights, 16)
            sp.dma_start(cw[:, :, :], t["relw"]).then_inc(s_weights, 16)
            sp.wait_ge(s_const, CONSTS)
            sp.dma_start(ptr[0:NP, :].rearrange("(p t) d -> p (t d)", p=P),
                         recm[:, :, :].rearrange("p t k -> p (t k)")).then_inc(s_ptr0, 16)
            sp.dma_start(h1[EP:EP + 1, :], zrow[:, :]).then_inc(s_mid, 16)
            sp.dma_start(dsts[0, :].rearrange("(p t) -> p t", t=T),
                         t["edge_dst"][:, 0, :]).then_inc(s_mid, 16)
            sp.wait_ge(s_set, SQ["setup"])
            for i in range(3):
                sp.dma_start(rows[i, :].rearrange("(p t) -> p t", t=T), L[1][3 + i][:, 0:T]).then_inc(s_mid, 16)
            sp.dma_start(dsts[1, :].rearrange("(p t) -> p t", t=T), idh[:, :]).then_inc(s_mid, 16)
            for h, r in enumerate((0, 1, 4, 5)):
                sp.dma_start(flag[r, :].rearrange("(p t) -> p t", t=T), fbf[:, h, :]).then_inc(s_mid, 16)
            sp.wait_ge(s_mid, 16 * MIDS)
            r4 = rows.rearrange("r (c p j) -> r p c j", p=P, j=4)
            r8 = rows.rearrange("r (c p j) -> r p c j", p=P, j=8)
            d4 = dsts.rearrange("r (c p j) -> r p c j", p=P, j=4)
            d8 = dsts.rearrange("r (c p j) -> r p c j", p=P, j=8)
            for to, of in ((first4, r4[1]), (rinv, r4[2]), (idd, d4[1])):
                sp.dma_start(to[:, :].rearrange("p (c j) -> p c j", j=4), of).then_inc(s_mask, 16)
            for to, of in ((last8, r8[0]), (first8, r8[1]), (dst8, d8[0])):
                sp.dma_start(to[:, :].rearrange("p (c j) -> p c j", j=8), of).then_inc(s_mask, 16)

            def pass_io(name, load, store, kinds=1):
                chunks = ph[name].chunks
                turns, rest = chunks // LANES, chunks % LANES

                def loads(i, n=LANES):
                    for g in range(n):
                        load(g, i, i * LANES + g)

                def stores(i, n=LANES):
                    for what in range(kinds):
                        for g in range(n):
                            store(g, i, i * LANES + g, what)

                loads(0)
                with sp.Fori(0, turns - 1, 1) as i:
                    loads(i + 1)
                    stores(i)
                loads(turns, rest)
                stores(turns - 1)
                stores(turns, rest)

            def sweep_io(name, last_use, last_step):
                way, _, hd, to = INFO[name]
                pz = ph[name]
                width = to.shape[1]
                tables_ready(sp, name)

                def loads(k, first, use, half, n=LANES):
                    for g in range(n):
                        e = there(first + g, way, SWEEPS)
                        sp.wait_ge(lane[g], pz.at(g, k - 1, last_use))
                        if way < 0:
                            sp.nop(nofuse=True)
                        sp.dma_start(ft[g][:, :], flag[:, bass.ds(e * W, W)]).then_inc(loaded[g], 16)
                        if name in ("rg1", "rg2"):
                            sp.dma_start(hots[g][:, :], hot[:, bass.ds(e * W, W)]).then_inc(loaded[g], 16)
                        if name in ("gat1", "gat2"):
                            sp.dma_start(wr_[g][:, :], wrow[:, bass.ds(e * W, W)]).then_inc(loaded[g], 16)
                        if hd is not None:
                            into = hring[g][:, :, :] if name == "gat2" else ring[half * LANES + g][:, :, D:P]
                            sp.dma_start(into, e4(hd)[:, bass.ds(e, 1), :, :].rearrange("p a j d -> p (a j) d")
                                         ).then_inc(loaded[g], 16)

                def stores(k, first, use, half, n=LANES):
                    for g in range(n):
                        e = there(first + g, way, SWEEPS)
                        r = half * LANES + g
                        if name == "rg1":
                            sp.wait_ge(gathered[r], ga[name].after(r, use))
                            sp.dma_start(e4(xdst)[:, bass.ds(e, 1), :, :].rearrange("p a j d -> p (a j) d"),
                                         ring[r][:, :, D:P]).then_inc(saved[r], 16)
                        sp.wait_ge(lane[g], pz.at(g, k, last_step))
                        if way < 0:
                            sp.nop(nofuse=True)
                        sp.dma_start(e4(to)[:, bass.ds(e, 1), :, :].rearrange("p a j d -> p (a j) d"),
                                     orow[g][:, :, 0:width]).then_inc(stored[g], 16)

                turns, rest = SWEEPS // SLOTS, SWEEPS % SLOTS
                loads(0, 0, 0, 0)
                with sp.Fori(0, turns - 1, 1) as i:
                    loads(i * 2 + 1, i * SLOTS + LANES, i, 1)
                    stores(i * 2, i * SLOTS, i, 0)
                    loads(i * 2 + 2, i * SLOTS + SLOTS, i + 1, 0)
                    stores(i * 2 + 1, i * SLOTS + LANES, i, 1)
                i = turns - 1
                loads(i * 2 + 1, i * SLOTS + LANES, i, 1)
                stores(i * 2, i * SLOTS, i, 0)
                loads(turns * 2, turns * SLOTS, turns, 0, rest)
                stores(i * 2 + 1, i * SLOTS + LANES, i, 1)
                stores(turns * 2, turns * SLOTS, turns, 0, rest)

            def load(g, k, c):
                sp.wait_ge(lane[g], ph["nodeA"].at(g, k - 1, "x_t"))
                if type(c) is int and c == NCH - 1:
                    sp.dma_start(tl(g, 0)[0:LASTP, :], xlast).then_inc(loaded[g], 16)
                else:
                    sp.dma_start(tl(g, 0), node_rows(xfull, c)).then_inc(loaded[g], 16)

            def store(g, k, c, what):
                n = ("x1", "xa", "xb", "h2", "xc", "g1")[what]
                sp.wait_ge(lane[g], ph["nodeA"].at(g, k, n + "_o"))
                sp.dma_start(node_rows(tabn[n], c), tl(g, 7 + what % 3)).then_inc(stored[g], 16)
            pass_io("nodeA", load, store, kinds=6)

            sp.wait_ge(s_rec, 16)
            tables_ready(sp, "rg1")
            sp.dma_start(recm[:, :, :], rec.rearrange("(p t) k -> p t k", t=T)).then_inc(s_keys, 16)
            sp.wait_ge(s_set, SQ["keys"])
            sp.dma_start(keys[0, 1:EP + 1].rearrange("(p t) -> p t", t=T), L[0][0][:, 0:T]).then_inc(s_keys, 16)
            sp.dma_start(keys[:, 0:1], L[0][1][0:1, 0:1]).then_inc(s_keys, 16)
            sp.dma_start(keys[:, EP + 1:EP + 2], L[0][1][0:1, 0:1]).then_inc(s_keys, 16)
            sp.wait_ge(s_keys, 4 * 16)
            sp.dma_start(L[0][2][:, 0:T], keys[0, 0:EP].rearrange("(p t) -> p t", t=T)).then_inc(s_keys, 16)
            sp.dma_start(L[0][3][:, 0:T], keys[0, 2:EP + 2].rearrange("(p t) -> p t", t=T)).then_inc(s_keys, 16)
            sp.wait_ge(s_set, SQ["flags"])
            for h, r in enumerate((2, 3)):
                sp.dma_start(flag[r, :].rearrange("(p t) -> p t", t=T), fbf[:, h, :]).then_inc(s_mid, 16)
            for q in range(3):
                for r in range(R):
                    sp.dma_start(hot[q * R + r, :].rearrange("(p t) -> p t", t=T), hotm(r)).then_inc(s_mid, 16)
            sp.dma_start(wrow[0, :].rearrange("(p t) -> p t", t=T), L[0][4][:, 0:T]).then_inc(s_mid, 16)
            sp.dma_start(recm[:, :, :].rearrange("p t k -> p (t k)").rearrange("p (c k) -> p c k", c=NCH),
                         ptr[0:NP, :].rearrange("(c p j) k -> p c (j k)", p=P, j=8)).then_inc(s_ptr1, 16)
            sp.wait_ge(s_mid, 16 * MIDT)

            def edge_pass(name, loads, to):
                tables_ready(sp, name)
                steps = {0: "a_t", 8: "c_t", 9: "b_t"}

                def load(g, k, c):
                    sp.wait_ge(lane[g], ph[name].at(g, k - 1, last_read[name]))
                    for i, of in loads:
                        sp.dma_start(tl(g, i), node_rows(of, c)).then_inc(loaded[g], 16)

                def store(g, k, c, _):
                    sp.wait_ge(lane[g], ph[name].at(g, k, "o"))
                    sp.dma_start(node_rows(to, c), tl(g, 7)).then_inc(stored[g], 16)
                if to is not None:
                    pass_io(name, load, store)
                else:
                    pass_io(name, load, lambda g, k, c, _: None)

            def out_store(name, load):
                def store(g, k, c, _):
                    sp.wait_ge(lane[g], ph[name].at(g, k, "o"))
                    if type(c) is int and c == NCH - 1:
                        sp.dma_start(olast, tl(g, 7)[0:LASTP, :]).then_inc(stored[g], 16)
                    else:
                        sp.dma_start(node_rows(ofull, c), tl(g, 7)).then_inc(stored[g], 16)
                pass_io(name, load, store)

            def wide(a, w):
                return a.rearrange("(c p h j) d -> h p c (j d)", p=P, h=2, j=4)[w]

            last_read = {"e01": "b_t", "e02": "c_t", "e12": "c_t", "e21": "b_t", "e22": "c_t", "e31": "b_t",
                         "e32": "b_t", "n2": "a_t", "n3": "c_t", "e33": "c_t", "nS": "st_p", "nOut": "o", "eOut": "o"}
            sweep_io("rg1", "keep", "agg_o")
            edge_pass("e01", [(0, e8(agg[0])), (9, e8(xdst))], tabe["x1"])
            sweep_io("rg2", "keep", "agg_o")
            edge_pass("e02", [(0, e8(agg[1])), (9, tabe["x1"]), (8, e8(xdst))], tabe["xa"])
            if upto >= 2:
                sweep_io("gat1", "reset", "rows")
                sweep_io("gat2", "reset", "rows")
                edge_pass("e12", [(0, wide(agg2, 0)), (8, wide(agg2, 1)), (9, tabe["xa"])], tabe["xb"])
            if upto >= 3:
                sweep_io("sage1", "keep", "agg_o")
                edge_pass("e21", [(0, e8(agg[2])), (9, tabe["xb"])], tabe["h2"])
                sweep_io("sage2", "keep", "agg_o")
                edge_pass("e22", [(0, e8(agg[3])), (9, tabe["h2"]), (8, tabe["xb"])], tabe["xc"])
            if upto >= 4:
                sweep_io("tr0", "reset", "hrows")
                edge_pass("e31", [(0, wide(aggh[0], 0)), (8, wide(aggh[0], 1))], tabe["g1"])
                edge_pass("nS", [(7, tabn["g1"])], None)
                sweep_io("tr1", "reset", "hrows")
                edge_pass("e32", [(0, wide(aggh[1], 0)), (8, wide(aggh[1], 1))], tabe["g2"])
                edge_pass("n2", [(0, tabn["g1"])], tabn["g2"])
                sweep_io("tr2", "reset", "hrows")
                tables_ready(sp, "n3")

                def load(g, k, c):
                    sp.wait_ge(lane[g], ph["n3"].at(g, k - 1, "c_t"))
                    sp.dma_start(tl(g, 0), node_rows(tabn["g2"], c)).then_inc(loaded[g], 16)
                    sp.dma_start(tl(g, 8), node_rows(tabn["xc"], c)).then_inc(loaded[g], 16)
                out_store("n3", load)
                tables_ready(sp, "e33")

                def load(g, k, c):
                    sp.wait_ge(lane[g], ph["e33"].at(g, k - 1, "c_t"))
                    sp.dma_start(tl(g, 0), node_rows(wide(aggh[2], 0), c)).then_inc(loaded[g], 16)
                    sp.dma_start(tl(g, 8), node_rows(wide(aggh[2], 1), c)).then_inc(loaded[g], 16)
                    sp.dma_start(tl(g, 9).rearrange("p (j d) -> p j d", d=D),
                                 aggh[0].rearrange("(c p j) d -> p c j d", p=P, j=8)[:, bass.ds(c, 1), :, D:P]
                                 .rearrange("p a j d -> p (a j) d")).then_inc(loaded[g], 16)
                pass_io("e33", load, lambda g, k, c, _: None)
            else:
                shown = tabn[("xa", "xb", "xc")[upto - 1]], tabe[("xa", "xb", "xc")[upto - 1]]
                tables_ready(sp, "nOut")

                def load(g, k, c):
                    sp.wait_ge(lane[g], ph["nOut"].at(g, k - 1, "o"))
                    sp.dma_start(tl(g, 0), node_rows(shown[0], c)).then_inc(loaded[g], 16)
                out_store("nOut", load)
                tables_ready(sp, "eOut")

                def load(g, k, c):
                    sp.wait_ge(lane[g], ph["eOut"].at(g, k - 1, "o"))
                    sp.dma_start(tl(g, 0), node_rows(shown[1], c)).then_inc(loaded[g], 16)
                pass_io("eOut", load, lambda g, k, c, _: None)
            for g in range(LANES):
                sp.wait_ge(stored[g], b2[g])
                sp.wait_ge(put[g], scattered.last[g])

        @block.gpsimd
        def _(gp):
            n = [0]

            def after(ins):
                n[0] += 1
                ins.then_inc(s_const, 1)
                gp.wait_ge(s_const, n[0])

            def eye(m, pattern, base, fill=1.0, cm=1):
                after(gp.affine_select(out=m, in_=m, compare_op=ALU.not_equal, fill=fill, base=base,
                                       pattern=pattern, channel_multiplier=cm))

            def keep_from(m, pattern, base, cm=1):
                after(gp.affine_select(out=m, in_=m, compare_op=ALU.is_ge, fill=0.0, base=base, pattern=pattern,
                                       channel_multiplier=cm))
            for m in (ident, fold2, sums, sel, selbig, zrow, spread):
                after(gp.memset(m[:], 0.0))
            for m in (mask16, mask64, mask3, real84):
                after(gp.memset(m[:], 1.0))
            after(gp.memset(scale1[:, :], float(D) ** -0.5))
            after(gp.memset(eps[:, :], EPS))
            eye(ident[:, :], [[-1, P]], 0)
            for h in range(2):
                eye(fold2[:, :], [[-1, D]], -D * h)
                eye(sums[:, h, :].rearrange("p (a f) -> p a f", a=2), [[0, 2], [-1, D]], -D * h)
            for q in range(4):
                for i in range(2):
                    eye(spread[:, q, i * D:(i + 1) * D].rearrange("p (b o) -> p b o", o=8), [[-8, 8], [0, 8]],
                        -(2 * q + i))
            eye(sel[:, :, :], [[-1, 6], [0, P]], 0)
            eye(selbig[:, :, :], [[-1, 6], [0, P]], 0, fill=-BIG)
            for m, w in ((mask16, 16), (mask64, D)):
                view = m[:, :].rearrange("p (h c) -> p h c", c=w)
                keep_from(view, [[-w, P // w], [0, w]], 0)
                keep_from(view, [[w, P // w], [0, w]], w - 1, cm=-1)
            keep_from(mask3[:, :], [[-R, 3]], 0)
            keep_from(mask3[:, :], [[R, 3]], R - 1, cm=-1)
            keep_from(real84[:, :], [[0, 1]], LASTP - 1, cm=-1)
            after(gp.iota(iota_e[:, :], [[1, T]], base=0, channel_multiplier=T))
            after(gp.iota(recm[:, :, :].rearrange("p t (a b) -> p (t a) b", b=2), [[1, 2 * T], [0, 2]], base=0,
                          channel_multiplier=2 * T))
            assert n[0] == CONSTS
            for g in range(LANES):
                gp.sem_inc(lane[g], START)

            H = GB // 2

            def setup_loop(number, copies, move):
                def turn(i, peeled):
                    for h in range(2):
                        if not peeled:
                            gp.wait_ge(s_sc[h], (i + number * (T // GB)) * (16 * H))
                        copies(i * GB + h * H, h)
                        gp.drain().then_inc(s_idx, 1)
                        gp.wait_ge(s_idx, i * 2 + (h + 1 + 2 * number * (T // GB)))
                        gp.nop(nofuse=True)
                        for q in range(H):
                            move(h, q).then_inc(s_sc[h], 16)
                turn(0, number == 0)
                with gp.Fori(1, T // GB, 1) as i:
                    turn(i, False)
                for h in range(2):
                    gp.wait_ge(s_sc[h], 16 * H * (number + 1) * (T // GB))

            def cols(a, c0, n):
                return a[:, bass.ds(c0, n)]

            gp.wait_ge(s_set, SQ["setup"])
            gp.wait_ge(s_ptr0, 16)

            def copies(c0, h):
                gp.tensor_copy(sidx[:, h, :], cols(pidx, c0, H))
                gp.tensor_copy(srec[:, h, :, 0:2], prec[:, bass.ds(c0, H), :])
            setup_loop(0, copies, lambda h, q: gp.indirect_dma_start(
                ptr, bass.IndirectOffsetOnAxis(sidx[:, h, q:q + 1], 0), srec[:, h, q, 0:2], None))

            def copies(c0, h):
                gp.tensor_copy(sidx[:, h, :], cols(pos, c0, H))
                gp.tensor_copy(srec[:, h, :, :], recg[:, bass.ds(c0, H), :])
            setup_loop(1, copies, lambda h, q: gp.indirect_dma_start(
                rec, bass.IndirectOffsetOnAxis(sidx[:, h, q:q + 1], 0), srec[:, h, q, :], None))
            gp.dma_start(recg[:, :, :].rearrange("p t k -> p (t k)").rearrange("p (c k) -> p c k", k=16),
                         rec.rearrange("(c p j) k -> p c (j k)", p=P, j=4)).then_inc(s_rec, 16)
            gp.wait_ge(s_rec, 16)

            def turn(i):
                for h in range(2):
                    gp.tensor_copy(sidx[:, h, :], recg[:, bass.ds(i * GB + h * H, H), 0:1].rearrange("p t k -> p (t k)"))
                    gp.drain().then_inc(s_idx, 1)
                    gp.wait_ge(s_idx, i * 2 + (h + 1 + 4 * (T // GB)))
                    gp.nop(nofuse=True)
                    for q in range(H):
                        gp.indirect_dma_start(srec[:, h, q, 0:2], None, ptr,
                                              bass.IndirectOffsetOnAxis(sidx[:, h, q:q + 1], 0)).then_inc(s_sc[h], 16)
                    gp.wait_ge(s_sc[h], (i + (1 + 2 * (T // GB))) * (16 * H))
                    gp.tensor_copy(spg[:, bass.ds(i * GB + h * H, H), :], srec[:, h, :, 0:2]).then_inc(s_spg, 1)
            with gp.Fori(0, T // GB, 1) as i:
                turn(i)

            tables = {"rg1": None, "rg2": spg[:, :, 0:1], "gat1": spg[:, :, 0:1], "gat2": None,
                      "sage1": spg[:, :, 0:1], "sage2": spg[:, :, 0:1], "tr0": spg[:, :, 0:1],
                      "tr1": spg[:, :, 1:2], "tr2": spg[:, :, 0:1]}
            used = [3 * 2 * (T // GB)]

            def sweep_gathers(name, last_read):
                way, table, _, _ = INFO[name]
                tables_ready(gp, name)

                def work(group, peeled):
                    for g, k, c, r, use in group:
                        e = there(c, way, SWEEPS)
                        if name == "rg1":
                            if not peeled:
                                gp.wait_ge(saved[r], use * 16)
                            gp.nop(nofuse=True)
                        gp.wait_ge(lane[g], ph[name].at(g, k - 2, last_read))
                        src = recg[:, bass.ds(e * 4, 4), 0:1] if name == "rg1" else \
                            idh[:, bass.ds(e * 4, 4)] if name == "gat2" else \
                            spg[:, bass.ds(e * 4, 4), 0:1] if name != "tr1" else spg[:, bass.ds(e * 4, 4), 1:2]
                        if name != "gat2":
                            src = src.rearrange("p t k -> p (t k)")
                        if name == "rg1":
                            gp.tensor_copy(idx[:, 1, 4 * r:4 * r + 4], idd[:, bass.ds(e * 4, 4)])
                        gp.tensor_copy(idx[:, 0, 4 * r:4 * r + 4], src).then_inc(s_idx, 1)
                        gp.wait_ge(s_idx, c + (used[0] + 1))
                        gp.nop(nofuse=True)
                        for j in range(4):
                            width = P if name == "gat2" else D
                            gp.indirect_dma_start(ring[r][:, j, 0:width], None, table, bass.IndirectOffsetOnAxis(
                                idx[:, 0, 4 * r + j:4 * r + j + 1], 0)).then_inc(gathered[r], 16)
                            if name == "rg1":
                                gp.indirect_dma_start(ring[r][:, j, D:P], None, table, bass.IndirectOffsetOnAxis(
                                    idx[:, 1, 4 * r + j:4 * r + j + 1], 0)).then_inc(gathered[r], 16)
                peel = [name == "rg1", name == "rg1"]

                def each(group):
                    first = len(peel) == 2 and peel[0] and type(group[0][1]) is int and group[0][1] < 2
                    work(group, first)
                sweep_groups(gp, each, peel=name == "rg1")
                used[0] += SWEEPS

            gp.wait_ge(s_mask, 6 * 16)
            sweep_gathers("rg1", "x_t")
            gp.wait_ge(s_mid, 16 * MIDT)
            sweep_gathers("rg2", "x0_t")
            if upto >= 2:
                sweep_gathers("gat1", "src_t")
                sweep_gathers("gat2", "src_t")
            if upto >= 3:
                sweep_gathers("sage1", "src_t")
                sweep_gathers("sage2", "src_t")
            if upto >= 4:
                for name in ("tr0", "tr1", "tr2"):
                    sweep_gathers(name, "src_t")

            gp.wait_ge(s_set, SQ["rows"])
            name = "e33" if upto >= 4 else "eOut"
            tables_ready(gp, name)

            def work(group):
                for g, k, c in group:
                    gp.wait_ge(lane[g], ph[name].at(g, k, "o"))
                    gp.tensor_copy(idx[:, 1, 8 * g:8 * g + 8], ido[:, bass.ds(c * 8, 8)]).then_inc(s_idx, 1)
                    gp.wait_ge(s_idx, c + (used[0] + 1))
                    gp.nop(nofuse=True)
                    for j in range(8):
                        gp.indirect_dma_start(out, bass.IndirectOffsetOnAxis(idx[:, 1, 8 * g + j:8 * g + j + 1], 0),
                                              tl(g, 7)[:, j * D:(j + 1) * D], None).then_inc(put[g], 16)
            pass_groups(gp, ECH, work)

        @block.tensor
        def _(pe):
            mm = nc.tensor.matmul
            I = ident[:, :]

            def turn_in(to, rows_):
                for i in range(4):
                    last = mm(to[:, i * P:(i + 1) * P], rows_[:, i * P:(i + 1) * P], I, start=(i == 0), stop=(i == 3),
                              is_transpose=True, skip_group_check=True)
                return last

            def product(to, terms):
                if to.shape[0] < P and terms[0][0].shape[0] < P:
                    pe.nop(nofuse=True)
                for i, (w, x) in enumerate(terms):
                    last = mm(to, w, x, start=(i == 0), stop=(i == len(terms) - 1))
                return last

            def step(g, phase, k, name, ins):
                ins.then_inc(lane[g], 1)

            def carries(a, b, scan_out):
                pe.wait_ge(s_set, SQ[a + "_last"])
                mm(bank[0][0][0:16, 0:P], L[3][0][:, 0:16], I, start=True, stop=True, is_transpose=True)
                mm(bank[0][1][0:16, 0:P], L[3][0][:, 16:32], I, start=True, stop=True,
                   is_transpose=True).then_inc(s_set, 1)
                pe.wait_ge(s_set, SQ[a + "_scan"])
                mm(bank[0][0][:, 0:16], scan_out, ident[0:16, 0:16], start=True, stop=True,
                   is_transpose=True).then_inc(s_set, 1)
            pe.wait_ge(s_const, CONSTS)
            carries("f", None, L[3][2][0:16, 0:P])
            carries("b", None, L[3][2][0:16, 1:P + 1])

            B0, B1 = bank[0][0], bank[0][1]
            col = lambda i: L[0][i][:, 0:1]

            def one(wait, to, terms):
                pe.wait_ge(s_set, SQ[wait])
                product(to[:, 0:1], terms).then_inc(s_set, 1)
            pe.wait_ge(s_set, SQ["att"])
            for i, n_ in enumerate(("bias2", "g_bc", "g_br", "bs2")):
                last = mm(B0[:, i:i + 1], center[:, :], v(n_), start=True, stop=True)
            last.then_inc(s_set, 1)
            one("bias", B0, [(bd["wc"], v("alone"))])
            one("sq0", B1, [(mean2[:, :], col(3))])
            one("ge0", B0, [(bd["wr"], col(1))])
            one("sq1", B1, [(mean2[:, :], col(3))])
            one("ge1", B0, [(center[:, :], col(1)), (center[:, :], col(2))])

            def nodes(group):
                pz = ph["nodeA"]

                def each(before_, make):
                    for g, k, c in group:
                        pe.wait_ge(lane[g], pz.at(g, k, before_))
                        make(g).then_inc(lane[g], 1)

                def var(i):
                    each(f"sq{i}", lambda g: product(bank[g][1][:, :], [(mean2[:, :], tl(g, 3))]))
                for g, k, c in group:
                    pe.wait_ge(lane[g], pz.begin(g, k))
                    pe.wait_ge(loaded[g], ld["nodeA"].after(g, k))
                    turn_in(bank[g][0], tl(g, 0)).then_inc(lane[g], 1)
                each("x", lambda g: product(bank[g][0][:, :], [(bd["root1"], tl(g, 1))]))
                each("x1", lambda g: turn_in(bank[g][1], tl(g, 2)))
                each("x1_o", lambda g: product(bank[g][0][:, :], [(bd["root2"], tl(g, 2)), (center[:, :], tl(g, 1))]))
                var(0)
                each("n0", lambda g: turn_in(bank[g][1], tl(g, 5)))
                each("xa_o", lambda g: product(bank[g][0][:, :], [(center[:, :], tl(g, 5))]))
                var(1)
                each("n1", lambda g: turn_in(bank[g][1], tl(g, 6)))
                each("xb_o", lambda g: product(bank[g][0][:, :], [(bd["wr1"], tl(g, 6))]))
                each("h2", lambda g: turn_in(bank[g][1], tl(g, 2)))
                each("h2_o", lambda g: product(bank[g][0][:, :], [(bd["wr2"], tl(g, 2))]))
                each("h3", lambda g: product(bank[g][0][:, :], [(center[:, :], tl(g, 1)), (center[:, :], tl(g, 6))]))
                var(2)
                each("n2", lambda g: turn_in(bank[g][1], tl(g, 5)))
                each("xc_o", lambda g: product(bank[g][0][:, :], [(bd["ws0"], tl(g, 5))]))
                each("g1", lambda g: turn_in(bank[g][1], tl(g, 2)))
            pe.wait_ge(s_set, SQ["alone"])
            pe.wait_ge(s_mid, 16 * MIDS)
            pass_groups(pe, NCH, nodes)

            def flags(to, r, g, table):
                return mm(to[:, :], table[:, r, :], ft[g][:, :], start=True, stop=True)

            def tiles(to, parts, make):
                if parts < P:
                    pe.nop(nofuse=True)
                for j in range(4):
                    last = mm(to[0:parts, j::4], make(j), I, start=(j == 0), stop=(j == 3), is_transpose=True,
                              skip_group_check=True)
                return last

            def rows_of(to, x, parts, first=0):
                if parts < P:
                    pe.nop(nofuse=True)
                for j in range(4):
                    last = mm(to[:, j * parts:(j + 1) * parts], x[:, j::4],
                              ident[first:first + parts, first:first + parts], start=(j == 0), stop=(j == 3),
                              is_transpose=True, skip_group_check=True)
                return last

            def rgcn(name):
                pz = ph[name]
                l = 0 if name == "rg1" else 1

                def work(group):
                    def each(before_, make):
                        for g, k, c, r, use in group:
                            pe.wait_ge(lane[g], pz.at(g, k, before_))
                            make(g, r).then_inc(lane[g], 1)
                    for g, k, c, r, use in group:
                        pe.wait_ge(lane[g], pz.begin(g, k))
                        pe.wait_ge(gathered[r], ga[name].after(r, use))
                        pe.wait_ge(loaded[g], ld[name].after(g, k))
                        if l == 0:
                            tiles(bank[g][1], D, lambda j: ring[r][:, j, 0:D]).then_inc(lane[g], 1)
                        else:
                            tiles(bank[g][0][0:D, :], D, lambda j: ring[r][:, j, 0:D])
                            for j in range(4):
                                last = mm(bank[g][0][D:P, j::4], ring[r][:, j, 0:D], I, start=True, stop=True)
                            last.then_inc(lane[g], 1)
                    if l == 0:
                        for q in range(4):
                            each(f"x{q - 1}" if q else "x", lambda g, r: product(
                                bank[g][0][:, :], [(spread[:, q, :], tl(g, 4)[0:D, :])]))
                    each(f"x{3 if l == 0 else 0}", lambda g, r: relation(g, 0))
                    for q in range(1, 4):
                        each(f"c{q - 1}", lambda g, r: relation(g, q))
                    each("c3", lambda g, r: product(bank[g][1][0:D, :], [
                        (fold2[:, :] if l == 0 else basew[:, q, :], tl(g, q if l == 0 else q + 1)) for q in range(4)]))
                    each("msg", lambda g, r: flags(bank[g][0], 2, g, selbig))
                    each("gmax", lambda g, r: flags(bank[g][0], 3, g, sel))
                    each("gpick", lambda g, r: flags(bank[g][0], 0, g, sel))
                    each("agg", lambda g, r: rows_of(bank[g][1], tl(g, 8)[0:D, :], D))

                def relation(g, q):
                    return mm(bank[g][0][:, :], cwb[:, l, q, :], hots[g][:, :], start=True, stop=True)

                sweep_groups(pe, work)

            def sage(name):
                pz = ph[name]

                def work(group):
                    def each(before_, make):
                        for g, k, c, r, use in group:
                            pe.wait_ge(lane[g], pz.at(g, k, before_))
                            make(g, r).then_inc(lane[g], 1)
                    for g, k, c, r, use in group:
                        pe.wait_ge(lane[g], pz.begin(g, k))
                        pe.wait_ge(gathered[r], ga[name].after(r, use))
                        pe.wait_ge(loaded[g], ld[name].after(g, k))
                        tiles(bank[g][0], D, lambda j: ring[r][:, j, 0:D]).then_inc(lane[g], 1)
                    each("src", lambda g, r: flags(bank[g][1], 0, g, sel))
                    each("agg", lambda g, r: rows_of(bank[g][0], tl(g, 8)[0:D, :], D))
                sweep_groups(pe, work)

            def soft(name):
                pz = ph[name]
                way = INFO[name][0]
                keep, reset = (0, 1) if way > 0 else (4, 5)
                l = int(name[-1])

                def work(group):
                    def each(before_, make):
                        for g, k, c, r, use in group:
                            pe.wait_ge(lane[g], pz.at(g, k, before_))
                            make(g, r).then_inc(lane[g], 1)
                    for g, k, c, r, use in group:
                        pe.wait_ge(lane[g], pz.begin(g, k))
                        pe.wait_ge(gathered[r], ga[name].after(r, use))
                        pe.wait_ge(loaded[g], ld[name].after(g, k))
                        tiles(bank[g][0], P, lambda j: ring[r][:, j, :]).then_inc(lane[g], 1)
                    if name == "gat2":
                        each("src", lambda g, r: tiles(bank[g][1], P, lambda j: hring[g][:, j, :]))
                        each("dst_in", lambda g, r: flags(bank[g][0], keep, g, sel))
                        each("dst_b", lambda g, r: product(bank[g][0][:, :], [
                            (g2l, tl(g, 0)), (g2r, tl(g, 1)), (we[:, 1, :], wr_[g][:, :])]))
                    else:
                        each("dst_in", lambda g, r: flags(bank[g][1], keep, g, sel))
                    if name == "gat1":
                        each("dst", lambda g, r: product(bank[g][0][:, :], [
                            (gw, tl(g, 0)), (we[:, 0, :], wr_[g][:, :])]))
                    if name[:3] == "gat":
                        each("z", lambda g, r: product(bank[g][1][:, :], [
                            ((att1m if name == "gat1" else att2m)[:, :], tl(g, 3))]))
                    else:
                        hb = 2
                        each("dst_b", lambda g, r: product(bank[g][0][:, :], [(wq[D:P, l, :], tl(g, hb)[D:P, :])]))
                        each("q", lambda g, r: product(bank[g][1][:, :], [(wkv[0:D, l, :], tl(g, 0)[0:D, :])]))
                        each("qk", lambda g, r: product(bank[g][1][:, :], [(scale1[D:P, :], tl(g, 6)[D:P, :])]))
                    each("s", lambda g, r: flags(bank[g][0], reset, g, selbig))
                    if name[:3] == "gat":
                        wl = g2l if name == "gat2" else gw[0:D, :]
                        each("ex", lambda g, r: product(bank[g][0][:, :], [
                            (wl, tl(g, 0) if name == "gat2" else tl(g, 0)[0:D, :])]))
                        each("den", lambda g, r: rows_of(bank[g][0], tl(g, 8), P))
                        each("num_t", lambda g, r: rows_of(bank[g][1], tl(g, 9), P))
                    else:
                        each("ex", lambda g, r: product(bank[g][0][0:D, :], [(wkv[0:D, l, 0:D], tl(g, 0)[0:D, :])]))
                        each("nd", lambda g, r: rows_of(bank[g][0], tl(g, 8), P))
                        each("nd_t", lambda g, r: rows_of(bank[g][1], tl(g, hb)[D:P, :], D, D))
                sweep_groups(pe, work)

            def passes(name):
                pz = ph[name]

                def turn_wide(g, to, part_):
                    pe.nop(nofuse=True)
                    for h in range(2):
                        for i in range(4):
                            last = mm(to[h * D:(h + 1) * D, i * P:(i + 1) * P], wide_row(g, 2 * i + h, part_), I,
                                      start=(h == 1 or i == 0), stop=(h == 1 or i == 3), is_transpose=(h == 0),
                                      skip_group_check=True)
                    return last

                def turn_sum(g, to):
                    for h in range(2):
                        for i in range(4):
                            for m in range(2):
                                last = mm(to[h * D:(h + 1) * D, i * P:(i + 1) * P], wide_row(g, 2 * i + h, m), I,
                                          start=(m == 0), stop=(m == 1), skip_group_check=True)
                    return last

                def wide_row(g, j, part_):
                    at_ = (j % 4) * P + part_ * D
                    return L[g][0 if j < 4 else 8][:, at_:at_ + D]
                C = center[:, :]
                parts = {"e31", "e32", "e33"}

                def work(group):
                    def each(before_, make):
                        for g, k, c in group:
                            pe.wait_ge(lane[g], pz.at(g, k, before_))
                            make(g).then_inc(lane[g], 1)

                    def var(i):
                        each(f"sq{i}", lambda g: product(bank[g][1][:, :], [(mean2[:, :], tl(g, 3))]))
                    for g, k, c in group:
                        pe.wait_ge(lane[g], pz.begin(g, k))
                        if name == "nS":
                            break
                        pe.wait_ge(loaded[g], ld[name].after(g, k))
                        (turn_wide(g, bank[g][0], 0) if name in parts else turn_sum(g, bank[g][0]) if name == "e12"
                         else turn_in(bank[g][0], tl(g, 0))).then_inc(lane[g], 1)
                    if "b_t" in pz.steps:
                        each("a", lambda g: turn_wide(g, bank[g][1], 1) if name in parts
                             else turn_in(bank[g][1], tl(g, 9)))
                    if "lin_p" in pz.steps:
                        terms = {"e01": (I, bd["root1"]), "e21": (bd["wl1"], bd["wr1"]), "e22": (bd["wl2"], bd["wr2"]),
                                 "e31": (I, bd["ws0"]), "e32": (I, bd["ws1"]), "n2": (bd["ws1"],)}[name]
                        each("b" if "b" in pz.steps else "a", lambda g: product(
                            bank[g][0][:, :], [(w_, tl(g, 1 + i)) for i, w_ in enumerate(terms)]))
                    out_of = 6
                    if name == "e12":
                        each("a", lambda g: product(bank[g][0][:, :], [(bd["wc"], tl(g, 1))]))
                        var(0)
                        each("ge0", lambda g: product(bank[g][0][:, :], [(bd["wr"], tl(g, 1))]))
                        var(1)
                        each("ge1", lambda g: turn_in(bank[g][0], tl(g, 9)))
                        each("c", lambda g: product(bank[g][0][:, :], [(C, tl(g, 1)), (C, tl(g, 2)), (C, tl(g, 5))]))
                        var(2)
                        each("n2", lambda g: turn_in(bank[g][1], tl(g, 6)))
                    elif "y0_p" in pz.steps:
                        each("lin" if "lin" in pz.steps else "b" if "b" in pz.steps else "a",
                             lambda g: turn_in(bank[g][0], tl(g, 9 if name == "e33" else 8)))
                        terms = {"e02": [(C, 1), (bd["root2"], 2), (C, 5)], "e22": [(C, 4), (C, 5)],
                                 "n3": [(bd["ws2"], 1), (C, 5)], "e33": [(C, 1), (bd["ws2"], 2), (C, 5)]}[name]
                        each("c", lambda g: product(bank[g][0][:, :], [(w_, tl(g, i)) for w_, i in terms]))
                        var(0)
                        each("n0", lambda g: turn_in(bank[g][1], tl(g, 6)))
                    elif "lin" in pz.steps:
                        each("lin", lambda g: turn_in(bank[g][1], tl(g, 4)))
                    if "st_p" in pz.steps:
                        for g, k, c in group:
                            pe.wait_ge(lane[g], pz.at(g, k, "q"))
                            m = {"e31": first8, "e32": last8}.get(name, alone8)
                            for h, i_ in ((0, 7), (1, 3)):
                                for i in range(4):
                                    last = mm(bank[g][1][:, 2 * h:2 * h + 2], tl(g, i_)[:, i * P:(i + 1) * P],
                                              m[:, bass.ds(c * 8 + 2 * i, 2)], start=(i == 0), stop=(i == 3))
                            last.then_inc(lane[g], 1)
                pass_groups(pe, pz.chunks, work)

            def batchnorm(l):
                for g in range(LANES):
                    pe.wait_ge(lane[g], ph[("tr1", "tr2")[l]].first[g])
                for i in range(2):
                    for h in range(2):
                        last = mm(B0[:, i:i + 1], sums[:, h, :], stats[:, l, 2 * i + h:2 * i + h + 1],
                                  start=(h == 0), stop=(h == 1))
                last.then_inc(s_set, 1)
                pe.wait_ge(s_set, SQ[f"bn{l}_done"])
            pe.wait_ge(s_mid, 16 * MIDT)
            pe.wait_ge(s_mask, 6 * 16)
            pe.wait_ge(s_set, SQ["rows"])
            rgcn("rg1")
            passes("e01")
            rgcn("rg2")
            passes("e02")
            if upto >= 2:
                soft("gat1")
                soft("gat2")
                passes("e12")
            if upto >= 3:
                sage("sage1")
                passes("e21")
                sage("sage2")
                passes("e22")
            if upto >= 4:
                soft("tr0")
                passes("e31")
                passes("nS")
                batchnorm(0)
                soft("tr1")
                passes("e32")
                passes("n2")
                batchnorm(1)
                soft("tr2")
                passes("n3")
                passes("e33")

        def y_bias(name, i):
            return {("nodeA", 0): "bias2c", ("nodeA", 1): "alone", ("e02", 0): "bias2c", ("e12", 0): "g_bcc",
                    ("e12", 1): "g_brc", ("n3", 0): "bs2c", ("e33", 0): "bs2c"}.get((name, i))

        @block.scalar
        def _(act):
            f = nc.scalar.activation

            def biased(out_, in_, func, bias=None, scale=1.0):
                if bias is None:
                    return f(out_, in_, func, scale=scale)
                return f(out_, in_, func, bias=v(bias) if type(bias) is str else bias, scale=scale)

            B0, B1 = bank[0][0], bank[0][1]

            def col(i):
                return L[0][i][:, 0:1]

            def one(wait, out_, in_, func, bias=None, scale=1.0):
                act.wait_ge(s_set, SQ[wait])
                biased(out_, in_, func, bias, scale).then_inc(s_set, 1)
            one("y0_p", col(3), B0[:, 0:1], ACT.Square, "g_bcc")
            one("var0_p", col(4), B1[:, 0:1], ACT.Sqrt, eps[:, :])
            one("n0", col(1), col(6), ACT.Gelu, "g_lnb", v("g_lng"))
            one("y1_p", col(3), B0[:, 0:1], ACT.Square, "g_brc")
            one("var1_p", col(4), B1[:, 0:1], ACT.Sqrt, eps[:, :])
            one("n1", col(2), col(6), ACT.Gelu, "g_lnrb", v("g_lnrg"))

            def nodes(group):
                pz = ph["nodeA"]

                def each(before_, make):
                    for g, k, c in group:
                        act.wait_ge(lane[g], pz.at(g, k, before_))
                        make(g).then_inc(lane[g], 1)

                def norm(i):
                    each(f"y{i}_p", lambda g: biased(tl(g, 3), bank[g][0][:, :], ACT.Square, y_bias("nodeA", i)))
                    each(f"var{i}_p", lambda g: biased(tl(g, 4), bank[g][1][:, :], ACT.Sqrt, eps[:, :]))
                each("x_t", lambda g: biased(tl(g, 1), bank[g][0][:, :], ACT.Copy))
                each("x1_p", lambda g: biased(tl(g, 2), bank[g][0][:, :], ACT.Relu, "bias1"))
                norm(0)
                each("xa_t", lambda g: biased(tl(g, 8), bank[g][1][:, :], ACT.Copy))
                norm(1)
                each("h2_p", lambda g: biased(tl(g, 2), bank[g][0][:, :], ACT.Relu, "s_b1"))
                for g, k, c in group:
                    act.wait_ge(stored[g], st["nodeA"].before(g, k) + 16 * 3)
                    act.wait_ge(lane[g], pz.at(g, k, "h2_t"))
                    biased(tl(g, 7), bank[g][1][:, :], ACT.Copy).then_inc(lane[g], 1)
                each("h3_p", lambda g: biased(tl(g, 1), bank[g][0][:, :], ACT.Relu, "s_b2"))
                norm(2)
                each("g1_p", lambda g: biased(tl(g, 2), bank[g][0][:, :], ACT.Identity, "bs0"))
            pass_groups(act, NCH, nodes)

            def rgcn(name):
                pz = ph[name]

                def work(group):
                    def each(before_, make):
                        for g, k, c, r, use in group:
                            act.wait_ge(lane[g], pz.at(g, k, before_))
                            make(g).then_inc(lane[g], 1)
                    if name == "rg1":
                        each("x_t", lambda g: biased(tl(g, 4)[0:D, :], bank[g][1][0:D, :], ACT.Copy))
                    for q in range(4 if name == "rg1" else 1):
                        each(f"x{q}_t", lambda g: biased(tl(g, q), bank[g][0][:, :], ACT.Copy))
                    each("msg_p", lambda g: biased(tl(g, 5)[0:D, :], bank[g][1][0:D, :], ACT.Copy))
                    for g, k, c, r, use in group:
                        act.wait_ge(stored[g], st[name].before(g, k))
                        act.wait_ge(lane[g], pz.at(g, k, "agg_t"))
                        biased(orow[g][:, :, 0:D], bank[g][1][:, 0:4 * D].rearrange("p (j d) -> p j d", d=D),
                               ACT.Copy).then_inc(lane[g], 1)
                sweep_groups(act, work)

            def sage(name):
                def work(group):
                    for g, k, c, r, use in group:
                        act.wait_ge(lane[g], ph[name].at(g, k, "src_t"))
                        biased(tl(g, 5)[0:D, :], bank[g][0][0:D, :], ACT.Copy).then_inc(lane[g], 1)
                sweep_groups(act, work)

            def soft(name):
                pz = ph[name]
                way = INFO[name][0]
                l = int(name[-1])
                bn = dict(bias=f"bn_b{l - 1}") if name[:2] == "tr" and l else None

                def work(group):
                    def each(before_, make):
                        for g, k, c, r, use in group:
                            act.wait_ge(lane[g], pz.at(g, k, before_))
                            make(g).then_inc(lane[g], 1)

                    def lower(a):
                        return a[0:D, :]

                    def upper(a):
                        return a[D:P, :]
                    if name == "gat2":
                        each("src_t", lambda g: biased(tl(g, 0), bank[g][0][:, :], ACT.Relu, "g_b1"))
                        each("dst_t", lambda g: biased(tl(g, 1), bank[g][1][:, :], ACT.Copy))
                        each("dst", lambda g: biased(tl(g, 1), tl(g, 10), ACT.Relu, "g_b1"))
                    elif name[:2] == "tr" and l:
                        vb, vs = v(f"bn_b{l - 1}"), v(f"bn_s{l - 1}")
                        each("src_t", lambda g: f(lower(tl(g, 0)), lower(bank[g][0]), ACT.Relu, bias=vb[0:D, :],
                                                  scale=vs[0:D, :]))
                        each("src", lambda g: biased(upper(tl(g, 1)), upper(bank[g][0]), ACT.Copy))
                        each("dst", lambda g: f(upper(tl(g, 2)), upper(tl(g, 10)), ACT.Relu, bias=vb[D:P, :],
                                                scale=vs[D:P, :]))
                    else:
                        each("src_t", lambda g: biased(lower(tl(g, 0)), lower(bank[g][0]), ACT.Copy))
                        each("src", lambda g: biased(upper(tl(g, 1)), upper(bank[g][0]), ACT.Copy))
                        if name == "tr0":
                            each("dst", lambda g: biased(upper(tl(g, 2)), upper(tl(g, 10)), ACT.Copy))
                    if name[:3] == "gat":
                        each("z_p", lambda g: biased(tl(g, 2), bank[g][0][:, :], ACT.Copy, scale=0.2))
                    else:
                        each("q_p", lambda g: f(upper(tl(g, 3)), upper(bank[g][0]), ACT.Identity,
                                                bias=v(f"bq{l}")[D:P, :]))
                    for g, k, c, r, use in group:
                        pg, pk = before(g, k)
                        act.wait_ge(lane[g], pz.at(g, k, "s_p"))
                        f(L[g][4][:, 1:W + 1], bank[g][1][:, :], ACT.Copy)
                        act.wait_ge(lane[pg], pz.at(pg, pk, "s"))
                        of, to_ = (W, 0) if way > 0 else (1, W + 1)
                        f(L[g][4][:, to_:to_ + 1], L[pg][4][:, of:of + 1], ACT.Copy).then_inc(lane[g], 1)
                    for g, k, c, r, use in group:
                        act.wait_ge(lane[g], pz.at(g, k, "hi"))
                        f(tl(g, 7), tl(g, 7), ACT.Exp)
                        f(tl(g, 6), tl(g, 6), ACT.Exp).then_inc(lane[g], 1)
                    if name[:2] == "tr":
                        each("rows", lambda g: biased(orow[g][:, :, D:P],
                                                      bank[g][1][:, 0:4 * D].rearrange("p (j d) -> p j d", d=D),
                                                      ACT.Copy))
                sweep_groups(act, work)

            def passes(name):
                pz = ph[name]

                def work(group):
                    def each(before_, make):
                        for g, k, c in group:
                            act.wait_ge(lane[g], pz.at(g, k, before_))
                            make(g).then_inc(lane[g], 1)

                    def norm(i):
                        each(f"y{i}_p", lambda g: biased(tl(g, 3), bank[g][0][:, :], ACT.Square, y_bias(name, i)))
                        each(f"var{i}_p", lambda g: biased(tl(g, 4), bank[g][1][:, :], ACT.Sqrt, eps[:, :]))
                    if name == "e12":
                        each("a_t", lambda g: biased(tl(g, 1), bank[g][0][:, :], ACT.Relu, "g_b2", 0.5))
                    elif name in ("n2", "n3"):
                        l = int(name[1]) - 2
                        each("a_t", lambda g: biased(tl(g, 1), bank[g][0][:, :], ACT.Relu, f"bn_b{l}", v(f"bn_s{l}")))
                    elif name != "nS":
                        each("a_t", lambda g: biased(tl(g, 1), bank[g][0][:, :], ACT.Copy))
                    if "lin" in pz.steps:
                        func, bias = {"e01": (ACT.Relu, "bias1"), "e21": (ACT.Relu, "s_b1"), "e22": (ACT.Relu, "s_b2"),
                                      "e31": (ACT.Identity, "bs0"), "e32": (ACT.Identity, "bs1"),
                                      "n2": (ACT.Identity, "bs1")}[name]
                        each("lin_p", lambda g: biased(tl(g, 4), bank[g][0][:, :], func, bias))
                    if name == "e12":
                        norm(0)
                        each("n0", lambda g: biased(tl(g, 1), tl(g, 6), ACT.Gelu, "g_lnb", v("g_lng")))
                        norm(1)
                        each("n1", lambda g: biased(tl(g, 2), tl(g, 6), ACT.Gelu, "g_lnrb", v("g_lnrg")))
                        each("c_t", lambda g: biased(tl(g, 5), bank[g][0][:, :], ACT.Copy))
                        norm(2)
                    elif "y0_p" in pz.steps:
                        each("c_t", lambda g: biased(tl(g, 5), bank[g][0][:, :], ACT.Copy))
                        norm(0)
                    if name == "nS":
                        for g, k, c in group:
                            act.wait_ge(lane[g], pz.begin(g, k))
                            act.wait_ge(loaded[g], ld[name].after(g, k))
                            biased(tl(g, 3), tl(g, 7), ACT.Square).then_inc(lane[g], 1)
                    elif "q" in pz.steps:
                        each("o", lambda g: biased(tl(g, 3), tl(g, 7), ACT.Square))
                pass_groups(act, pz.chunks, work)

            def batchnorm(l):
                one(f"bn{l}_var", col(4), v("var"), ACT.Sqrt, eps[:, :])
                act.wait_ge(s_set, SQ[f"bn{l}_done"])
            rgcn("rg1")
            passes("e01")
            rgcn("rg2")
            passes("e02")
            if upto >= 2:
                soft("gat1")
                soft("gat2")
                passes("e12")
            if upto >= 3:
                sage("sage1")
                passes("e21")
                sage("sage2")
                passes("e22")
            if upto >= 4:
                soft("tr0")
                passes("e31")
                passes("nS")
                batchnorm(0)
                soft("tr1")
                passes("e32")
                passes("n2")
                batchnorm(1)
                soft("tr2")
                passes("n3")
                passes("e33")

        @block.vector
        def _(dve):
            V = nc.vector

            def chained(ins):
                links[0] += 1
                ins.then_inc(s_link, 1)
                dve.wait_ge(s_link, links[0])

            for g in range(LANES):
                for i in range(NT):
                    if g or i > 2:
                        V.memset(L[g][i][:, :], 0.0)
                V.memset(orow[g][:, :, :], 0.0)
            chained(V.memset(stats[:, :, :], 0.0))

            def S(i):
                return L[1][i][:, 0:T]

            def S0(i):
                return L[0][i][:, 0:T]
            DST, TYP, ENDS, FIRST, RINV, KEEP, KEEPB, ONE, CNT, ACC = (S(i) for i in (0, 1, 3, 4, 5, 6, 7, 8, 9, 10))
            PICK, RUN1, EI, ACCB, PREV, NEXT = (S0(i) for i in (5, 6, 7, 8, 3, 4))
            lastk, carry, cin = L[3][0], L[3][2], L[3][3]
            dve.wait_ge(s_in, 4 * 16)
            V.tensor_copy(DST, L[0][0][:, 0:T].bitcast(I32))
            V.tensor_copy(PREV, L[0][1][:, 0:T].bitcast(I32))
            V.tensor_copy(NEXT, L[0][2][:, 0:T].bitcast(I32))
            V.tensor_copy(TYP, recg[:, :, 1:2].rearrange("p t k -> p (t k)"))
            dve.wait_ge(s_const, CONSTS)
            chained(V.tensor_copy(EI, iota_e[:, :]))
            chained(V.tensor_tensor(FIRST, DST, PREV, ALU.not_equal))
            chained(V.tensor_tensor(ENDS, DST, NEXT, ALU.not_equal))
            V.tensor_scalar(KEEP, FIRST, -1.0, 1.0, ALU.mult, ALU.add)
            chained(V.tensor_scalar(KEEPB, ENDS, -1.0, 1.0, ALU.mult, ALU.add))

            def counts(a, keep, way, cmp, acc):
                def rev(x):
                    return turned(x, way)

                def one_(r):
                    if r < R:
                        chained(V.tensor_scalar(ONE, TYP, float(r), None, ALU.is_equal))
                    else:
                        chained(V.tensor_tensor(ONE, FIRST, EI, ALU.mult))

                kinds = R + 1 if way > 0 else R
                edge = T - 1 if way > 0 else 0
                chained(V.memset(lastk[:, 0:16], 0.0))
                for r in range(kinds):
                    one_(r)
                    chained(V.tensor_tensor_scan(rev(CNT), rev(keep), rev(ONE), 0.0, ALU.mult, ALU.add))
                    chained(V.tensor_copy(lastk[:, r:r + 1], CNT[:, edge:edge + 1]))
                chained(V.tensor_reduce(PICK[:, 0:1], keep, axis=AX.X, op=ALU.min))
                V.tensor_copy(lastk[:, 16:32], PICK[:, 0:1].to_broadcast([P, 16])).then_inc(s_set, 1)
                dve.wait_ge(s_set, SQ[a + "_turn"])
                chained(V.tensor_copy(carry[16 * 0:16, 256:256 + P], bank[0][1][0:16, 0:P]))
                chained(V.memset(carry[0:16, 0:P + 1], 0.0))
                into = carry[0:16, 1:P + 1] if way > 0 else carry[0:16, 0:P]
                V.tensor_tensor_scan(rev(into), rev(carry[0:16, 256:256 + P]), rev(bank[0][0][0:16, 0:P]), 0.0,
                                     ALU.mult, ALU.add).then_inc(s_set, 1)
                dve.wait_ge(s_set, SQ[a + "_back"])
                chained(V.tensor_copy(cin[:, 0:16], bank[0][0][:, 0:16]))
                chained(V.memset(acc, 0.0))
                for r in range(kinds):
                    one_(r)
                    to = CNT if r < R else RUN1
                    chained(V.tensor_tensor_scan(rev(to), rev(keep), rev(ONE), cin[:, r:r + 1], ALU.mult, ALU.add))
                    if r < R:
                        chained(V.scalar_tensor_tensor(PICK, TYP, float(r), CNT, cmp, ALU.mult))
                        chained(V.tensor_tensor(acc, acc, PICK, ALU.add))
            counts("f", KEEP, 1, ALU.is_lt, ACC)
            counts("b", KEEPB, -1, ALU.is_gt, ACCB)
            chained(V.tensor_tensor(ACC, EI, ACC, ALU.subtract))
            chained(V.tensor_tensor(pos[:, :], ACC, ACCB, ALU.add))
            chained(V.scalar_tensor_tensor(PICK, EI, 1.0, RUN1, ALU.add, ALU.subtract))
            chained(V.reciprocal(RINV, PICK))
            V.tensor_scalar(prec[:, :, 0:1].rearrange("p t k -> p (t k)"), EI, float(NP), None, ALU.add)
            V.tensor_scalar(prec[:, :, 1:2].rearrange("p t k -> p (t k)"), RUN1, float(NP), None, ALU.add)
            chained(V.tensor_scalar(ACCB, EI, float(NP), None, ALU.add))
            chained(V.tensor_tensor(PICK, DST, ACCB, ALU.subtract))
            chained(V.tensor_tensor(PICK, PICK, ENDS, ALU.mult))
            V.tensor_tensor(pidx[:, :], PICK, ACCB, ALU.add)
            V.tensor_scalar(idh[:, :], DST, float(N - 1), None, ALU.min)
            V.tensor_copy(fbf[:, 0, :], KEEP)
            V.tensor_copy(fbf[:, 1, :], FIRST)
            V.tensor_copy(fbf[:, 2, :], KEEPB)
            V.tensor_copy(fbf[:, 3, :], ENDS).then_inc(s_set, 1)

            dve.wait_ge(s_weights, 2 * 16)
            V.tensor_copy(vec[:, 0:len(LOADED)], part["loaded"])
            chained(V.tensor_scalar(mean2[:, :], mask64[:, :], 1.0 / D, None, ALU.mult))
            chained(V.tensor_tensor(center[:, :], ident[:, :], mean2[:, :], ALU.subtract))
            V.tensor_scalar(att1m[:, :], mask16[:, :], v("att1"), None, ALU.mult)
            V.tensor_scalar(att2m[:, :], mask64[:, :], v("att2"), None, ALU.mult)
            small = L[2][1]
            for n_ in ("root2", "wc", "wr", "ws2"):
                m = bd[n_].rearrange("p (a f) -> p a f", a=2)
                chained(V.tensor_reduce(small[:, 0:2], m, axis=AX.X, op=ALU.add))
                chained(V.tensor_scalar(small[:, 2:4], small[:, 0:2], 1.0 / D, None, ALU.mult))
                chained(V.tensor_tensor(m, m, small[:, 2:4].unsqueeze(2).to_broadcast([P, 2, D]), ALU.subtract))
            for l in range(2):
                Q = 3 * R
                w, parts = cw[:, l, :], [L[2][2 + i][0:Q, 0:4 * P] for i in range(3)]
                half = L[2][5][0:Q, :].bitcast(BF16)[:, 0:4 * P]
                rest = L[2][6][0:Q, 0:4 * P]
                chained(V.tensor_copy(half, w))
                chained(V.tensor_copy(parts[0], half))
                chained(V.tensor_tensor(rest, w, parts[0], ALU.subtract))
                chained(V.tensor_copy(half, rest))
                chained(V.tensor_copy(parts[1], half))
                chained(V.tensor_tensor(parts[2], rest, parts[1], ALU.subtract))
                chained(V.tensor_scalar(parts[0], parts[0], mask3[:, 0:1], None, ALU.mult))
                for i in (1, 2):
                    to = parts[0] if i == 1 else cwb[:, l, :, :].rearrange("p j m -> p (j m)")
                    chained(V.scalar_tensor_tensor(to, parts[i], mask3[:, i:i + 1], parts[0], ALU.mult, ALU.add))
            chained(V.tensor_scalar(v("alone"), v("g_b2"), 0.0, None, ALU.max))
            V.tensor_copy(v("var"), v("alone")).then_inc(s_set, 1)
            B0 = bank[0][0]

            def col(i):
                return L[0][i][:, 0:1]
            dve.wait_ge(s_set, SQ["bias_p"])
            i0 = VECS.index("bias2c")
            V.tensor_copy(vec[:, i0:i0 + 4], B0[:, 0:4]).then_inc(s_set, 1)
            for i, b_ in enumerate(("g_bcc", "g_brc")):
                dve.wait_ge(s_set, SQ[f"sd{i}"])
                chained(V.reciprocal(col(3), col(4)))
                V.scalar_tensor_tensor(col(6), B0[:, 0:1], v(b_), col(3), ALU.add, ALU.mult).then_inc(s_set, 1)
            dve.wait_ge(s_set, SQ["y2_p"])
            V.tensor_copy(v("alone"), B0[:, 0:1]).then_inc(s_set, 1)

            def normed(out_, name, i, g):
                b_ = y_bias(name, i)
                if b_ is None:
                    return V.tensor_tensor(out_, bank[g][0][:, :], tl(g, 3), ALU.mult)
                return V.scalar_tensor_tensor(out_, bank[g][0][:, :], v(b_), tl(g, 3), ALU.add, ALU.mult)

            def nodes(group):
                pz = ph["nodeA"]

                def each(before_, make):
                    for g, k, c in group:
                        dve.wait_ge(lane[g], pz.at(g, k, before_))
                        make(g).then_inc(lane[g], 1)

                def norm(i, to):
                    each(f"sd{i}", lambda g: V.reciprocal(tl(g, 3), tl(g, 4)))
                    each(f"rs{i}", lambda g: normed(tl(g, to), "nodeA", i, g))
                for g, k, c in group:
                    if type(k) is not int or k > 0:
                        dve.wait_ge(stored[g], st["nodeA"].before(g, k))
                    dve.wait_ge(lane[g], pz.at(g, k, "x1_t"))
                    V.tensor_copy(tl(g, 7), bank[g][1][:, :]).then_inc(lane[g], 1)
                norm(0, 5)
                norm(1, 6)
                each("xb_t", lambda g: V.tensor_copy(tl(g, 9), bank[g][1][:, :]))
                norm(2, 5)
                each("xc_t", lambda g: V.tensor_copy(tl(g, 8), bank[g][1][:, :]))
                each("g1_t", lambda g: V.tensor_copy(tl(g, 9), bank[g][1][:, :]))
            pass_groups(dve, NCH, nodes, peel=True)

            dve.wait_ge(s_keys, 16)
            REL, KEY, WGT = L[0][5][:, 0:T], L[0][0][:, 0:T], L[0][4][:, 0:T]

            def field(i):
                return recm[:, :, i:i + 1].rearrange("p t k -> p (t k)")
            V.memset(L[0][1][0:1, 0:1], -1.0)
            V.tensor_copy(L[0][6][:, 0:T], field(3))
            V.tensor_copy(WGT, field(2).bitcast(F32))
            chained(V.tensor_copy(REL, field(1)))
            V.scalar_tensor_tensor(KEY, L[0][6][:, 0:T], 16.0, REL, ALU.mult, ALU.add).then_inc(s_set, 1)
            dve.wait_ge(s_keys, 6 * 16)
            V.tensor_tensor(fbf[:, 0, :], KEY, L[0][2][:, 0:T], ALU.not_equal)
            V.tensor_tensor(fbf[:, 1, :], KEY, L[0][3][:, 0:T], ALU.not_equal)
            for r in range(R):
                last = V.tensor_scalar(hotm(r), REL, float(r), None, ALU.is_equal)
            last.then_inc(s_set, 1)
            dve.wait_ge(s_spg, 2 * (T // GB))
            dve.wait_ge(s_ptr1, 16)
            dve.wait_ge(s_mask, 6 * 16)
            A, B, C = (L[1][i][:, 0:T] for i in (0, 1, 2))
            chained(V.tensor_scalar(A, spg[:, :, 1:2].rearrange("p t k -> p (t k)"), -float(NP), None, ALU.add))
            chained(V.tensor_scalar(B, A, 0.0, None, ALU.is_lt))
            chained(V.tensor_scalar(C, B, -1.0, 1.0, ALU.mult, ALU.add))
            chained(V.tensor_tensor(A, A, C, ALU.mult))
            chained(V.scalar_tensor_tensor(idh[:, :], B, float(EP), A, ALU.mult, ALU.add))
            V.tensor_scalar(alone8[:, :], recm[:, :, :].rearrange("p t (a b) -> p (t a) b", b=2)[:, :, 0:1]
                            .rearrange("p t k -> p (t k)"), float(NP), None, ALU.is_lt)
            chained(V.tensor_copy(A, dst8[:, :]))
            chained(V.tensor_scalar(alone8[:, (NCH - 1) * 8:], alone8[:, (NCH - 1) * 8:], real84[:, :], None, ALU.mult))
            SPARE = L[1][3][:, 0:T]
            chained(V.tensor_scalar(SPARE, iota_e[:, :], float(SPARE_OUT), None, ALU.add))
            chained(V.tensor_tensor(A, A, SPARE, ALU.subtract))
            has = (last8, last8, last8, first8)[upto - 1]
            chained(V.tensor_tensor(B, A, has[:, :], ALU.mult))
            V.tensor_tensor(ido[:, :], B, SPARE, ALU.add).then_inc(s_set, 1)

            def scan(pz, step, before_, way, group, make):
                for g, k, c, r, use in group:
                    pg, pk = before(g, k)
                    dve.wait_ge(lane[pg], pz.at(pg, pk, step))
                    dve.wait_ge(lane[g], pz.at(g, k, before_))
                    make(g, pg).then_inc(lane[g], 1)

            def rgcn(name):
                pz = ph[name]
                l = 0 if name == "rg1" else 1

                def work(group):
                    def each(before_, make):
                        for g, k, c, r, use in group:
                            dve.wait_ge(lane[g], pz.at(g, k, before_))
                            make(g).then_inc(lane[g], 1)

                    def low(g, i):
                        return tl(g, i)[0:D, :]

                    def state(g, i):
                        return L[g][i][0:D, W - 1:W]
                    for q in range(4):
                        each(f"c{q}_p", lambda g: V.tensor_tensor(
                            tl(g, q + l), bank[g][0][:, :], tl(g, q if l == 0 else 0), ALU.mult))
                    scan(pz, "gmax", "gfirst", 1, group, lambda g, pg: V.tensor_tensor_scan(
                        low(g, 6), bank[g][0][0:D, :], low(g, 5), state(pg, 6), ALU.add, ALU.max))
                    each("glast", lambda g: V.tensor_tensor(low(g, 7), bank[g][0][0:D, :], low(g, 6), ALU.mult))
                    scan(pz, "agg", "keep", 1, group, lambda g, pg: V.tensor_tensor_scan(
                        low(g, 8), bank[g][0][0:D, :], low(g, 7), state(pg, 8), ALU.mult, ALU.add))
                sweep_groups(dve, work)

            def sage(name):
                pz = ph[name]

                def work(group):
                    scan(pz, "agg", "keep", 1, group, lambda g, pg: V.tensor_tensor_scan(
                        tl(g, 8)[0:D, :], bank[g][1][0:D, :], tl(g, 5)[0:D, :], L[pg][8][0:D, W - 1:W], ALU.mult,
                        ALU.add))
                    for g, k, c, r, use in group:
                        dve.wait_ge(stored[g], st[name].before(g, k))
                        dve.wait_ge(lane[g], pz.at(g, k, "agg_t"))
                        V.tensor_tensor(orow[g][:, :, 0:D], bank[g][0][:, 0:4 * D].rearrange("p (j d) -> p j d", d=D),
                                        rinv[:, bass.ds(c * 4, 4)].unsqueeze(2).to_broadcast([P, 4, D]),
                                        ALU.mult).then_inc(lane[g], 1)
                sweep_groups(dve, work)

            def soft(name):
                pz = ph[name]
                way = INFO[name][0]
                l = int(name[-1])
                gat = name[:3] == "gat"
                heads = {"gat1": 8, "gat2": 2}.get(name)
                end = W - 1 if way > 0 else 0

                def on(a):
                    return turned(a, way)

                def work(group):
                    def each(before_, make):
                        for g, k, c, r, use in group:
                            dve.wait_ge(lane[g], pz.at(g, k, before_))
                            make(g).then_inc(lane[g], 1)
                    if name == "gat2":
                        scan(pz, "dst", "keep", way, group, lambda g, pg: V.tensor_tensor_scan(
                            on(tl(g, 10)), on(bank[g][0][:, :]), on(tl(g, 1)), L[pg][10][:, end:end + 1], ALU.mult,
                            ALU.add))
                    else:
                        i = 0 if name == "gat1" else 10
                        scan(pz, "dst", "keep", way, group, lambda g, pg: V.tensor_tensor_scan(
                            on(tl(g, i)[D:P, :]), on(bank[g][1][D:P, :]), on(tl(g, 1)[D:P, :]),
                            L[pg][i][D:P, end:end + 1], ALU.mult, ALU.add))
                    if gat:
                        each("z_s", lambda g: V.tensor_tensor(tl(g, 3), bank[g][0][:, :], tl(g, 2), ALU.max))
                    else:
                        each("kv_p", lambda g: V.scalar_tensor_tensor(
                            tl(g, 6)[D:P, :], bank[g][1][D:P, :], v(f"bk{l}")[D:P, :], tl(g, 3)[D:P, :], ALU.add,
                            ALU.mult))
                    s0 = 0 if way > 0 else 2
                    scan(pz, "y", "reset", way, group, lambda g, pg: V.tensor_tensor_scan(
                        on(tl(g, 5)), on(L[g][4][:, s0:s0 + W]), on(bank[g][0][:, :]), L[pg][5][:, end:end + 1],
                        ALU.max, ALU.add))
                    each("y", lambda g: V.tensor_tensor(tl(g, 6), bank[g][1][:, :], tl(g, 5), ALU.subtract))
                    each("d", lambda g: V.tensor_scalar(tl(g, 7), tl(g, 6), 0.0, None, ALU.min))
                    each("lo", lambda g: V.tensor_scalar(tl(g, 6), tl(g, 6), -1.0, 0.0, ALU.mult, ALU.min))
                    if gat:
                        each("v_p", lambda g: V.tensor_tensor(tl(g, 2), bank[g][0][:, :], tl(g, 7), ALU.mult))
                        for step, before_, i, o in (("num", "wv", 2, 8), ("den", "num", 7, 9)):
                            scan(pz, step, before_, way, group, lambda g, pg: V.tensor_tensor_scan(
                                on(tl(g, o)), on(tl(g, 6)), on(tl(g, i)), L[pg][o][:, end:end + 1], ALU.mult, ALU.add))
                        n4 = 4 * heads
                        for g, k, c, r, use in group:
                            dve.wait_ge(lane[g], pz.at(g, k, "den_t"))
                            den = bank[g][1][:, :].rearrange("p (m w) -> p m w", m=n4)[:, :, 0:1].rearrange(
                                "p m w -> p (m w)")
                            if name == "gat1":
                                e = there(c, way, SWEEPS)
                                V.reciprocal(L[g][3][:, 0:n4], den).then_inc(lane[g], 1)
                                dve.wait_ge(lane[g], pz.at(g, k, "rc"))
                                V.tensor_tensor(L[g][3][:, 64:64 + n4].rearrange("p (j h) -> p j h", j=4),
                                                L[g][3][:, 0:n4].rearrange("p (j h) -> p j h", j=4),
                                                first4[:, bass.ds(e * 4, 4)].unsqueeze(2).to_broadcast([P, 4, heads]),
                                                ALU.mult).then_inc(lane[g], 1)
                            else:
                                V.reciprocal(L[g][3][:, 64:64 + n4], den).then_inc(lane[g], 1)
                        for g, k, c, r, use in group:
                            dve.wait_ge(stored[g], st[name].before(g, k))
                            dve.wait_ge(lane[g], pz.at(g, k, "rcp"))
                            V.tensor_tensor(orow[g][:, :, :].rearrange("p j (h w) -> p (j h) w", h=heads),
                                            bank[g][0][:, :].rearrange("p (m w) -> p m w", m=n4),
                                            L[g][3][:, 64:64 + n4].unsqueeze(2).to_broadcast([P, n4, P // heads]),
                                            ALU.mult).then_inc(lane[g], 1)
                    else:
                        each("v_p", lambda g: V.scalar_tensor_tensor(
                            tl(g, 7)[0:D, :], bank[g][0][0:D, :], v(f"bv{l}")[0:D, :], tl(g, 7)[0:D, :], ALU.add,
                            ALU.mult))
                        scan(pz, "nd", "wv", way, group, lambda g, pg: V.tensor_tensor_scan(
                            on(tl(g, 8)), on(tl(g, 6)), on(tl(g, 7)), L[pg][8][:, end:end + 1], ALU.mult, ALU.add))
                        each("h_t", lambda g: V.reciprocal(
                            L[g][3][:, 0:4], bank[g][0][:, :].rearrange("p (j w) -> p j w", j=4)[:, :, D:D + 1].rearrange(
                                "p j w -> p (j w)")))
                        for g, k, c, r, use in group:
                            dve.wait_ge(stored[g], st[name].before(g, k))
                            dve.wait_ge(lane[g], pz.at(g, k, "rcp"))
                            V.tensor_tensor(orow[g][:, :, 0:D],
                                            bank[g][0][:, :].rearrange("p (j w) -> p j w", j=4)[:, :, 0:D],
                                            L[g][3][:, 0:4].unsqueeze(2).to_broadcast([P, 4, D]),
                                            ALU.mult).then_inc(lane[g], 1)
                sweep_groups(dve, work)

            def passes(name):
                pz = ph[name]
                mask = {"e01": last8, "e02": last8, "e12": last8, "e21": last8, "e22": last8, "e31": first8,
                        "e32": last8}.get(name)

                def work(group):
                    def each(before_, make):
                        for g, k, c in group:
                            dve.wait_ge(lane[g], pz.at(g, k, before_))
                            make(g).then_inc(lane[g], 1)

                    def tile7_free(g, k):
                        if name != last_pass:
                            dve.wait_ge(stored[g], st[name].before(g, k))
                        elif type(k) is not int or k > 0:
                            dve.wait_ge(put[g], scattered.before(g, k))

                    def norm(i):
                        each(f"sd{i}", lambda g: V.reciprocal(tl(g, 3), tl(g, 4)))
                        each(f"rs{i}", lambda g: normed(tl(g, 6), name, i, g))
                    if "b" in pz.steps:
                        each("b_t", lambda g: V.tensor_copy(tl(g, 2), bank[g][1][:, :]))
                    for i in range(3):
                        if f"y{i}_p" in pz.steps:
                            norm(i)
                    if name in ("nOut", "eOut"):
                        for g, k, c in group:
                            dve.wait_ge(lane[g], pz.begin(g, k))
                            dve.wait_ge(loaded[g], ld[name].after(g, k))
                            tile7_free(g, k)
                            V.tensor_copy(tl(g, 7), tl(g, 0)).then_inc(lane[g], 1)
                    elif "o" in pz.steps:
                        for g, k, c in group:
                            tile7_free(g, k)
                            dve.wait_ge(lane[g], pz.at(g, k, "o_t"))
                            if mask is None:
                                V.tensor_copy(tl(g, 7), bank[g][1][:, :]).then_inc(lane[g], 1)
                            else:
                                V.tensor_tensor(tl(g, 7).rearrange("p (j d) -> p j d", d=D),
                                                bank[g][1][:, :].rearrange("p (j d) -> p j d", d=D),
                                                mask[:, bass.ds(c * 8, 8)].unsqueeze(2).to_broadcast([P, 8, D]),
                                                ALU.mult).then_inc(lane[g], 1)
                    if "st" in pz.steps:
                        l = 1 if name in ("e32", "n2") else 0
                        for g, k, c in group:
                            pg, pk = before(g, k)
                            dve.wait_ge(lane[pg], pz.at(pg, pk, "st"))
                            dve.wait_ge(lane[g], pz.at(g, k, "st_p"))
                            V.tensor_tensor(stats[:, l, :], bank[g][1][:, 0:4], stats[:, l, :],
                                            ALU.add).then_inc(lane[g], 1)
                pass_groups(dve, pz.chunks, work, peel=name == last_pass)

            def batchnorm(l):
                m = L[0][0]
                dve.wait_ge(s_set, SQ[f"bn{l}_p"])
                chained(V.tensor_scalar(m[:, 0:2], B0[:, 0:2], 1.0 / N, None, ALU.mult))
                chained(V.tensor_tensor(m[:, 2:3], m[:, 0:1], m[:, 0:1], ALU.mult))
                V.tensor_tensor(v("var"), m[:, 1:2], m[:, 2:3], ALU.subtract).then_inc(s_set, 1)
                dve.wait_ge(s_set, SQ[f"bn{l}_sd"])
                chained(V.reciprocal(m[:, 3:4], col(4)))
                chained(V.tensor_tensor(v(f"bn_s{l}"), v(f"gamma{l}"), m[:, 3:4], ALU.mult))
                chained(V.tensor_tensor(m[:, 4:5], m[:, 0:1], v(f"bn_s{l}"), ALU.mult))
                V.tensor_tensor(v(f"bn_b{l}"), v(f"beta{l}"), m[:, 4:5], ALU.subtract).then_inc(s_set, 1)
            rgcn("rg1")
            passes("e01")
            rgcn("rg2")
            passes("e02")
            if upto >= 2:
                soft("gat1")
                soft("gat2")
                passes("e12")
            if upto >= 3:
                sage("sage1")
                passes("e21")
                sage("sage2")
                passes("e22")
            if upto >= 4:
                soft("tr0")
                passes("e31")
                passes("nS")
                batchnorm(0)
                soft("tr1")
                passes("e32")
                passes("n2")
                batchnorm(1)
                soft("tr2")
                passes("n3")
                passes("e33")
            else:
                passes("nOut")
                passes("eOut")


def pack(a):
    import numpy as np

    f32 = np.float32
    x = {n: np.asarray(b) for n, b in a.items()}

    def padded(b, fill):
        return np.concatenate([b, np.full((EP - E,) + b.shape[1:], fill, b.dtype)])
    dst = padded(x["dst"].astype(np.int32), PAD_DST)
    prev = np.concatenate([np.full(1, -1, np.int32), dst[:-1]])
    nxt = np.concatenate([dst[1:], np.full(1, -1, np.int32)])
    edge_dst = np.ascontiguousarray(np.stack([dst, prev, nxt]).reshape(3, P, T).transpose(1, 0, 2))
    rec = np.stack([padded(x["src"].astype(np.int32), 0), padded(x["edge_type_14"].astype(np.int32), 0),
                    padded(np.ascontiguousarray(x["edge_weight1"][:, 0]).view(np.int32), 0), dst], axis=1)

    def twice(m):
        z = np.zeros((P, P), f32)
        z[:D, :D] = m
        z[D:, D:] = m
        return z
    g, s, r3 = (lambda n: x["L1_gnn_" + n]), (lambda n: x["L2_gnn_" + n]), (lambda n: x["L3_gnn_" + n])
    mats = {"root1": x["L0_gnn_root1"], "root2": x["L0_gnn_root2"], "wc": g("wc"), "wr": g("wr"), "wl1": s("Wl1").T,
            "wr1": s("Wr1").T, "wl2": s("Wl2").T, "wr2": s("Wr2").T, "ws0": r3("Ws")[0], "ws1": r3("Ws")[1],
            "ws2": r3("Ws")[2]}
    parts = {n: twice(m) for n, m in mats.items()}
    parts["basew"] = x["L0_gnn_bases2"].reshape(4, 2 * D, D).transpose(1, 0, 2).reshape(P, 4 * D)
    parts["gw"] = np.concatenate([g("w1_l"), g("w1_r")])
    parts["g2l"], parts["g2r"] = g("w2_l"), g("w2_r")
    we = np.zeros((P, 2 * P), f32)
    we[0] = np.concatenate([g("w1_e")[0], g("w2_e")[0]])
    parts["we"] = we
    wkv, wq = np.zeros((P, 3, P), f32), np.zeros((P, 3, P), f32)
    for l in range(3):
        wkv[:D, l, :D], wkv[:D, l, D:] = r3("Wv")[l], r3("Wk")[l]
        wq[D:, l, D:] = r3("Wq")[l]
    parts["wkv"], parts["wq"] = wkv.reshape(P, -1), wq.reshape(P, -1)
    vecs = [x["L0_gnn_bias1"], x["L0_gnn_bias2"], g("b1"), g("b2"), g("bc"), g("ln_g"), g("ln_b"), g("br"), g("lnr_g"),
            g("lnr_b"), g("att1").reshape(-1), g("att2").reshape(-1), s("b1"), s("b2")]
    vecs += [r3(n)[l] for n in ("bq", "bk", "bv", "bs") for l in range(3)]
    vecs += [r3(n)[l] for n in ("gamma", "beta") for l in range(2)]
    parts["loaded"] = np.stack([b if b.shape[0] == P else np.concatenate([b, b]) for b in vecs], axis=1)
    packed = np.concatenate([parts[n] for n, _ in PACKED], axis=1)
    w1 = x["L0_gnn_w1"].transpose(0, 2, 1, 3).reshape(R, 4 * P)
    comp = np.repeat(x["L0_gnn_comp2"].reshape(R, 8, 1), D, axis=2).reshape(R, 4 * P)
    relw = np.concatenate([np.stack([w1, comp], axis=1)] * 3)
    return {"x": x["x"], "edge_dst": edge_dst, "edge_rec": rec.reshape(P, T, 4), "packed": packed.astype(f32),
            "relw": relw.astype(f32)}


def kernel(**inputs):
    import concourse.bacc as bacc
    import numpy as np
    from concourse.bass_utils import run_bass_kernel_spmd

    nc = bacc.Bacc("TRN2", target_bir_lowering=False, num_devices=1)
    arrays = {f"in_{n}": np.ascontiguousarray(a) for n, a in pack(inputs).items()}
    t = {n[3:]: nc.dram_tensor(n, a.shape, mybir.dt.from_np(a.dtype), kind="ExternalInput").ap()
         for n, a in arrays.items()}
    out = nc.dram_tensor("out", (OUT_ROWS, D), F32, kind="ExternalOutput").ap()
    build(nc, t, out, UPTO)
    r = run_bass_kernel_spmd(nc, [arrays], core_ids=[0])
    return r.results[0]["out"][:N]
```

```python
from contextlib import ExitStack

import concourse.bass as bass
from concourse import mybir

F32 = mybir.dt.float32
BF16 = mybir.dt.bfloat16
I32 = mybir.dt.int32
ALU = mybir.AluOpType
ACT = mybir.ActivationFunctionType
AX = mybir.AxisListType

P = 128
D = 64
N = 100000
E = 50000
R = 14
W = 512
LANES = 4
SLOTS = 8
CROWS = 1024
EP = 50176
NP = 100352
T = EP // P
SWEEPS = EP // W
NCH = NP // CROWS
ECH = EP // CROWS
LASTROWS = N - (NCH - 1) * CROWS
LASTP = LASTROWS // 8
SPARE_OUT = N + 256
PAD_DST = N + 200
OUT_ROWS = SPARE_OUT + EP
CONSTS = 40
BIG = 1.0e30
EPS = 1.0e-5
GB = 28


LOADED = ["bias1", "bias2", "g_b1", "g_b2", "g_bc", "g_lng", "g_lnb", "g_br", "g_lnrg", "g_lnrb", "att1", "att2",
          "s_b1", "s_b2"] + [f"{n}{i}" for n in ("bvq", "bk", "bs") for i in range(3)] + \
    [f"{n}{i}" for n in ("gamma", "beta") for i in range(2)]
VECS = LOADED + ["bias2c", "g_bcc", "g_brc", "bs2c", "alone", "bn_s0", "bn_b0", "bn_s1", "bn_b1", "mean", "var"]
NVEC = len(VECS)
MATS = ["root1", "root2", "wc", "wr", "wl1", "wr1", "wl2", "wr2", "ws0", "ws1", "ws2"]

PACKED = [(n, P) for n in MATS] + [("basew", 4 * D), ("gw", P), ("g2l", P), ("g2r", P), ("we", 2 * P),
                                   ("wvq", 3 * P), ("wk", 3 * P), ("loaded", len(LOADED))]
BIGW = sum(w for _, w in PACKED)


class Phase:

    def __init__(self, names, chunks, base, sweep=False, shift=None):
        self.sweep, self.names = sweep, list(names)
        self.shift = len(names) // LANES if shift is None else shift
        self.steps = {n: i + 1 for i, n in enumerate(names)}
        self.first = list(base)
        self.chunks = chunks
        self.n = len(names)
        assert len(self.steps) == self.n
        self.last = [base[g] + self.n * len(range(g, chunks, LANES)) for g in range(LANES)]

    def at(self, g, k, step):
        return k * self.n + (self.first[g] + self.steps[step])

    def after(self, step):
        return self.names[self.names.index(step) + 1]

    def begin(self, g, k):
        return k * self.n + self.first[g]


class Seq:

    def __init__(self, names):
        self.steps = {n: i + 1 for i, n in enumerate(names)}
        assert len(self.steps) == len(names)

    def __getitem__(self, name):
        return self.steps[name]


class Dmas:

    def __init__(self, per, chunks, base, lanes=LANES):
        self.per, self.first, self.lanes = per, list(base), lanes
        self.last = [base[g] + 16 * per * len(range(g, chunks, lanes)) for g in range(lanes)]

    def before(self, g, k):
        return k * (16 * self.per) + self.first[g]

    def after(self, g, k):
        return k * (16 * self.per) + (self.first[g] + 16 * self.per)


def in_turns(eng, pz, work, peel_last=False):
    unroll = SLOTS // LANES if pz.sweep else 1
    turns, rest = pz.chunks // LANES, pz.chunks % LANES
    assert turns % unroll == 0
    steps = list(pz.steps)

    def chunk_of(i, h, g):
        back = 0
        if h < 0:
            h, back = h + unroll, 1
        turn_ = h - back * unroll
        chunk = (g, i * unroll + turn_, i * (unroll * LANES) + (turn_ * LANES + g))
        return chunk + ((h * LANES + g, i - back) if pz.sweep else ())

    def issue(step, chunk):
        work(lambda name: (chunk,) if name == step else ())

    def turn(i, h, lanes=LANES, first=False):
        for s in range(len(steps)):
            for g in range(LANES):
                if s >= g * pz.shift:
                    if g < lanes:
                        issue(steps[s - g * pz.shift], chunk_of(i, h, g))
                elif not first:
                    issue(steps[s - g * pz.shift], chunk_of(i, h - 1, g))

    def full(i, first=False):
        for h in range(unroll):
            turn(i, h, first=first and h == 0)
    full(0, True)
    loops = turns // unroll
    with eng.Fori(1, loops - peel_last, 1) as i:
        full(i)
    if peel_last:
        full(loops - 1)
    turn(loops, 0, lanes=rest)
    for s in range(len(steps)):
        for g in range(rest):
            if s < g * pz.shift:
                issue(steps[s - g * pz.shift], chunk_of(loops, 0, g))


def in_order(eng, chunks, work):
    turns = chunks // LANES
    with eng.Fori(0, turns, 1) as i:
        work([(g, i, i * LANES + g) for g in range(LANES)])
    if chunks % LANES:
        work([(g, turns, turns * LANES + g) for g in range(chunks % LANES)])


def slots_in_order(eng, work, peel=False):
    turns = SWEEPS // SLOTS

    def turn(i):
        for h in range(2):
            work([(g, i * 2 + h, i * SLOTS + (h * LANES + g), h * LANES + g, i) for g in range(LANES)])
    if peel:
        turn(0)
    with eng.Fori(int(peel), turns, 1) as i:
        turn(i)
    work([(g, turns * 2, turns * SLOTS + g, g, turns) for g in range(SWEEPS - turns * SLOTS)])


def build(nc, t, out):
    with ExitStack() as ctx:
        def sb(name, shape, dt=F32):
            return ctx.enter_context(nc.sbuf_tensor(name, shape, dt))

        def sem(name):
            return ctx.enter_context(nc.semaphore(name))

        def dram(name, shape, dt=F32):
            return nc.dram_tensor(name, shape, dt, kind="Internal").ap()

        names = ["x1", "xa", "xb", "h2", "xc", "g1", "g2"]
        tab = {n: dram(f"tab_{n}", (NP + EP, D)) for n in names}
        h1 = dram("tab_h1", (EP + 1, P))
        agg = [dram(f"agg_{i}", (EP, D)) for i in range(4)]
        agg2 = dram("agg_gat2", (EP, P))
        aggh = [dram(f"agg_tr{i}", (EP, P)) for i in range(3)]
        xdst = dram("x_dst", (EP, D))
        rec = dram("rec", (EP, 4), I32)
        ptr = dram("ptr", (NP + EP, 2), I32)
        rows = dram("rows", (3, EP))
        dsts = dram("dsts", (2, EP), I32)
        keys = dram("keys", (1, EP + 2))
        flag = dram("flag", (6, EP), BF16)
        hot = dram("hot", (3 * R, EP), BF16)
        wrow = dram("wrow", (9, EP), BF16)

        def rows8(a, lo, count, width):
            return a[lo:lo + count * CROWS, :].rearrange("(c p j) d -> p c (j d)", p=P, j=8)

        def rows4(a, lo, width):
            return a[lo:lo + EP, :].rearrange("(c p j) d -> p c j d", p=P, j=4)

        ident = sb("ident", [P, P])
        center = sb("center", [P, P])
        mean2 = sb("mean2", [P, P])
        fold2 = sb("fold2", [P, D])
        mask64 = sb("mask64", [P, P])
        mask16 = sb("mask16", [P, P])
        sums = sb("sums", [P, 2, P])
        spread = sb("spread", [D, 4, P])
        mask3 = sb("mask3", [3 * R, 3])
        scale1 = sb("scale1", [P, P])
        zrow = sb("zrow", [1, P])
        sel = sb("sel", [6, 6, P], BF16)
        selbig = sb("selbig", [6, 6, P], BF16)
        eps = sb("eps", [P, 1])
        big = sb("big", [P, BIGW])
        at = 0
        part = {}
        for n, w in PACKED:
            part[n] = big[:, at:at + w]
            at += w
        bd = {n: part[n] for n in MATS}
        vec = sb("vec", [P, NVEC])
        cw_all = sb("cw", [P, 2, 4 * P])
        cw = cw_all[0:3 * R, :, :]
        cwb = sb("cwb", [3 * R, 2, 4, P], BF16)
        basew = part["basew"].rearrange("p (j d) -> p j d", j=4)
        gw, g2l, g2r = part["gw"], part["g2l"], part["g2r"]
        we = sb("we9", [9, 2, P], BF16)
        mask9 = sb("mask9", [9, 3])
        wvq = part["wvq"].rearrange("p (l m) -> p l m", l=3)
        wk = part["wk"].rearrange("p (l m) -> p l m", l=3)
        att1m = sb("att1m", [P, P])
        att2m = sb("att2m", [P, P])
        recg = sb("recg", [P, T, 4], I32)
        spg = sb("spg", [P, T, 2], I32)
        idx = sb("idx", [P, 2, 4 * SLOTS], I32)
        idh = sb("idh", [P, T], I32)
        idd = sb("idd", [P, T], I32)
        ido = sb("ido", [P, T], I32)
        dst8 = sb("dst8", [P, T], I32)
        real84 = sb("real84", [P, 1])
        fbf = sb("fbf", [P, 4, T], BF16)
        rinv = sb("rinv", [P, T])
        first4 = sb("first4", [P, T])
        last8 = sb("last8", [P, T])
        first8 = sb("first8", [P, T])
        alone8 = sb("alone8", [P, NCH * 8])
        stats = sb("stats", [P, 2, 4])
        pos = sb("pos", [P, T], I32)
        pidx = sb("pidx", [P, T], I32)
        prec = sb("prec", [P, T, 2], I32)
        sidx = sb("sidx", [P, 2, GB // 2], I32)
        srec = sb("srec", [P, 2, GB // 2, 4], I32)
        iota_e = sb("iota_e", [P, T], I32)
        recm = sb("recm", [P, T, 4], I32)
        orow = [sb(f"orow{g}", [P, 4, P]) for g in range(LANES)]
        NT = 11
        L = [[sb(f"lane{g}_{i}", [P, W + 2]) for i in range(NT)] for g in range(LANES)]
        ft = [sb(f"flags{g}", [6, W], BF16) for g in range(LANES)]
        hots = [sb(f"hots{g}", [3 * R, W], BF16) for g in range(LANES)]
        wr_ = [sb(f"wrow{g}", [9, W], BF16) for g in range(LANES)]
        ring = [sb(f"ring{r}", [P, 4, P]) for r in range(SLOTS)]
        hring = [cw_all[:, g, :].rearrange("p (j d) -> p j d", d=P) for g in range(2)] + \
            [sb(f"hring{g}", [P, 4, P]) for g in range(2, LANES)]
        bank = [[ctx.enter_context(nc.psum_tensor(f"bank{g}_{i}", [P, W], F32)) for i in range(2)]
                for g in range(LANES)]

        def tl(g, i):
            return L[g][i][:, 0:W]

        def v(name):
            i = VECS.index(name)
            return vec[:, i:i + 1]

        def hotm(r):
            return L[2][r // 2][:, :].bitcast(BF16)[:, 400 * (r % 2):400 * (r % 2) + T]

        lane = [sem(f"lane{g}_step") for g in range(LANES)]
        loaded = [sem(f"lane{g}_loaded") for g in range(LANES)]
        stored = [sem(f"lane{g}_stored") for g in range(LANES)]
        gathered = [sem(f"slot{r}_gathered") for r in range(SLOTS)]
        s_const = sem("constants_built")
        s_weights = sem("weights_loaded")
        s_in = sem("edges_loaded")
        s_link = sem("vector_chain")
        s_set = sem("setup_step")
        s_ptr0 = sem("ptr_filled")
        s_idx = sem("indices_copied")
        s_sc = [sem(f"setup_moved{h}") for h in range(2)]
        saved = [sem(f"slot{r}_saved") for r in range(SLOTS)]
        s_mid = sem("masks_moved")
        put = [sem(f"lane{g}_scattered") for g in range(LANES)]
        s_mask = sem("masks_loaded")
        s_rec = sem("records_loaded")
        s_keys = sem("keys_moved")
        s_spg = sem("pointers_gathered")
        s_ptr1 = sem("ptr_loaded")
        links = [0]

        def layernorm(i):
            return [f"y{i}_p", f"y{i}", f"var{i}_p", f"sd{i}", f"rs{i}"]

        NODE_A = ["x_t", "x", "x1_p", "x1", "x1_t", "x1_o"] + layernorm(0) + ["xa_o", "n0_t", "n0"] + layernorm(1) + \
            ["xb_o", "n1_t", "n1", "h2_p", "h2", "h2_t", "h2_o", "h3_p", "h3"] + layernorm(2) + \
            ["xc_o", "n2_t", "n2", "g1_p", "g1", "g1_t", "g1_o"]
        RGCN = [f"c{j}{s}" for j in range(4) for s in ("_p", "")] + \
            ["msg_p", "msg", "gfirst", "gmax", "glast", "gpick", "keep", "agg", "agg_t", "agg_o"]
        RG1 = ["x_t", "x"] + [f"x{j}{s}" for j in range(4) for s in ("_t", "")] + RGCN
        RG2 = ["x0_t", "x0"] + RGCN
        SAGE = ["src_t", "src", "keep", "agg", "agg_t", "agg_o"]
        SOFT = ["s_p", "s", "reset", "y", "d", "lo", "hi", "ex", "v_p", "wv"]
        GAT1 = ["src_t", "src", "dst_in", "keep", "dst", "z_p", "z_s", "z"] + SOFT + \
            ["num", "den", "num_t", "den_t", "rc", "rcp", "rows"]
        GAT2 = ["src_t", "src", "dst_t", "dst_in", "keep", "dst", "dst_b", "z_p", "z_s", "z"] + SOFT + \
            ["num", "den", "num_t", "den_t", "rcp", "rows"]
        TR = ["src_t", "src", "dst_in", "keep", "dst", "dst_b", "q_p", "q", "kv_p", "qk"] + [s for s in SOFT if s != "v_p"] + \
            ["nd", "nd_t", "h_t", "rcp", "rows", "hrows"]
        IN2 = ["a_t", "a", "b_t", "b"]
        LIN = ["lin_p", "lin"]
        OUT = ["o_t", "o"]
        STAT = ["q", "st_p", "st"]
        plan = [("nodeA", NODE_A, NCH, 1, 6, 0),
                ("rg1", RG1, SWEEPS, 2, 1, 8), ("e01", IN2 + LIN + OUT, ECH, 2, 1, 0),
                ("rg2", RG2, SWEEPS, 2, 1, 4), ("e02", IN2 + ["c_t", "c"] + layernorm(0) + ["rm", "o"], ECH, 3, 1, 0)]
        plan += [("gat1", GAT1, SWEEPS, 3, 1, 4), ("gat2", GAT2, SWEEPS, 3, 1, 4),
                 ("e12", ["heads", "a_t", "a"] + layernorm(0) + ["o0", "n0_t", "ge0"] + layernorm(1) +
                  ["o1", "n1_t", "ge1", "c_t", "c"] + layernorm(2) + ["rm", "o"], ECH, 3, 1, 0)]
        plan += [("sage1", SAGE, SWEEPS, 1, 1, 4), ("e21", IN2 + LIN + OUT, ECH, 2, 1, 0),
                 ("sage2", SAGE, SWEEPS, 1, 1, 4),
                 ("e22", IN2 + LIN + ["c_t", "c"] + layernorm(0) + ["rm", "o"], ECH, 3, 1, 0)]
        plan += [("tr0", TR, SWEEPS, 2, 1, 4), ("e31", IN2 + LIN + OUT + STAT, ECH, 2, 1, 0),
                 ("nS", STAT, NCH, 1, 0, 0), ("tr1", TR, SWEEPS, 2, 1, 4),
                 ("e32", IN2 + LIN + OUT + STAT, ECH, 2, 1, 0),
                 ("n2", ["a_t", "a"] + LIN + OUT + STAT, NCH, 1, 1, 0), ("tr2", TR, SWEEPS, 2, 1, 4),
                 ("n3", ["a_t", "a", "c_t", "c"] + layernorm(0) + ["o"], NCH, 2, 1, 0),
                 ("e33", IN2 + ["c_t", "c"] + layernorm(0) + ["o"], ECH, 3, 0, 0)]
        SHIFTS = {"nS": 0, "e12": 1, "e33": 0}
        ph, ld, st, ga = {}, {}, {}, {}
        b0, b1, b2, b3 = [200] * LANES, [0] * LANES, [0] * LANES, [0] * SLOTS
        for name, steps, chunks, loads, stores, gathers in plan:
            ph[name] = Phase(steps, chunks, b0, sweep=gathers > 0, shift=SHIFTS.get(name))
            ld[name] = Dmas(loads, chunks, b1)
            st[name] = Dmas(stores, chunks, b2)
            ga[name] = Dmas(gathers, chunks if gathers else 0, b3, SLOTS)
            b0, b1, b2, b3 = ph[name].last, ld[name].last, st[name].last, ga[name].last
        last_pass = "e33"
        scattered = Dmas(8, ECH, [0] * LANES)
        START = 200

        LNP = lambda i: [f"y{i}_p", f"sq{i}", f"var{i}_p", f"sd{i}", f"n{i}"]
        SQ = Seq(["f_last", "f_turn", "f_scan", "f_back", "b_last", "b_turn", "b_scan", "b_back", "setup",
                  "att", "bias_p", "bias"] + LNP(0) + ["ge0"] + LNP(1) + ["ge1", "y2_p", "alone", "keys", "flags", "rows"] +
                 [f"bn{l}_{s}" for l in range(2) for s in ("p", "var", "sd", "done")])
        MIDS = 1 + 1 + 3 + 1 + 4
        MIDT = MIDS + 2 + 3 * R + 9

        INFO = {
            "rg1": (1, t["x"], None, agg[0]), "rg2": (1, tab["x1"], None, agg[1]),
            "gat1": (-1, tab["xa"], tab["xa"][NP:NP + EP, :], h1[0:EP, :]),
            "gat2": (1, h1, h1[0:EP, :], agg2),
            "sage1": (1, tab["xb"], None, agg[2]), "sage2": (1, tab["h2"], None, agg[3]),
            "tr0": (-1, tab["xc"], tab["xc"][NP:NP + EP, :], aggh[0]),
            "tr1": (1, tab["g1"], tab["g1"][NP:NP + EP, :], aggh[1]),
            "tr2": (-1, tab["g2"], tab["g2"][NP:NP + EP, :], aggh[2])}

        def weight_part(a):
            return L[1][5 + a][:, :].bitcast(BF16)[:, 0:T]

        def rowwise(g, i):
            return L[g][10][:, 8 * i:8 * i + 8]

        def there(c, way, count):
            return c if way > 0 else (count - 1) - c

        def tables_ready(eng, name):
            for g in range(LANES):
                eng.wait_ge(lane[g], ph[name].first[g])
                if st[name].first[g]:
                    eng.wait_ge(stored[g], st[name].first[g])

        def turned(a, way):
            return a if way > 0 else a[:, ::-1]

        def before(g, k):
            return (g - 1, k) if g else (LANES - 1, k - 1)

        def node_rows(a, c):
            return a[:, bass.ds(c, 1), :].rearrange("p a n -> p (a n)")

        tabn = {n: a[0:NP, :].rearrange("(c p j) d -> p c (j d)", p=P, j=8) for n, a in tab.items()}
        tabe = {n: a[NP:NP + EP, :].rearrange("(c p j) d -> p c (j d)", p=P, j=8) for n, a in tab.items()}
        xfull = t["x"][0:(NCH - 1) * CROWS, :].rearrange("(c p j) d -> p c (j d)", p=P, j=8)
        xlast = t["x"][(NCH - 1) * CROWS:N, :].rearrange("(p j) d -> p (j d)", j=8)
        ofull = out[0:(NCH - 1) * CROWS, :].rearrange("(c p j) d -> p c (j d)", p=P, j=8)
        olast = out[(NCH - 1) * CROWS:N, :].rearrange("(p j) d -> p (j d)", j=8)

        def e8(a):
            return a.rearrange("(c p j) d -> p c (j d)", p=P, j=8)

        def e4(a):
            return a.rearrange("(c p j) d -> p c j d", p=P, j=4)

        def halves(a):
            return a.rearrange("(c p h j) d -> p c h (j d)", p=P, h=2, j=4)

        block = ctx.enter_context(nc.Block())

        @block.sync
        def _(sp):
            for i in range(3):
                sp.dma_start(L[0][i][:, 0:T].bitcast(I32), t["edge_dst"][:, i, :]).then_inc(s_in, 16)
            sp.dma_start(recg[:, :, :], t["edge_rec"]).then_inc(s_in, 16)
            sp.dma_start(big[:, :], t["packed"]).then_inc(s_weights, 16)
            sp.dma_start(cw[:, :, :], t["relw"]).then_inc(s_weights, 16)
            sp.wait_ge(s_const, CONSTS)
            sp.dma_start(ptr[0:NP, :].rearrange("(p t) d -> p (t d)", p=P),
                         recm[:, :, :].rearrange("p t k -> p (t k)")).then_inc(s_ptr0, 16)
            sp.dma_start(h1[EP:EP + 1, :], zrow[:, :]).then_inc(s_mid, 16)
            sp.dma_start(dsts[0, :].rearrange("(p t) -> p t", t=T),
                         t["edge_dst"][:, 0, :]).then_inc(s_mid, 16)
            sp.wait_ge(s_set, SQ["setup"])
            for i in range(3):
                sp.dma_start(rows[i, :].rearrange("(p t) -> p t", t=T), L[1][3 + i][:, 0:T]).then_inc(s_mid, 16)
            sp.dma_start(dsts[1, :].rearrange("(p t) -> p t", t=T), idh[:, :]).then_inc(s_mid, 16)
            for h, r in enumerate((0, 1, 4, 5)):
                sp.dma_start(flag[r, :].rearrange("(p t) -> p t", t=T), fbf[:, h, :]).then_inc(s_mid, 16)
            sp.wait_ge(s_mid, 16 * MIDS)
            r4 = rows.rearrange("r (c p j) -> r p c j", p=P, j=4)
            r8 = rows.rearrange("r (c p j) -> r p c j", p=P, j=8)
            d4 = dsts.rearrange("r (c p j) -> r p c j", p=P, j=4)
            d8 = dsts.rearrange("r (c p j) -> r p c j", p=P, j=8)
            for to, of in ((first4, r4[1]), (rinv, r4[2]), (idd, d4[1])):
                sp.dma_start(to[:, :].rearrange("p (c j) -> p c j", j=4), of).then_inc(s_mask, 16)
            for to, of in ((last8, r8[0]), (first8, r8[1]), (dst8, d8[0])):
                sp.dma_start(to[:, :].rearrange("p (c j) -> p c j", j=8), of).then_inc(s_mask, 16)

            def pass_io(name, last_read, load, *stores):
                pz = ph[name]

                def work(at):
                    for g, k, c in at(last_read):
                        if type(c) is not int or c + LANES < pz.chunks:
                            sp.wait_ge(lane[g], pz.at(g, k, last_read))
                            load(g, c + LANES)
                    for step, store in stores:
                        for g, k, c in at(step):
                            sp.wait_ge(lane[g], pz.at(g, k, step))
                            store(g, c)
                for g in range(LANES):
                    load(g, g)
                in_turns(sp, pz, work, peel_last=True)

            def sweep_io(name, last_use, last_step):
                way, _, hd, to = INFO[name]
                pz = ph[name]
                width = to.shape[1]
                tables_ready(sp, name)

                def load(g, c, r):
                    e = there(c, way, SWEEPS)
                    if way < 0:
                        sp.nop(nofuse=True)
                    sp.dma_start(ft[g][:, :], flag[:, bass.ds(e * W, W)]).then_inc(loaded[g], 16)
                    if name in ("rg1", "rg2"):
                        sp.dma_start(hots[g][:, :], hot[:, bass.ds(e * W, W)]).then_inc(loaded[g], 16)
                    if name in ("gat1", "gat2"):
                        sp.dma_start(wr_[g][:, :], wrow[:, bass.ds(e * W, W)]).then_inc(loaded[g], 16)
                    if hd is not None:
                        into = hring[g][:, :, :] if name == "gat2" else ring[r][:, :, D:P]
                        sp.dma_start(into, e4(hd)[:, bass.ds(e, 1), :, :].rearrange("p a j d -> p (a j) d")
                                     ).then_inc(loaded[g], 16)

                def work(at):
                    for g, k, c, r, use in at(last_use):
                        if type(c) is not int or c + LANES < SWEEPS:
                            sp.wait_ge(lane[g], pz.at(g, k, last_use))
                            if way < 0:
                                sp.nop(nofuse=True)
                            load(g, c + LANES, (r + LANES) % SLOTS)
                    for g, k, c, r, use in at(last_step):
                        if name == "rg1":
                            sp.wait_ge(gathered[r], ga[name].after(r, use))
                            sp.dma_start(e4(xdst)[:, bass.ds(c, 1), :, :].rearrange("p a j d -> p (a j) d"),
                                         ring[r][:, :, D:P]).then_inc(saved[r], 16)
                        sp.wait_ge(lane[g], pz.at(g, k, last_step))
                        if way < 0:
                            sp.nop(nofuse=True)
                        e = there(c, way, SWEEPS)
                        sp.dma_start(e4(to)[:, bass.ds(e, 1), :, :].rearrange("p a j d -> p (a j) d"),
                                     orow[g][:, :, 0:width]).then_inc(stored[g], 16)
                for g in range(LANES):
                    load(g, g, g)
                in_turns(sp, pz, work, peel_last=True)

            def load(g, c):
                if type(c) is int and c == NCH - 1:
                    sp.dma_start(tl(g, 0)[0:LASTP, :], xlast).then_inc(loaded[g], 16)
                else:
                    sp.dma_start(tl(g, 0), node_rows(xfull, c)).then_inc(loaded[g], 16)

            def row_store(n, tile):
                return lambda g, c: sp.dma_start(node_rows(tabn[n], c), tl(g, tile)).then_inc(stored[g], 16)
            pass_io("nodeA", "x_t", load, ("x1_o", row_store("x1", 7)), ("xa_o", row_store("xa", 8)),
                    ("xb_o", row_store("xb", 9)), ("h2_o", row_store("h2", 7)), ("xc_o", row_store("xc", 8)),
                    ("g1_o", row_store("g1", 9)))

            sp.wait_ge(s_rec, 16)
            tables_ready(sp, "rg1")
            sp.dma_start(recm[:, :, :], rec.rearrange("(p t) k -> p t k", t=T)).then_inc(s_keys, 16)
            sp.wait_ge(s_set, SQ["keys"])
            sp.dma_start(keys[0, 1:EP + 1].rearrange("(p t) -> p t", t=T), L[0][0][:, 0:T]).then_inc(s_keys, 16)
            sp.dma_start(keys[:, 0:1], L[0][1][0:1, 0:1]).then_inc(s_keys, 16)
            sp.dma_start(keys[:, EP + 1:EP + 2], L[0][1][0:1, 0:1]).then_inc(s_keys, 16)
            sp.wait_ge(s_keys, 4 * 16)
            sp.dma_start(L[0][2][:, 0:T], keys[0, 0:EP].rearrange("(p t) -> p t", t=T)).then_inc(s_keys, 16)
            sp.dma_start(L[0][3][:, 0:T], keys[0, 2:EP + 2].rearrange("(p t) -> p t", t=T)).then_inc(s_keys, 16)
            sp.wait_ge(s_set, SQ["flags"])
            for h, r in enumerate((2, 3)):
                sp.dma_start(flag[r, :].rearrange("(p t) -> p t", t=T), fbf[:, h, :]).then_inc(s_mid, 16)
            for q in range(3):
                for r in range(R):
                    sp.dma_start(hot[q * R + r, :].rearrange("(p t) -> p t", t=T), hotm(r)).then_inc(s_mid, 16)
            for i in range(9):
                sp.dma_start(wrow[i, :].rearrange("(p t) -> p t", t=T), weight_part(i % 3)).then_inc(s_mid, 16)
            sp.dma_start(recm[:, :, :].rearrange("p t k -> p (t k)").rearrange("p (c k) -> p c k", c=NCH),
                         ptr[0:NP, :].rearrange("(c p j) k -> p c (j k)", p=P, j=8)).then_inc(s_ptr1, 16)
            sp.wait_ge(s_mid, 16 * MIDT)

            def edge_pass(name, loads, to):
                tables_ready(sp, name)

                def load(g, c):
                    for i, of in loads:
                        sp.dma_start(tl(g, i), node_rows(of, c)).then_inc(loaded[g], 16)

                def store(g, c):
                    sp.dma_start(node_rows(to, c), tl(g, 7)).then_inc(stored[g], 16)
                pass_io(name, last_read[name], load, *([("o", store)] if to is not None else []))

            def out_rows(g, c):
                if type(c) is int and c == NCH - 1:
                    sp.dma_start(olast, tl(g, 7)[0:LASTP, :]).then_inc(stored[g], 16)
                else:
                    sp.dma_start(node_rows(ofull, c), tl(g, 7)).then_inc(stored[g], 16)

            def wide(a, w):
                return a.rearrange("(c p h j) d -> h p c (j d)", p=P, h=2, j=4)[w]

            last_read = {"e01": "b_t", "e02": "c_t", "e12": "c_t", "e21": "b_t", "e22": "c_t", "e31": "b_t",
                         "e32": "b_t", "n2": "a_t", "n3": "c_t", "e33": "c_t", "nS": "st_p"}
            sweep_io("rg1", "keep", "agg_o")
            edge_pass("e01", [(0, e8(agg[0])), (9, e8(xdst))], tabe["x1"])
            sweep_io("rg2", "keep", "agg_o")
            edge_pass("e02", [(0, e8(agg[1])), (9, tabe["x1"]), (8, e8(xdst))], tabe["xa"])
            sweep_io("gat1", "reset", "rows")
            sweep_io("gat2", "reset", "rows")
            edge_pass("e12", [(0, wide(agg2, 0)), (8, wide(agg2, 1)), (9, tabe["xa"])], tabe["xb"])
            sweep_io("sage1", "keep", "agg_o")
            edge_pass("e21", [(0, e8(agg[2])), (9, tabe["xb"])], tabe["h2"])
            sweep_io("sage2", "keep", "agg_o")
            edge_pass("e22", [(0, e8(agg[3])), (9, tabe["h2"]), (8, tabe["xb"])], tabe["xc"])
            sweep_io("tr0", "reset", "hrows")
            edge_pass("e31", [(0, wide(aggh[0], 0)), (8, wide(aggh[0], 1))], tabe["g1"])
            edge_pass("nS", [(7, tabn["g1"])], None)
            sweep_io("tr1", "reset", "hrows")
            edge_pass("e32", [(0, wide(aggh[1], 0)), (8, wide(aggh[1], 1))], tabe["g2"])
            edge_pass("n2", [(0, tabn["g1"])], tabn["g2"])
            sweep_io("tr2", "reset", "hrows")
            tables_ready(sp, "n3")

            def load(g, c):
                sp.dma_start(tl(g, 0), node_rows(tabn["g2"], c)).then_inc(loaded[g], 16)
                sp.dma_start(tl(g, 8), node_rows(tabn["xc"], c)).then_inc(loaded[g], 16)
            pass_io("n3", "c_t", load, ("o", out_rows))
            tables_ready(sp, "e33")

            def load(g, c):
                sp.dma_start(tl(g, 0), node_rows(wide(aggh[2], 0), c)).then_inc(loaded[g], 16)
                sp.dma_start(tl(g, 8), node_rows(wide(aggh[2], 1), c)).then_inc(loaded[g], 16)
                sp.dma_start(tl(g, 9).rearrange("p (j d) -> p j d", d=D),
                             aggh[0].rearrange("(c p j) d -> p c j d", p=P, j=8)[:, bass.ds(c, 1), :, D:P]
                             .rearrange("p a j d -> p (a j) d")).then_inc(loaded[g], 16)
            pass_io("e33", "c_t", load)
            for g in range(LANES):
                sp.wait_ge(stored[g], b2[g])
                sp.wait_ge(put[g], scattered.last[g])

        @block.gpsimd
        def _(gp):
            n = [0]

            def after(ins):
                n[0] += 1
                ins.then_inc(s_const, 1)
                gp.wait_ge(s_const, n[0])

            def eye(m, pattern, base, fill=1.0, cm=1):
                after(gp.affine_select(out=m, in_=m, compare_op=ALU.not_equal, fill=fill, base=base,
                                       pattern=pattern, channel_multiplier=cm))

            def keep_from(m, pattern, base, cm=1):
                after(gp.affine_select(out=m, in_=m, compare_op=ALU.is_ge, fill=0.0, base=base, pattern=pattern,
                                       channel_multiplier=cm))
            for m in (ident, fold2, sums, sel, selbig, zrow, spread):
                after(gp.memset(m[:], 0.0))
            for m in (mask16, mask64, mask3, mask9, real84):
                after(gp.memset(m[:], 1.0))
            after(gp.memset(scale1[:, :], float(D) ** -0.5))
            after(gp.memset(eps[:, :], EPS))
            eye(ident[:, :], [[-1, P]], 0)
            for h in range(2):
                eye(fold2[:, :], [[-1, D]], -D * h)
                eye(sums[:, h, :].rearrange("p (a f) -> p a f", a=2), [[0, 2], [-1, D]], -D * h)
            for q in range(4):
                for i in range(2):
                    eye(spread[:, q, i * D:(i + 1) * D].rearrange("p (b o) -> p b o", o=8), [[-8, 8], [0, 8]],
                        -(2 * q + i))
            eye(sel[:, :, :], [[-1, 6], [0, P]], 0)
            eye(selbig[:, :, :], [[-1, 6], [0, P]], 0, fill=-BIG)
            for m, w in ((mask16, 16), (mask64, D)):
                view = m[:, :].rearrange("p (h c) -> p h c", c=w)
                keep_from(view, [[-w, P // w], [0, w]], 0)
                keep_from(view, [[w, P // w], [0, w]], w - 1, cm=-1)
            keep_from(mask3[:, :], [[-R, 3]], 0)
            keep_from(mask3[:, :], [[R, 3]], R - 1, cm=-1)
            keep_from(mask9[:, :], [[-3, 3]], 0)
            keep_from(mask9[:, :], [[3, 3]], 2, cm=-1)
            keep_from(real84[:, :], [[0, 1]], LASTP - 1, cm=-1)
            after(gp.iota(iota_e[:, :], [[1, T]], base=0, channel_multiplier=T))
            after(gp.iota(recm[:, :, :].rearrange("p t (a b) -> p (t a) b", b=2), [[1, 2 * T], [0, 2]], base=0,
                          channel_multiplier=2 * T))
            assert n[0] == CONSTS
            for g in range(LANES):
                gp.sem_inc(lane[g], START)

            H = GB // 2

            def setup_loop(number, copies, move):
                def turn(i, peeled):
                    for h in range(2):
                        if not peeled:
                            gp.wait_ge(s_sc[h], (i + number * (T // GB)) * (16 * H))
                        copies(i * GB + h * H, h)
                        gp.drain().then_inc(s_idx, 1)
                        gp.wait_ge(s_idx, i * 2 + (h + 1 + 2 * number * (T // GB)))
                        gp.nop(nofuse=True)
                        for q in range(H):
                            move(h, q).then_inc(s_sc[h], 16)
                turn(0, number == 0)
                with gp.Fori(1, T // GB, 1) as i:
                    turn(i, False)
                for h in range(2):
                    gp.wait_ge(s_sc[h], 16 * H * (number + 1) * (T // GB))

            def cols(a, c0, n):
                return a[:, bass.ds(c0, n)]

            gp.wait_ge(s_set, SQ["setup"])
            gp.wait_ge(s_ptr0, 16)

            def copies(c0, h):
                gp.tensor_copy(sidx[:, h, :], cols(pidx, c0, H))
                gp.tensor_copy(srec[:, h, :, 0:2], prec[:, bass.ds(c0, H), :])
            setup_loop(0, copies, lambda h, q: gp.indirect_dma_start(
                ptr, bass.IndirectOffsetOnAxis(sidx[:, h, q:q + 1], 0), srec[:, h, q, 0:2], None))

            def copies(c0, h):
                gp.tensor_copy(sidx[:, h, :], cols(pos, c0, H))
                gp.tensor_copy(srec[:, h, :, :], recg[:, bass.ds(c0, H), :])
            setup_loop(1, copies, lambda h, q: gp.indirect_dma_start(
                rec, bass.IndirectOffsetOnAxis(sidx[:, h, q:q + 1], 0), srec[:, h, q, :], None))
            gp.dma_start(recg[:, :, :].rearrange("p t k -> p (t k)").rearrange("p (c k) -> p c k", k=16),
                         rec.rearrange("(c p j) k -> p c (j k)", p=P, j=4)).then_inc(s_rec, 16)
            gp.wait_ge(s_rec, 16)

            def turn(i):
                for h in range(2):
                    gp.tensor_copy(sidx[:, h, :], recg[:, bass.ds(i * GB + h * H, H), 0:1].rearrange("p t k -> p (t k)"))
                    gp.drain().then_inc(s_idx, 1)
                    gp.wait_ge(s_idx, i * 2 + (h + 1 + 4 * (T // GB)))
                    gp.nop(nofuse=True)
                    for q in range(H):
                        gp.indirect_dma_start(srec[:, h, q, 0:2], None, ptr,
                                              bass.IndirectOffsetOnAxis(sidx[:, h, q:q + 1], 0)).then_inc(s_sc[h], 16)
                    gp.wait_ge(s_sc[h], (i + (1 + 2 * (T // GB))) * (16 * H))
                    gp.tensor_copy(spg[:, bass.ds(i * GB + h * H, H), :], srec[:, h, :, 0:2]).then_inc(s_spg, 1)
            with gp.Fori(0, T // GB, 1) as i:
                turn(i)

            tables = {"rg1": None, "rg2": spg[:, :, 0:1], "gat1": spg[:, :, 0:1], "gat2": None,
                      "sage1": spg[:, :, 0:1], "sage2": spg[:, :, 0:1], "tr0": spg[:, :, 0:1],
                      "tr1": spg[:, :, 1:2], "tr2": spg[:, :, 0:1]}
            used = [3 * 2 * (T // GB)]

            def sweep_gathers(name, last_read):
                way, table, _, _ = INFO[name]
                tables_ready(gp, name)

                def work(group, peeled):
                    for g, k, c, r, use in group:
                        e = there(c, way, SWEEPS)
                        if name == "rg1":
                            if not peeled:
                                gp.wait_ge(saved[r], use * 16)
                            gp.nop(nofuse=True)
                        gp.wait_ge(lane[g], ph[name].at(g, k - 2, last_read))
                        src = recg[:, bass.ds(e * 4, 4), 0:1] if name == "rg1" else \
                            idh[:, bass.ds(e * 4, 4)] if name == "gat2" else \
                            spg[:, bass.ds(e * 4, 4), 0:1] if name != "tr1" else spg[:, bass.ds(e * 4, 4), 1:2]
                        if name != "gat2":
                            src = src.rearrange("p t k -> p (t k)")
                        if name == "rg1":
                            gp.tensor_copy(idx[:, 1, 4 * r:4 * r + 4], idd[:, bass.ds(e * 4, 4)])
                        gp.tensor_copy(idx[:, 0, 4 * r:4 * r + 4], src).then_inc(s_idx, 1)
                        gp.wait_ge(s_idx, c + (used[0] + 1))
                        gp.nop(nofuse=True)
                        for j in range(4):
                            width = P if name == "gat2" else D
                            gp.indirect_dma_start(ring[r][:, j, 0:width], None, table, bass.IndirectOffsetOnAxis(
                                idx[:, 0, 4 * r + j:4 * r + j + 1], 0)).then_inc(gathered[r], 16)
                            if name == "rg1":
                                gp.indirect_dma_start(ring[r][:, j, D:P], None, table, bass.IndirectOffsetOnAxis(
                                    idx[:, 1, 4 * r + j:4 * r + j + 1], 0)).then_inc(gathered[r], 16)

                def each(group):
                    k = group[0][1]
                    work(group, type(k) is int and k < SLOTS // LANES)
                slots_in_order(gp, each, peel=name == "rg1")
                used[0] += SWEEPS

            gp.wait_ge(s_mask, 6 * 16)
            sweep_gathers("rg1", "x_t")
            gp.wait_ge(s_mid, 16 * MIDT)
            sweep_gathers("rg2", "x0_t")
            sweep_gathers("gat1", "src_t")
            sweep_gathers("gat2", "src_t")
            sweep_gathers("sage1", "src_t")
            sweep_gathers("sage2", "src_t")
            for name in ("tr0", "tr1", "tr2"):
                sweep_gathers(name, "src_t")

            gp.wait_ge(s_set, SQ["rows"])
            name = last_pass
            tables_ready(gp, name)

            def work(group):
                for g, k, c in group:
                    gp.wait_ge(lane[g], ph[name].at(g, k, "o"))
                    gp.tensor_copy(idx[:, 1, 8 * g:8 * g + 8], ido[:, bass.ds(c * 8, 8)]).then_inc(s_idx, 1)
                    gp.wait_ge(s_idx, c + (used[0] + 1))
                    gp.nop(nofuse=True)
                    for j in range(8):
                        gp.indirect_dma_start(out, bass.IndirectOffsetOnAxis(idx[:, 1, 8 * g + j:8 * g + j + 1], 0),
                                              tl(g, 7)[:, j * D:(j + 1) * D], None).then_inc(put[g], 16)
            in_order(gp, ECH, work)

        @block.tensor
        def _(pe):
            mm = nc.tensor.matmul
            I = ident[:, :]

            def turn_in(to, rows_):
                for i in range(4):
                    last = mm(to[:, i * P:(i + 1) * P], rows_[:, i * P:(i + 1) * P], I, start=(i == 0), stop=(i == 3),
                              is_transpose=True, skip_group_check=True)
                return last

            def product(to, terms):
                if to.shape[0] < P and terms[0][0].shape[0] < P:
                    pe.nop(nofuse=True)
                for i, (w, x) in enumerate(terms):
                    last = mm(to, w, x, start=(i == 0), stop=(i == len(terms) - 1))
                return last

            def variance(g, y):
                for i in range(4):
                    mm(bank[g][1][:, 2 * i:2 * i + 2], tl(g, 3)[:, i * P:(i + 1) * P], mean2[:, 0::D], start=True,
                       stop=True)
                return turn_in(bank[g][0], tl(g, y))

            def carries(a, scan_out):
                pe.wait_ge(s_set, SQ[a + "_last"])
                mm(bank[0][0][0:16, 0:P], L[3][0][:, 0:16], I, start=True, stop=True, is_transpose=True)
                mm(bank[0][1][0:16, 0:P], L[3][0][:, 16:32], I, start=True, stop=True,
                   is_transpose=True).then_inc(s_set, 1)
                pe.wait_ge(s_set, SQ[a + "_scan"])
                mm(bank[0][0][:, 0:16], scan_out, ident[0:16, 0:16], start=True, stop=True,
                   is_transpose=True).then_inc(s_set, 1)
            pe.wait_ge(s_const, CONSTS)
            carries("f", L[3][2][0:16, 0:P])
            carries("b", L[3][2][0:16, 1:P + 1])

            B0, B1 = bank[0][0], bank[0][1]
            col = lambda i: L[0][i][:, 0:1]

            def one(wait, to, terms):
                pe.wait_ge(s_set, SQ[wait])
                product(to[:, 0:1], terms).then_inc(s_set, 1)
            pe.wait_ge(s_set, SQ["att"])
            for i, n_ in enumerate(("bias2", "g_bc", "g_br", "bs2")):
                last = mm(B0[:, i:i + 1], center[:, :], v(n_), start=True, stop=True)
            last.then_inc(s_set, 1)
            one("bias", B0, [(bd["wc"], v("alone"))])
            one("sq0", B1, [(mean2[:, :], col(3))])
            one("ge0", B0, [(bd["wr"], col(1))])
            one("sq1", B1, [(mean2[:, :], col(3))])
            one("ge1", B0, [(center[:, :], col(1)), (center[:, :], col(2))])

            def nodes(at):
                pz = ph["nodeA"]

                def each(before_, make):
                    for g, k, c in at(pz.after(before_)):
                        pe.wait_ge(lane[g], pz.at(g, k, before_))
                        make(g).then_inc(lane[g], 1)

                for g, k, c in at("x_t"):
                    pe.wait_ge(lane[g], pz.begin(g, k))
                    pe.wait_ge(loaded[g], ld["nodeA"].after(g, k))
                    turn_in(bank[g][0], tl(g, 0)).then_inc(lane[g], 1)
                each("x", lambda g: product(bank[g][0][:, :], [(bd["root1"], tl(g, 1))]))
                each("x1", lambda g: turn_in(bank[g][1], tl(g, 2)))
                each("x1_o", lambda g: product(bank[g][0][:, :], [(bd["root2"], tl(g, 2)), (center[:, :], tl(g, 1))]))
                each("y0", lambda g: variance(g, 5))
                each("xa_o", lambda g: turn_in(bank[g][0], tl(g, 8)))
                each("n0", lambda g: product(bank[g][0][:, :], [(center[:, :], tl(g, 5))]))
                each("y1", lambda g: variance(g, 6))
                each("xb_o", lambda g: turn_in(bank[g][0], tl(g, 9)))
                each("n1", lambda g: product(bank[g][0][:, :], [(bd["wr1"], tl(g, 6))]))
                each("h2", lambda g: turn_in(bank[g][1], tl(g, 2)))
                each("h2_o", lambda g: product(bank[g][0][:, :], [(bd["wr2"], tl(g, 2))]))
                each("h3", lambda g: product(bank[g][0][:, :], [(center[:, :], tl(g, 1)), (center[:, :], tl(g, 6))]))
                each("y2", lambda g: variance(g, 5))
                each("xc_o", lambda g: turn_in(bank[g][0], tl(g, 8)))
                each("n2", lambda g: product(bank[g][0][:, :], [(bd["ws0"], tl(g, 5))]))
                each("g1", lambda g: turn_in(bank[g][1], tl(g, 2)))
            pe.wait_ge(s_set, SQ["alone"])
            pe.wait_ge(s_mid, 16 * MIDS)
            in_turns(pe, ph["nodeA"], nodes)

            def flags(to, r, g, table):
                return mm(to[:, :], table[:, r, :], ft[g][:, :], start=True, stop=True)

            def tiles(to, parts, make):
                if parts < P:
                    pe.nop(nofuse=True)
                for j in range(4):
                    last = mm(to[0:parts, j::4], make(j), I, start=(j == 0), stop=(j == 3), is_transpose=True,
                              skip_group_check=True)
                return last

            def rows_of(to, x, parts, first=0):
                if parts < P:
                    pe.nop(nofuse=True)
                for j in range(4):
                    last = mm(to[:, j * parts:(j + 1) * parts], x[:, j::4],
                              ident[first:first + parts, first:first + parts], start=(j == 0), stop=(j == 3),
                              is_transpose=True, skip_group_check=True)
                return last

            def rgcn(name):
                pz = ph[name]
                l = 0 if name == "rg1" else 1

                def work(at):
                    def each(before_, make):
                        for g, k, c, r, use in at(pz.after(before_)):
                            pe.wait_ge(lane[g], pz.at(g, k, before_))
                            make(g, r).then_inc(lane[g], 1)
                    for g, k, c, r, use in at("x_t" if l == 0 else "x0_t"):
                        pe.wait_ge(lane[g], pz.begin(g, k))
                        pe.wait_ge(gathered[r], ga[name].after(r, use))
                        pe.wait_ge(loaded[g], ld[name].after(g, k))
                        if l == 0:
                            tiles(bank[g][1], D, lambda j: ring[r][:, j, 0:D]).then_inc(lane[g], 1)
                        else:
                            tiles(bank[g][0][0:D, :], D, lambda j: ring[r][:, j, 0:D])
                            for j in range(4):
                                last = mm(bank[g][0][D:P, j::4], ring[r][:, j, 0:D], I, start=True, stop=True)
                            last.then_inc(lane[g], 1)
                    if l == 0:
                        for q in range(4):
                            each(f"x{q - 1}" if q else "x", lambda g, r: product(
                                bank[g][0][:, :], [(spread[:, q, :], tl(g, 4)[0:D, :])]))
                    each(f"x{3 if l == 0 else 0}", lambda g, r: relation(g, 0))
                    for q in range(1, 4):
                        each(f"c{q - 1}", lambda g, r: relation(g, q))
                    each("c3", lambda g, r: product(bank[g][1][0:D, :], [
                        (fold2[:, :] if l == 0 else basew[:, q, :], tl(g, q if l == 0 else q + 1)) for q in range(4)]))
                    each("msg", lambda g, r: flags(bank[g][0], 2, g, selbig))
                    each("gmax", lambda g, r: flags(bank[g][0], 3, g, sel))
                    each("gpick", lambda g, r: flags(bank[g][0], 0, g, sel))
                    each("agg", lambda g, r: rows_of(bank[g][1], tl(g, 8)[0:D, :], D))

                def relation(g, q):
                    return mm(bank[g][0][:, :], cwb[:, l, q, :], hots[g][:, :], start=True, stop=True)

                in_turns(pe, pz, work)

            def sage(name):
                pz = ph[name]

                def work(at):
                    def each(before_, make):
                        for g, k, c, r, use in at(pz.after(before_)):
                            pe.wait_ge(lane[g], pz.at(g, k, before_))
                            make(g, r).then_inc(lane[g], 1)
                    for g, k, c, r, use in at("src_t"):
                        pe.wait_ge(lane[g], pz.begin(g, k))
                        pe.wait_ge(gathered[r], ga[name].after(r, use))
                        pe.wait_ge(loaded[g], ld[name].after(g, k))
                        tiles(bank[g][0], D, lambda j: ring[r][:, j, 0:D]).then_inc(lane[g], 1)
                    each("src", lambda g, r: flags(bank[g][1], 0, g, sel))
                    each("agg", lambda g, r: rows_of(bank[g][0], tl(g, 8)[0:D, :], D))
                in_turns(pe, pz, work)

            def soft(name):
                pz = ph[name]
                way = INFO[name][0]
                keep, reset = (0, 1) if way > 0 else (4, 5)
                l = int(name[-1])

                def work(at):
                    def each(before_, make):
                        for g, k, c, r, use in at(pz.after(before_)):
                            pe.wait_ge(lane[g], pz.at(g, k, before_))
                            make(g, r).then_inc(lane[g], 1)
                    for g, k, c, r, use in at("src_t"):
                        pe.wait_ge(lane[g], pz.begin(g, k))
                        pe.wait_ge(gathered[r], ga[name].after(r, use))
                        pe.wait_ge(loaded[g], ld[name].after(g, k))
                        tiles(bank[g][0], P, lambda j: ring[r][:, j, :]).then_inc(lane[g], 1)
                    if name == "gat2":
                        each("src", lambda g, r: tiles(bank[g][1], P, lambda j: hring[g][:, j, :]))
                        each("dst_in", lambda g, r: flags(bank[g][0], keep, g, sel))
                        each("dst_b", lambda g, r: product(bank[g][0][:, :], [
                            (g2l, tl(g, 0)), (g2r, tl(g, 1)), (we[:, 1, :], wr_[g][:, :])]))
                    else:
                        each("dst_in", lambda g, r: flags(bank[g][1], keep, g, sel))
                    if name == "gat1":
                        each("dst", lambda g, r: product(bank[g][0][:, :], [
                            (gw, tl(g, 0)), (we[:, 0, :], wr_[g][:, :])]))
                    if name[:3] == "gat":
                        each("z", lambda g, r: product(bank[g][1][:, :], [
                            ((att1m if name == "gat1" else att2m)[:, :], tl(g, 3))]))
                    else:
                        each("dst_b", lambda g, r: product(bank[g][0][:, :], [(wvq[:, l, :], tl(g, 0))]))
                        each("q", lambda g, r: product(bank[g][1][:, :], [(wk[0:D, l, :], tl(g, 0)[0:D, :])]))
                        each("qk", lambda g, r: product(bank[g][1][:, :], [(scale1[D:P, :], tl(g, 6)[D:P, :])]))
                    each("s", lambda g, r: flags(bank[g][0], reset, g, selbig))
                    if name[:3] == "gat":
                        wl = g2l if name == "gat2" else gw[0:D, :]
                        each("ex", lambda g, r: product(bank[g][0][:, :], [
                            (wl, tl(g, 0) if name == "gat2" else tl(g, 0)[0:D, :])]))
                        each("den", lambda g, r: rows_of(bank[g][0], tl(g, 8), P))
                        each("num_t", lambda g, r: rows_of(bank[g][1], tl(g, 9), P))
                    else:
                        each("nd", lambda g, r: rows_of(bank[g][0], tl(g, 8), P))
                        each("nd_t", lambda g, r: rows_of(bank[g][1], tl(g, 0)[D:P, :], D, D))
                in_turns(pe, pz, work)

            def passes(name):
                pz = ph[name]

                def turn_wide(g, to, part_):
                    pe.nop(nofuse=True)
                    for h in range(2):
                        for i in range(4):
                            last = mm(to[h * D:(h + 1) * D, i * P:(i + 1) * P], wide_row(g, 2 * i + h, part_), I,
                                      start=(h == 1 or i == 0), stop=(h == 1 or i == 3), is_transpose=(h == 0),
                                      skip_group_check=True)
                    return last

                def wide_row(g, j, part_):
                    at_ = (j % 4) * P + part_ * D
                    return L[g][0 if j < 4 else 8][:, at_:at_ + D]
                C = center[:, :]
                parts = {"e31", "e32", "e33"}

                def work(at):
                    def each(before_, make):
                        for g, k, c in at(pz.after(before_)):
                            pe.wait_ge(lane[g], pz.at(g, k, before_))
                            make(g).then_inc(lane[g], 1)

                    for g, k, c in at("a_t"):
                        pe.wait_ge(lane[g], pz.begin(g, k) + (name == "e12"))
                        pe.wait_ge(loaded[g], ld[name].after(g, k))
                        (turn_wide(g, bank[g][0], 0) if name in parts
                         else turn_in(bank[g][0], tl(g, 5 if name == "e12" else 0))).then_inc(lane[g], 1)
                    if "b_t" in pz.steps:
                        each("a", lambda g: turn_wide(g, bank[g][1], 1) if name in parts
                             else turn_in(bank[g][1], tl(g, 9)))
                    if "lin_p" in pz.steps:
                        terms = {"e01": (I, bd["root1"]), "e21": (bd["wl1"], bd["wr1"]), "e22": (bd["wl2"], bd["wr2"]),
                                 "e31": (I, bd["ws0"]), "e32": (I, bd["ws1"]), "n2": (bd["ws1"],)}[name]
                        each("b" if "b" in pz.steps else "a", lambda g: product(
                            bank[g][0][:, :], [(w_, tl(g, 1 + i)) for i, w_ in enumerate(terms)]))
                    for i in range(3):
                        if f"y{i}" in pz.steps:
                            each(f"y{i}", lambda g: variance(g, 6))
                    if name == "e12":
                        each("a", lambda g: product(bank[g][0][:, :], [(bd["wc"], tl(g, 1))]))
                        each("o0", lambda g: turn_in(bank[g][0], tl(g, 5)))
                        each("ge0", lambda g: product(bank[g][0][:, :], [(bd["wr"], tl(g, 1))]))
                        each("o1", lambda g: turn_in(bank[g][0], tl(g, 5)))
                        each("ge1", lambda g: turn_in(bank[g][0], tl(g, 9)))
                        each("c", lambda g: product(bank[g][0][:, :], [(C, tl(g, 1)), (C, tl(g, 2)), (C, tl(g, 5))]))
                    elif "y0_p" in pz.steps:
                        each("lin" if "lin" in pz.steps else "b" if "b" in pz.steps else "a",
                             lambda g: turn_in(bank[g][0], tl(g, 9 if name == "e33" else 8)))
                        terms = {"e02": [(C, 1), (bd["root2"], 2), (C, 5)], "e22": [(C, 4), (C, 5)],
                                 "n3": [(bd["ws2"], 1), (C, 5)], "e33": [(C, 1), (bd["ws2"], 2), (C, 5)]}[name]
                        each("c", lambda g: product(bank[g][0][:, :], [(w_, tl(g, i)) for w_, i in terms]))
                    elif "lin" in pz.steps:
                        each("lin", lambda g: turn_in(bank[g][1], tl(g, 4)))
                    if "st_p" in pz.steps:
                        for g, k, c in at("st_p"):
                            pe.wait_ge(lane[g], pz.at(g, k, "q"))
                            m = {"e31": first8, "e32": last8}.get(name, alone8)
                            for h, i_ in ((0, 7), (1, 3)):
                                for i in range(4):
                                    last = mm(bank[g][1][:, 2 * h:2 * h + 2], tl(g, i_)[:, i * P:(i + 1) * P],
                                              m[:, bass.ds(c * 8 + 2 * i, 2)], start=(i == 0), stop=(i == 3))
                            last.then_inc(lane[g], 1)
                in_turns(pe, pz, work)

            def batchnorm(l):
                for g in range(LANES):
                    pe.wait_ge(lane[g], ph[("tr1", "tr2")[l]].first[g])
                for i in range(2):
                    for h in range(2):
                        last = mm(B0[:, i:i + 1], sums[:, h, :], stats[:, l, 2 * i + h:2 * i + h + 1],
                                  start=(h == 0), stop=(h == 1))
                last.then_inc(s_set, 1)
                pe.wait_ge(s_set, SQ[f"bn{l}_done"])
            pe.wait_ge(s_mid, 16 * MIDT)
            pe.wait_ge(s_mask, 6 * 16)
            pe.wait_ge(s_set, SQ["rows"])
            rgcn("rg1")
            passes("e01")
            rgcn("rg2")
            passes("e02")
            soft("gat1")
            soft("gat2")
            passes("e12")
            sage("sage1")
            passes("e21")
            sage("sage2")
            passes("e22")
            soft("tr0")
            passes("e31")
            passes("nS")
            batchnorm(0)
            soft("tr1")
            passes("e32")
            passes("n2")
            batchnorm(1)
            soft("tr2")
            passes("n3")
            passes("e33")

        def y_bias(name, i):
            return {("nodeA", 0): "bias2c", ("nodeA", 1): "alone", ("e02", 0): "bias2c", ("e12", 0): "g_bcc",
                    ("e12", 1): "g_brc", ("n3", 0): "bs2c", ("e33", 0): "bs2c"}.get((name, i))

        @block.scalar
        def _(act):
            f = nc.scalar.activation

            def biased(out_, in_, func, bias=None, scale=1.0):
                if bias is None:
                    return f(out_, in_, func, scale=scale)
                return f(out_, in_, func, bias=v(bias) if type(bias) is str else bias, scale=scale)

            def centered(name, i, g, to):
                b_ = y_bias(name, i)
                biased(tl(g, to), bank[g][0][:, :], ACT.Identity if b_ else ACT.Copy, b_)
                return biased(tl(g, 3), bank[g][0][:, :], ACT.Square, b_)

            B0, B1 = bank[0][0], bank[0][1]

            def col(i):
                return L[0][i][:, 0:1]

            def one(wait, out_, in_, func, bias=None, scale=1.0):
                act.wait_ge(s_set, SQ[wait])
                biased(out_, in_, func, bias, scale).then_inc(s_set, 1)
            one("y0_p", col(3), B0[:, 0:1], ACT.Square, "g_bcc")
            one("var0_p", col(4), B1[:, 0:1], ACT.Sqrt, eps[:, :])
            one("n0", col(1), col(6), ACT.Gelu, "g_lnb", v("g_lng"))
            one("y1_p", col(3), B0[:, 0:1], ACT.Square, "g_brc")
            one("var1_p", col(4), B1[:, 0:1], ACT.Sqrt, eps[:, :])
            one("n1", col(2), col(6), ACT.Gelu, "g_lnrb", v("g_lnrg"))

            def nodes(at):
                pz = ph["nodeA"]

                def each(before_, make):
                    for g, k, c in at(pz.after(before_)):
                        act.wait_ge(lane[g], pz.at(g, k, before_))
                        make(g).then_inc(lane[g], 1)

                def norm(i, to):
                    each(f"y{i}_p", lambda g: centered("nodeA", i, g, to))
                    each(f"var{i}_p", lambda g: biased(rowwise(g, 0), bank[g][1][:, 0:8], ACT.Sqrt, eps[:, :]))
                each("x1_p", lambda g: biased(tl(g, 2), bank[g][0][:, :], ACT.Relu, "bias1"))
                norm(0, 5)
                norm(1, 6)
                each("n1_t", lambda g: biased(tl(g, 6), bank[g][0][:, :], ACT.Copy))
                each("h2_p", lambda g: biased(tl(g, 2), bank[g][0][:, :], ACT.Relu, "s_b1"))
                each("h3_p", lambda g: biased(tl(g, 1), bank[g][0][:, :], ACT.Relu, "s_b2"))
                norm(2, 5)
                each("g1_p", lambda g: biased(tl(g, 2), bank[g][0][:, :], ACT.Identity, "bs0"))
            in_turns(act, ph["nodeA"], nodes)

            def rgcn(name):
                pz = ph[name]

                def work(at):
                    def each(before_, make):
                        for g, k, c, r, use in at(pz.after(before_)):
                            act.wait_ge(lane[g], pz.at(g, k, before_))
                            make(g).then_inc(lane[g], 1)
                    if name == "rg1":
                        each("x_t", lambda g: biased(tl(g, 4)[0:D, :], bank[g][1][0:D, :], ACT.Copy))
                    for q in range(4 if name == "rg1" else 1):
                        each(f"x{q}_t", lambda g: biased(tl(g, q), bank[g][0][:, :], ACT.Copy))
                    each("msg_p", lambda g: biased(tl(g, 5)[0:D, :], bank[g][1][0:D, :], ACT.Copy))
                    for g, k, c, r, use in at("agg_o"):
                        act.wait_ge(stored[g], st[name].before(g, k))
                        act.wait_ge(lane[g], pz.at(g, k, "agg_t"))
                        biased(orow[g][:, :, 0:D], bank[g][1][:, 0:4 * D].rearrange("p (j d) -> p j d", d=D),
                               ACT.Copy).then_inc(lane[g], 1)
                in_turns(act, pz, work)

            def sage(name):
                pz = ph[name]

                def work(at):
                    for g, k, c, r, use in at("src"):
                        act.wait_ge(lane[g], ph[name].at(g, k, "src_t"))
                        biased(tl(g, 5)[0:D, :], bank[g][0][0:D, :], ACT.Copy).then_inc(lane[g], 1)
                in_turns(act, pz, work)

            def soft(name):
                pz = ph[name]
                way = INFO[name][0]
                l = int(name[-1])
                bn = dict(bias=f"bn_b{l - 1}") if name[:2] == "tr" and l else None

                def work(at):
                    def each(before_, make):
                        for g, k, c, r, use in at(pz.after(before_)):
                            act.wait_ge(lane[g], pz.at(g, k, before_))
                            make(g).then_inc(lane[g], 1)

                    def lower(a):
                        return a[0:D, :]

                    def upper(a):
                        return a[D:P, :]
                    if name == "gat2":
                        each("src_t", lambda g: biased(tl(g, 0), bank[g][0][:, :], ACT.Relu, "g_b1"))
                        each("dst_t", lambda g: biased(tl(g, 1), bank[g][1][:, :], ACT.Copy))
                        each("dst", lambda g: biased(tl(g, 1), tl(g, 10), ACT.Relu, "g_b1"))
                    elif name[:2] == "tr" and l:
                        vb, vs = v(f"bn_b{l - 1}"), v(f"bn_s{l - 1}")
                        each("src_t", lambda g: f(lower(tl(g, 0)), lower(bank[g][0]), ACT.Relu, bias=vb[0:D, :],
                                                  scale=vs[0:D, :]))
                        each("src", lambda g: biased(upper(tl(g, 1)), upper(bank[g][0]), ACT.Copy))
                        each("dst", lambda g: f(upper(tl(g, 0)), upper(tl(g, 10)), ACT.Relu, bias=vb[D:P, :],
                                                scale=vs[D:P, :]))
                    else:
                        each("src_t", lambda g: biased(lower(tl(g, 0)), lower(bank[g][0]), ACT.Copy))
                        each("src", lambda g: biased(upper(tl(g, 1)), upper(bank[g][0]), ACT.Copy))
                        if name == "tr0":
                            each("dst", lambda g: biased(upper(tl(g, 0)), upper(tl(g, 10)), ACT.Copy))
                    if name[:3] == "gat":
                        each("z_p", lambda g: biased(tl(g, 2), bank[g][0][:, :], ACT.Copy, scale=0.2))
                    else:
                        each("q_p", lambda g: biased(tl(g, 3), bank[g][0][:, :], ACT.Identity, f"bvq{l}"))
                    for g, k, c, r, use in at("s"):
                        pg, pk = before(g, k)
                        act.wait_ge(lane[g], pz.at(g, k, "s_p"))
                        f(L[g][4][:, 1:W + 1], bank[g][1][:, :], ACT.Copy)
                        act.wait_ge(lane[pg], pz.at(pg, pk, "s"))
                        of, to_ = (W, 0) if way > 0 else (1, W + 1)
                        f(L[g][4][:, to_:to_ + 1], L[pg][4][:, of:of + 1], ACT.Copy).then_inc(lane[g], 1)
                    for g, k, c, r, use in at("ex"):
                        act.wait_ge(lane[g], pz.at(g, k, "hi"))
                        f(tl(g, 7), tl(g, 7), ACT.Exp)
                        f(tl(g, 6), tl(g, 6), ACT.Exp).then_inc(lane[g], 1)
                    if name[:2] == "tr":
                        each("rows", lambda g: biased(orow[g][:, :, D:P],
                                                      bank[g][1][:, 0:4 * D].rearrange("p (j d) -> p j d", d=D),
                                                      ACT.Copy))
                in_turns(act, pz, work)

            def passes(name):
                pz = ph[name]

                def work(at):
                    def each(before_, make):
                        for g, k, c in at(pz.after(before_)):
                            act.wait_ge(lane[g], pz.at(g, k, before_))
                            make(g).then_inc(lane[g], 1)

                    def norm(i):
                        each(f"y{i}_p", lambda g: centered(name, i, g, 6))
                        each(f"var{i}_p", lambda g: biased(rowwise(g, 0), bank[g][1][:, 0:8], ACT.Sqrt, eps[:, :]))
                    if name == "e12":
                        each("a_t", lambda g: biased(tl(g, 1), bank[g][0][:, :], ACT.Relu, "g_b2", 0.5))
                    elif name in ("n2", "n3"):
                        l = int(name[1]) - 2
                        each("a_t", lambda g: biased(tl(g, 1), bank[g][0][:, :], ACT.Relu, f"bn_b{l}", v(f"bn_s{l}")))
                    elif name != "nS":
                        each("a_t", lambda g: biased(tl(g, 1), bank[g][0][:, :], ACT.Copy))
                    if "lin" in pz.steps:
                        func, bias = {"e01": (ACT.Relu, "bias1"), "e21": (ACT.Relu, "s_b1"), "e22": (ACT.Relu, "s_b2"),
                                      "e31": (ACT.Identity, "bs0"), "e32": (ACT.Identity, "bs1"),
                                      "n2": (ACT.Identity, "bs1")}[name]
                        each("lin_p", lambda g: biased(tl(g, 4), bank[g][0][:, :], func, bias))
                    if name == "e12":
                        norm(0)
                        each("n0_t", lambda g: biased(tl(g, 1), bank[g][0][:, :], ACT.Gelu, "g_lnb", v("g_lng")))
                        norm(1)
                        each("n1_t", lambda g: biased(tl(g, 2), bank[g][0][:, :], ACT.Gelu, "g_lnrb", v("g_lnrg")))
                        each("c_t", lambda g: biased(tl(g, 5), bank[g][0][:, :], ACT.Copy))
                        norm(2)
                    elif "y0_p" in pz.steps:
                        each("c_t", lambda g: biased(tl(g, 5), bank[g][0][:, :], ACT.Copy))
                        norm(0)
                    if name == "nS":
                        for g, k, c in at("q"):
                            act.wait_ge(lane[g], pz.begin(g, k))
                            act.wait_ge(loaded[g], ld[name].after(g, k))
                            biased(tl(g, 3), tl(g, 7), ACT.Square).then_inc(lane[g], 1)
                    elif "q" in pz.steps:
                        each("o", lambda g: biased(tl(g, 3), tl(g, 7), ACT.Square))
                in_turns(act, pz, work)

            def batchnorm(l):
                one(f"bn{l}_var", col(4), v("var"), ACT.Sqrt, eps[:, :])
                act.wait_ge(s_set, SQ[f"bn{l}_done"])
            rgcn("rg1")
            passes("e01")
            rgcn("rg2")
            passes("e02")
            soft("gat1")
            soft("gat2")
            passes("e12")
            sage("sage1")
            passes("e21")
            sage("sage2")
            passes("e22")
            soft("tr0")
            passes("e31")
            passes("nS")
            batchnorm(0)
            soft("tr1")
            passes("e32")
            passes("n2")
            batchnorm(1)
            soft("tr2")
            passes("n3")
            passes("e33")

        @block.vector
        def _(dve):
            V = nc.vector

            def chained(ins):
                links[0] += 1
                ins.then_inc(s_link, 1)
                dve.wait_ge(s_link, links[0])

            for g in range(LANES):
                for i in range(NT):
                    if g or i > 2:
                        V.memset(L[g][i][:, :], 0.0)
                V.memset(orow[g][:, :, :], 0.0)
            chained(V.memset(stats[:, :, :], 0.0))

            def S(i):
                return L[1][i][:, 0:T]

            def S0(i):
                return L[0][i][:, 0:T]
            DST, TYP, ENDS, FIRST, RINV, KEEP, KEEPB, ONE, CNT, ACC = (S(i) for i in (0, 1, 3, 4, 5, 6, 7, 8, 9, 10))
            PICK, RUN1, EI, ACCB, PREV, NEXT = (S0(i) for i in (5, 6, 7, 8, 3, 4))
            lastk, carry, cin = L[3][0], L[3][2], L[3][3]
            dve.wait_ge(s_in, 4 * 16)
            V.tensor_copy(DST, L[0][0][:, 0:T].bitcast(I32))
            V.tensor_copy(PREV, L[0][1][:, 0:T].bitcast(I32))
            V.tensor_copy(NEXT, L[0][2][:, 0:T].bitcast(I32))
            V.tensor_copy(TYP, recg[:, :, 1:2].rearrange("p t k -> p (t k)"))
            dve.wait_ge(s_const, CONSTS)
            chained(V.tensor_copy(EI, iota_e[:, :]))
            chained(V.tensor_tensor(FIRST, DST, PREV, ALU.not_equal))
            chained(V.tensor_tensor(ENDS, DST, NEXT, ALU.not_equal))
            V.tensor_scalar(KEEP, FIRST, -1.0, 1.0, ALU.mult, ALU.add)
            chained(V.tensor_scalar(KEEPB, ENDS, -1.0, 1.0, ALU.mult, ALU.add))

            def counts(a, keep, way, cmp, acc):
                def rev(x):
                    return turned(x, way)

                def one_(r):
                    if r < R:
                        chained(V.tensor_scalar(ONE, TYP, float(r), None, ALU.is_equal))
                    else:
                        chained(V.tensor_tensor(ONE, FIRST, EI, ALU.mult))

                kinds = R + 1 if way > 0 else R
                edge = T - 1 if way > 0 else 0
                chained(V.memset(lastk[:, 0:16], 0.0))
                for r in range(kinds):
                    one_(r)
                    chained(V.tensor_tensor_scan(rev(CNT), rev(keep), rev(ONE), 0.0, ALU.mult, ALU.add))
                    chained(V.tensor_copy(lastk[:, r:r + 1], CNT[:, edge:edge + 1]))
                chained(V.tensor_reduce(PICK[:, 0:1], keep, axis=AX.X, op=ALU.min))
                V.tensor_copy(lastk[:, 16:32], PICK[:, 0:1].to_broadcast([P, 16])).then_inc(s_set, 1)
                dve.wait_ge(s_set, SQ[a + "_turn"])
                chained(V.tensor_copy(carry[0:16, 256:256 + P], bank[0][1][0:16, 0:P]))
                chained(V.memset(carry[0:16, 0:P + 1], 0.0))
                into = carry[0:16, 1:P + 1] if way > 0 else carry[0:16, 0:P]
                V.tensor_tensor_scan(rev(into), rev(carry[0:16, 256:256 + P]), rev(bank[0][0][0:16, 0:P]), 0.0,
                                     ALU.mult, ALU.add).then_inc(s_set, 1)
                dve.wait_ge(s_set, SQ[a + "_back"])
                chained(V.tensor_copy(cin[:, 0:16], bank[0][0][:, 0:16]))
                chained(V.memset(acc, 0.0))
                for r in range(kinds):
                    one_(r)
                    to = CNT if r < R else RUN1
                    chained(V.tensor_tensor_scan(rev(to), rev(keep), rev(ONE), cin[:, r:r + 1], ALU.mult, ALU.add))
                    if r < R:
                        chained(V.scalar_tensor_tensor(PICK, TYP, float(r), CNT, cmp, ALU.mult))
                        chained(V.tensor_tensor(acc, acc, PICK, ALU.add))
            counts("f", KEEP, 1, ALU.is_lt, ACC)
            counts("b", KEEPB, -1, ALU.is_gt, ACCB)
            chained(V.tensor_tensor(ACC, EI, ACC, ALU.subtract))
            chained(V.tensor_tensor(pos[:, :], ACC, ACCB, ALU.add))
            chained(V.scalar_tensor_tensor(PICK, EI, 1.0, RUN1, ALU.add, ALU.subtract))
            chained(V.reciprocal(RINV, PICK))
            V.tensor_scalar(prec[:, :, 0:1].rearrange("p t k -> p (t k)"), EI, float(NP), None, ALU.add)
            V.tensor_scalar(prec[:, :, 1:2].rearrange("p t k -> p (t k)"), RUN1, float(NP), None, ALU.add)
            chained(V.tensor_scalar(ACCB, EI, float(NP), None, ALU.add))
            chained(V.tensor_tensor(PICK, DST, ACCB, ALU.subtract))
            chained(V.tensor_tensor(PICK, PICK, ENDS, ALU.mult))
            V.tensor_tensor(pidx[:, :], PICK, ACCB, ALU.add)
            V.tensor_scalar(idh[:, :], DST, float(N - 1), None, ALU.min)
            V.tensor_copy(fbf[:, 0, :], KEEP)
            V.tensor_copy(fbf[:, 1, :], FIRST)
            V.tensor_copy(fbf[:, 2, :], KEEPB)
            V.tensor_copy(fbf[:, 3, :], ENDS).then_inc(s_set, 1)

            dve.wait_ge(s_weights, 2 * 16)
            V.tensor_copy(vec[:, 0:len(LOADED)], part["loaded"])
            chained(V.tensor_scalar(mean2[:, :], mask64[:, :], 1.0 / D, None, ALU.mult))
            chained(V.tensor_tensor(center[:, :], ident[:, :], mean2[:, :], ALU.subtract))
            V.tensor_scalar(att1m[:, :], mask16[:, :], v("att1"), None, ALU.mult)
            V.tensor_scalar(att2m[:, :], mask64[:, :], v("att2"), None, ALU.mult)
            small = L[2][1]
            for n_ in ("root2", "wc", "wr", "ws2"):
                m = bd[n_].rearrange("p (a f) -> p a f", a=2)
                chained(V.tensor_reduce(small[:, 0:2], m, axis=AX.X, op=ALU.add))
                chained(V.tensor_scalar(small[:, 2:4], small[:, 0:2], 1.0 / D, None, ALU.mult))
                chained(V.tensor_tensor(m, m, small[:, 2:4].unsqueeze(2).to_broadcast([P, 2, D]), ALU.subtract))

            def in_parts(to, w, mask):
                q, n_ = w.shape
                parts = [L[2][2 + i][0:q, 0:n_] for i in range(3)]
                half = L[2][5][0:q, :].bitcast(BF16)[:, 0:n_]
                rest = L[2][6][0:q, 0:n_]
                chained(V.tensor_copy(half, w))
                chained(V.tensor_copy(parts[0], half))
                chained(V.tensor_tensor(rest, w, parts[0], ALU.subtract))
                chained(V.tensor_copy(half, rest))
                chained(V.tensor_copy(parts[1], half))
                chained(V.tensor_tensor(parts[2], rest, parts[1], ALU.subtract))
                chained(V.tensor_scalar(parts[0], parts[0], mask[:, 0:1], None, ALU.mult))
                for i in (1, 2):
                    chained(V.scalar_tensor_tensor(parts[0] if i == 1 else to, parts[i], mask[:, i:i + 1], parts[0],
                                                   ALU.mult, ALU.add))
            for l in range(2):
                in_parts(cwb[:, l, :, :].rearrange("p j m -> p (j m)"), cw[:, l, :], mask3)
            in_parts(we[:, :, :].rearrange("p l m -> p (l m)"), part["we"][0:9, :], mask9)
            chained(V.tensor_scalar(v("alone"), v("g_b2"), 0.0, None, ALU.max))
            V.tensor_copy(v("var"), v("alone")).then_inc(s_set, 1)
            B0 = bank[0][0]

            def col(i):
                return L[0][i][:, 0:1]
            dve.wait_ge(s_set, SQ["bias_p"])
            i0 = VECS.index("bias2c")
            V.tensor_copy(vec[:, i0:i0 + 4], B0[:, 0:4]).then_inc(s_set, 1)
            for i, b_ in enumerate(("g_bcc", "g_brc")):
                dve.wait_ge(s_set, SQ[f"sd{i}"])
                chained(V.reciprocal(col(3), col(4)))
                V.scalar_tensor_tensor(col(6), B0[:, 0:1], v(b_), col(3), ALU.add, ALU.mult).then_inc(s_set, 1)
            dve.wait_ge(s_set, SQ["y2_p"])
            V.tensor_copy(v("alone"), B0[:, 0:1]).then_inc(s_set, 1)

            def by_row(to, of, factors):
                return V.tensor_tensor(to.rearrange("p (j d) -> p j d", d=D), of[:, :].rearrange("p (j d) -> p j d", d=D),
                                       factors.unsqueeze(2).to_broadcast([P, 8, D]), ALU.mult)

            def nodes(at):
                pz = ph["nodeA"]

                def each(before_, make):
                    for g, k, c in at(pz.after(before_)):
                        dve.wait_ge(lane[g], pz.at(g, k, before_))
                        make(g).then_inc(lane[g], 1)

                for g, k, c in at("x1_o"):
                    if type(k) is not int or k > 0:
                        dve.wait_ge(stored[g], st["nodeA"].before(g, k))
                    dve.wait_ge(lane[g], pz.at(g, k, "x1_t"))
                    V.tensor_copy(tl(g, 7), bank[g][1][:, :]).then_inc(lane[g], 1)
                for i in range(3):
                    each(f"sd{i}", lambda g: V.reciprocal(rowwise(g, 1), rowwise(g, 0)))
                    each(f"rs{i}", lambda g: by_row(tl(g, (8, 9, 8)[i]), bank[g][0], rowwise(g, 1)))
                each("x_t", lambda g: V.tensor_copy(tl(g, 1), bank[g][0][:, :]))
                each("n0_t", lambda g: V.tensor_copy(tl(g, 5), bank[g][0][:, :]))
                for g, k, c in at("h2_o"):
                    dve.wait_ge(stored[g], st["nodeA"].before(g, k) + 16 * 3)
                    dve.wait_ge(lane[g], pz.at(g, k, "h2_t"))
                    V.tensor_copy(tl(g, 7), bank[g][1][:, :]).then_inc(lane[g], 1)
                each("n2_t", lambda g: V.tensor_copy(tl(g, 5), bank[g][0][:, :]))
                each("g1_t", lambda g: V.tensor_copy(tl(g, 9), bank[g][1][:, :]))
            in_turns(dve, ph["nodeA"], nodes)

            dve.wait_ge(s_keys, 16)
            REL, KEY, WGT = L[0][5][:, 0:T], L[0][0][:, 0:T], L[0][4][:, 0:T]

            def field(i):
                return recm[:, :, i:i + 1].rearrange("p t k -> p (t k)")
            V.memset(L[0][1][0:1, 0:1], -1.0)
            V.tensor_copy(L[0][6][:, 0:T], field(3))
            V.tensor_copy(WGT, field(2).bitcast(F32))
            chained(V.tensor_copy(REL, field(1)))
            V.scalar_tensor_tensor(KEY, L[0][6][:, 0:T], 16.0, REL, ALU.mult, ALU.add).then_inc(s_set, 1)
            dve.wait_ge(s_keys, 6 * 16)
            V.tensor_tensor(fbf[:, 0, :], KEY, L[0][2][:, 0:T], ALU.not_equal)
            V.tensor_tensor(fbf[:, 1, :], KEY, L[0][3][:, 0:T], ALU.not_equal)
            f_, rest = L[1][8][:, 0:T], L[1][9][:, 0:T]
            chained(V.tensor_copy(weight_part(0), WGT))
            chained(V.tensor_copy(f_, weight_part(0)))
            chained(V.tensor_tensor(rest, WGT, f_, ALU.subtract))
            chained(V.tensor_copy(weight_part(1), rest))
            chained(V.tensor_copy(f_, weight_part(1)))
            chained(V.tensor_tensor(rest, rest, f_, ALU.subtract))
            V.tensor_copy(weight_part(2), rest)
            for r in range(R):
                last = V.tensor_scalar(hotm(r), REL, float(r), None, ALU.is_equal)
            last.then_inc(s_set, 1)
            dve.wait_ge(s_spg, 2 * (T // GB))
            dve.wait_ge(s_ptr1, 16)
            dve.wait_ge(s_mask, 6 * 16)
            A, B, C = (L[1][i][:, 0:T] for i in (0, 1, 2))
            chained(V.tensor_scalar(A, spg[:, :, 1:2].rearrange("p t k -> p (t k)"), -float(NP), None, ALU.add))
            chained(V.tensor_scalar(B, A, 0.0, None, ALU.is_lt))
            chained(V.tensor_scalar(C, B, -1.0, 1.0, ALU.mult, ALU.add))
            chained(V.tensor_tensor(A, A, C, ALU.mult))
            chained(V.scalar_tensor_tensor(idh[:, :], B, float(EP), A, ALU.mult, ALU.add))
            V.tensor_scalar(alone8[:, :], recm[:, :, :].rearrange("p t (a b) -> p (t a) b", b=2)[:, :, 0:1]
                            .rearrange("p t k -> p (t k)"), float(NP), None, ALU.is_lt)
            chained(V.tensor_copy(A, dst8[:, :]))
            chained(V.tensor_scalar(alone8[:, (NCH - 1) * 8:], alone8[:, (NCH - 1) * 8:], real84[:, :], None, ALU.mult))
            SPARE = L[1][3][:, 0:T]
            chained(V.tensor_scalar(SPARE, iota_e[:, :], float(SPARE_OUT), None, ALU.add))
            chained(V.tensor_tensor(A, A, SPARE, ALU.subtract))
            chained(V.tensor_tensor(B, A, first8[:, :], ALU.mult))
            V.tensor_tensor(ido[:, :], B, SPARE, ALU.add).then_inc(s_set, 1)

            def scan(pz, step, before_, at, make):
                for g, k, c, r, use in at(step):
                    pg, pk = before(g, k)
                    dve.wait_ge(lane[pg], pz.at(pg, pk, step))
                    dve.wait_ge(lane[g], pz.at(g, k, before_))
                    make(g, pg).then_inc(lane[g], 1)

            def rgcn(name):
                pz = ph[name]
                l = 0 if name == "rg1" else 1

                def work(at):
                    def each(before_, make):
                        for g, k, c, r, use in at(pz.after(before_)):
                            dve.wait_ge(lane[g], pz.at(g, k, before_))
                            make(g).then_inc(lane[g], 1)

                    def low(g, i):
                        return tl(g, i)[0:D, :]

                    def state(g, i):
                        return L[g][i][0:D, W - 1:W]
                    for q in range(4):
                        each(f"c{q}_p", lambda g: V.tensor_tensor(
                            tl(g, q + l), bank[g][0][:, :], tl(g, q if l == 0 else 0), ALU.mult))
                    scan(pz, "gmax", "gfirst", at, lambda g, pg: V.tensor_tensor_scan(
                        low(g, 6), bank[g][0][0:D, :], low(g, 5), state(pg, 6), ALU.add, ALU.max))
                    each("glast", lambda g: V.tensor_tensor(low(g, 7), bank[g][0][0:D, :], low(g, 6), ALU.mult))
                    scan(pz, "agg", "keep", at, lambda g, pg: V.tensor_tensor_scan(
                        low(g, 8), bank[g][0][0:D, :], low(g, 7), state(pg, 8), ALU.mult, ALU.add))
                in_turns(dve, pz, work)

            def sage(name):
                pz = ph[name]

                def work(at):
                    scan(pz, "agg", "keep", at, lambda g, pg: V.tensor_tensor_scan(
                        tl(g, 8)[0:D, :], bank[g][1][0:D, :], tl(g, 5)[0:D, :], L[pg][8][0:D, W - 1:W], ALU.mult,
                        ALU.add))
                    for g, k, c, r, use in at("agg_o"):
                        dve.wait_ge(stored[g], st[name].before(g, k))
                        dve.wait_ge(lane[g], pz.at(g, k, "agg_t"))
                        V.tensor_tensor(orow[g][:, :, 0:D], bank[g][0][:, 0:4 * D].rearrange("p (j d) -> p j d", d=D),
                                        rinv[:, bass.ds(c * 4, 4)].unsqueeze(2).to_broadcast([P, 4, D]),
                                        ALU.mult).then_inc(lane[g], 1)
                in_turns(dve, pz, work)

            def soft(name):
                pz = ph[name]
                way = INFO[name][0]
                l = int(name[-1])
                gat = name[:3] == "gat"
                heads = {"gat1": 8, "gat2": 2}.get(name)
                end = W - 1 if way > 0 else 0

                def on(a):
                    return turned(a, way)

                def work(at):
                    def each(before_, make):
                        for g, k, c, r, use in at(pz.after(before_)):
                            dve.wait_ge(lane[g], pz.at(g, k, before_))
                            make(g).then_inc(lane[g], 1)
                    if name == "gat2":
                        scan(pz, "dst", "keep", at, lambda g, pg: V.tensor_tensor_scan(
                            on(tl(g, 10)), on(bank[g][0][:, :]), on(tl(g, 1)), L[pg][10][:, end:end + 1], ALU.mult,
                            ALU.add))
                    else:
                        i = 0 if name == "gat1" else 10
                        scan(pz, "dst", "keep", at, lambda g, pg: V.tensor_tensor_scan(
                            on(tl(g, i)[D:P, :]), on(bank[g][1][D:P, :]), on(tl(g, 1)[D:P, :]),
                            L[pg][i][D:P, end:end + 1], ALU.mult, ALU.add))
                    if gat:
                        each("z_s", lambda g: V.tensor_tensor(tl(g, 3), bank[g][0][:, :], tl(g, 2), ALU.max))
                    else:
                        each("kv_p", lambda g: V.scalar_tensor_tensor(
                            tl(g, 6)[D:P, :], bank[g][1][D:P, :], v(f"bk{l}")[D:P, :], tl(g, 3)[D:P, :], ALU.add,
                            ALU.mult))
                    s0 = 0 if way > 0 else 2
                    scan(pz, "y", "reset", at, lambda g, pg: V.tensor_tensor_scan(
                        on(tl(g, 5)), on(L[g][4][:, s0:s0 + W]), on(bank[g][0][:, :]), L[pg][5][:, end:end + 1],
                        ALU.max, ALU.add))
                    each("y", lambda g: V.tensor_tensor(tl(g, 6), bank[g][1][:, :], tl(g, 5), ALU.subtract))
                    each("d", lambda g: V.tensor_scalar(tl(g, 7), tl(g, 6), 0.0, None, ALU.min))
                    each("lo", lambda g: V.tensor_scalar(tl(g, 6), tl(g, 6), -1.0, 0.0, ALU.mult, ALU.min))
                    if gat:
                        each("v_p", lambda g: V.tensor_tensor(tl(g, 2), bank[g][0][:, :], tl(g, 7), ALU.mult))
                        for step, before_, i, o in (("num", "wv", 2, 8), ("den", "num", 7, 9)):
                            scan(pz, step, before_, at, lambda g, pg: V.tensor_tensor_scan(
                                on(tl(g, o)), on(tl(g, 6)), on(tl(g, i)), L[pg][o][:, end:end + 1], ALU.mult, ALU.add))
                        n4 = 4 * heads
                        for g, k, c, r, use in at("rc" if heads == 8 else "rcp"):
                            e = there(c, way, SWEEPS)
                            dve.wait_ge(lane[g], pz.at(g, k, "den_t"))
                            den = bank[g][1][:, :].rearrange("p (m w) -> p m w", m=n4)[:, :, 0:1].rearrange(
                                "p m w -> p (m w)")
                            if name == "gat1":
                                V.reciprocal(L[g][3][:, 0:n4], den).then_inc(lane[g], 1)
                                dve.wait_ge(lane[g], pz.at(g, k, "rc"))
                                dve.nop(nofuse=True)
                                V.tensor_tensor(L[g][3][:, 64:64 + n4].rearrange("p (j h) -> p j h", j=4),
                                                L[g][3][:, 0:n4].rearrange("p (j h) -> p j h", j=4),
                                                first4[:, bass.ds(e * 4, 4)].unsqueeze(2).to_broadcast([P, 4, heads]),
                                                ALU.mult).then_inc(lane[g], 1)
                            else:
                                V.reciprocal(L[g][3][:, 64:64 + n4], den).then_inc(lane[g], 1)
                        for g, k, c, r, use in at("rows"):
                            dve.wait_ge(stored[g], st[name].before(g, k))
                            dve.wait_ge(lane[g], pz.at(g, k, "rcp"))
                            V.tensor_tensor(orow[g][:, :, :].rearrange("p j (h w) -> p (j h) w", h=heads),
                                            bank[g][0][:, :].rearrange("p (m w) -> p m w", m=n4),
                                            L[g][3][:, 64:64 + n4].unsqueeze(2).to_broadcast([P, n4, P // heads]),
                                            ALU.mult).then_inc(lane[g], 1)
                    else:
                        each("ex", lambda g: V.tensor_tensor(tl(g, 7)[0:D, :], tl(g, 3)[0:D, :], tl(g, 7)[0:D, :],
                                                             ALU.mult))
                        scan(pz, "nd", "wv", at, lambda g, pg: V.tensor_tensor_scan(
                            on(tl(g, 8)), on(tl(g, 6)), on(tl(g, 7)), L[pg][8][:, end:end + 1], ALU.mult, ALU.add))
                        each("h_t", lambda g: V.reciprocal(
                            L[g][3][:, 0:4], bank[g][0][:, :].rearrange("p (j w) -> p j w", j=4)[:, :, D:D + 1].rearrange(
                                "p j w -> p (j w)")))
                        for g, k, c, r, use in at("rows"):
                            dve.wait_ge(stored[g], st[name].before(g, k))
                            dve.wait_ge(lane[g], pz.at(g, k, "rcp"))
                            V.tensor_tensor(orow[g][:, :, 0:D],
                                            bank[g][0][:, :].rearrange("p (j w) -> p j w", j=4)[:, :, 0:D],
                                            L[g][3][:, 0:4].unsqueeze(2).to_broadcast([P, 4, D]),
                                            ALU.mult).then_inc(lane[g], 1)
                in_turns(dve, pz, work)

            def passes(name):
                pz = ph[name]
                mask = {"e01": last8, "e02": last8, "e12": last8, "e21": last8, "e22": last8, "e31": first8,
                        "e32": last8}.get(name)

                def work(at):
                    def each(before_, make):
                        for g, k, c in at(pz.after(before_)):
                            dve.wait_ge(lane[g], pz.at(g, k, before_))
                            make(g).then_inc(lane[g], 1)

                    def tile7_free(g, k):
                        if name != last_pass:
                            dve.wait_ge(stored[g], st[name].before(g, k))
                        elif type(k) is not int or k > 0:
                            dve.wait_ge(put[g], scattered.before(g, k))

                    for g, k, c in at("heads"):
                        dve.wait_ge(lane[g], pz.begin(g, k))
                        dve.wait_ge(loaded[g], ld[name].after(g, k))
                        for i in (0, 8):
                            x = tl(g, i).rearrange("p (j h d) -> p j h d", h=2, d=D)
                            o = tl(g, 5)[:, 32 * i:32 * i + 4 * D].rearrange("p (j d) -> p j d", d=D)
                            last = V.tensor_tensor(o, x[:, :, 0, :], x[:, :, 1, :], ALU.add)
                        last.then_inc(lane[g], 1)
                    if "b" in pz.steps:
                        each("b_t", lambda g: V.tensor_copy(tl(g, 2), bank[g][1][:, :]))
                    for i in range(3):
                        if f"sd{i}" in pz.steps:
                            each(f"sd{i}", lambda g: V.reciprocal(rowwise(g, 1), rowwise(g, 0)))
                        if f"o{i}" in pz.steps:
                            each(f"rs{i}", lambda g: by_row(tl(g, 5), bank[g][0], rowwise(g, 1)))
                    for g, k, c in at("rm"):
                        dve.wait_ge(lane[g], pz.at(g, k, f"rs{2 if name == 'e12' else 0}"))
                        V.tensor_tensor(rowwise(g, 2), rowwise(g, 1), mask[:, bass.ds(c * 8, 8)], ALU.mult).then_inc(
                            lane[g], 1)
                    if "y0" in pz.steps:
                        for g, k, c in at("o"):
                            tile7_free(g, k)
                            dve.wait_ge(lane[g], pz.at(g, k, "rm" if mask is not None else "rs0"))
                            by_row(tl(g, 7), bank[g][0], rowwise(g, 1 if mask is None else 2)).then_inc(lane[g], 1)
                    elif "o" in pz.steps:
                        for g, k, c in at("o"):
                            tile7_free(g, k)
                            dve.wait_ge(lane[g], pz.at(g, k, "o_t"))
                            if mask is None:
                                V.tensor_copy(tl(g, 7), bank[g][1][:, :]).then_inc(lane[g], 1)
                            else:
                                V.tensor_tensor(tl(g, 7).rearrange("p (j d) -> p j d", d=D),
                                                bank[g][1][:, :].rearrange("p (j d) -> p j d", d=D),
                                                mask[:, bass.ds(c * 8, 8)].unsqueeze(2).to_broadcast([P, 8, D]),
                                                ALU.mult).then_inc(lane[g], 1)
                    if "st" in pz.steps:
                        l = 1 if name in ("e32", "n2") else 0
                        for g, k, c in at("st"):
                            pg, pk = before(g, k)
                            dve.wait_ge(lane[pg], pz.at(pg, pk, "st"))
                            dve.wait_ge(lane[g], pz.at(g, k, "st_p"))
                            V.tensor_tensor(stats[:, l, :], bank[g][1][:, 0:4], stats[:, l, :],
                                            ALU.add).then_inc(lane[g], 1)
                in_turns(dve, pz, work)

            def batchnorm(l):
                m = L[0][0]
                dve.wait_ge(s_set, SQ[f"bn{l}_p"])
                chained(V.tensor_scalar(m[:, 0:2], B0[:, 0:2], 1.0 / N, None, ALU.mult))
                chained(V.tensor_tensor(m[:, 2:3], m[:, 0:1], m[:, 0:1], ALU.mult))
                V.tensor_tensor(v("var"), m[:, 1:2], m[:, 2:3], ALU.subtract).then_inc(s_set, 1)
                dve.wait_ge(s_set, SQ[f"bn{l}_sd"])
                chained(V.reciprocal(m[:, 3:4], col(4)))
                chained(V.tensor_tensor(v(f"bn_s{l}"), v(f"gamma{l}"), m[:, 3:4], ALU.mult))
                chained(V.tensor_tensor(m[:, 4:5], m[:, 0:1], v(f"bn_s{l}"), ALU.mult))
                V.tensor_tensor(v(f"bn_b{l}"), v(f"beta{l}"), m[:, 4:5], ALU.subtract).then_inc(s_set, 1)
            rgcn("rg1")
            passes("e01")
            rgcn("rg2")
            passes("e02")
            soft("gat1")
            soft("gat2")
            passes("e12")
            sage("sage1")
            passes("e21")
            sage("sage2")
            passes("e22")
            soft("tr0")
            passes("e31")
            passes("nS")
            batchnorm(0)
            soft("tr1")
            passes("e32")
            passes("n2")
            batchnorm(1)
            soft("tr2")
            passes("n3")
            passes("e33")
def pack(a):
    import numpy as np

    f32 = np.float32
    x = {n: np.asarray(b) for n, b in a.items()}

    def padded(b, fill):
        return np.concatenate([b, np.full((EP - E,) + b.shape[1:], fill, b.dtype)])
    dst = padded(x["dst"].astype(np.int32), PAD_DST)
    prev = np.concatenate([np.full(1, -1, np.int32), dst[:-1]])
    nxt = np.concatenate([dst[1:], np.full(1, -1, np.int32)])
    edge_dst = np.ascontiguousarray(np.stack([dst, prev, nxt]).reshape(3, P, T).transpose(1, 0, 2))
    rec = np.stack([padded(x["src"].astype(np.int32), 0), padded(x["edge_type_14"].astype(np.int32), 0),
                    padded(np.ascontiguousarray(x["edge_weight1"][:, 0]).view(np.int32), 0), dst], axis=1)

    def twice(m):
        z = np.zeros((P, P), f32)
        z[:D, :D] = m
        z[D:, D:] = m
        return z
    g, s, r3 = (lambda n: x["L1_gnn_" + n]), (lambda n: x["L2_gnn_" + n]), (lambda n: x["L3_gnn_" + n])
    mats = {"root1": x["L0_gnn_root1"], "root2": x["L0_gnn_root2"], "wc": g("wc"), "wr": g("wr"), "wl1": s("Wl1").T,
            "wr1": s("Wr1").T, "wl2": s("Wl2").T, "wr2": s("Wr2").T, "ws0": r3("Ws")[0], "ws1": r3("Ws")[1],
            "ws2": r3("Ws")[2]}
    parts = {n: twice(m) for n, m in mats.items()}
    parts["basew"] = x["L0_gnn_bases2"].reshape(4, 2 * D, D).transpose(1, 0, 2).reshape(P, 4 * D)
    parts["gw"] = np.concatenate([g("w1_l"), g("w1_r")])
    parts["g2l"], parts["g2r"] = g("w2_l"), g("w2_r")
    we = np.zeros((P, 2 * P), f32)
    we[0:9] = np.concatenate([g("w1_e")[0], g("w2_e")[0]])
    parts["we"] = we
    wk, wvq = np.zeros((P, 3, P), f32), np.zeros((P, 3, P), f32)
    for l in range(3):
        wvq[:D, l, :D], wvq[D:, l, D:], wk[:D, l, D:] = r3("Wv")[l], r3("Wq")[l], r3("Wk")[l]
    parts["wvq"], parts["wk"] = wvq.reshape(P, -1), wk.reshape(P, -1)
    vecs = [x["L0_gnn_bias1"], x["L0_gnn_bias2"], g("b1"), g("b2"), g("bc"), g("ln_g"), g("ln_b"), g("br"), g("lnr_g"),
            g("lnr_b"), g("att1").reshape(-1), g("att2").reshape(-1), s("b1"), s("b2")]
    vecs += [np.concatenate([r3("bv")[l], r3("bq")[l]]) for l in range(3)]
    vecs += [r3(n)[l] for n in ("bk", "bs") for l in range(3)]
    vecs += [r3(n)[l] for n in ("gamma", "beta") for l in range(2)]
    parts["loaded"] = np.stack([b if b.shape[0] == P else np.concatenate([b, b]) for b in vecs], axis=1)
    packed = np.concatenate([parts[n] for n, _ in PACKED], axis=1)
    w1 = x["L0_gnn_w1"].transpose(0, 2, 1, 3).reshape(R, 4 * P)
    comp = np.repeat(x["L0_gnn_comp2"].reshape(R, 8, 1), D, axis=2).reshape(R, 4 * P)
    relw = np.concatenate([np.stack([w1, comp], axis=1)] * 3)
    return {"x": x["x"], "edge_dst": edge_dst, "edge_rec": rec.reshape(P, T, 4), "packed": packed.astype(f32),
            "relw": relw.astype(f32)}


def kernel(**inputs):
    import concourse.bacc as bacc
    import numpy as np
    from concourse.bass_utils import run_bass_kernel_spmd

    nc = bacc.Bacc("TRN2", target_bir_lowering=False, num_devices=1)
    arrays = {f"in_{n}": np.ascontiguousarray(a) for n, a in pack(inputs).items()}
    t = {n[3:]: nc.dram_tensor(n, a.shape, mybir.dt.from_np(a.dtype), kind="ExternalInput").ap()
         for n, a in arrays.items()}
    out = nc.dram_tensor("out", (OUT_ROWS, D), F32, kind="ExternalOutput").ap()
    build(nc, t, out)
    r = run_bass_kernel_spmd(nc, [arrays], core_ids=[0])
    return r.results[0]["out"][:N]
```
